# Optimizing a Trainium2 kernel written in Bass

```python
import numpy as np
import jax
import jax.numpy as jnp

def _softmax(x, axis=-1):
    return jax.nn.softmax(x, axis=axis)

def _gelu(x):
    return jax.nn.gelu(x, approximate=True)

def _silu(x):
    return jax.nn.silu(x)

def _sigmoid(x):
    return jax.nn.sigmoid(x)

def _layernorm(x, axis=-1, eps=1e-05):
    m = jnp.mean(x, axis=axis, keepdims=True)
    v = jnp.var(x, axis=axis, keepdims=True)
    return (x - m) / jnp.sqrt(v + eps)

def _scatter_add(tgt, idx, src, axis=0):
    return tgt.at[idx].add(src)

def _segment_sum(src, seg, n):
    return jax.ops.segment_sum(src, seg, n)
kernel_name = 'mk_adaln_d1_jaxref_r8_a552fe'

def setup_inputs(seed: int=0):
    np.random.seed(seed)
    _w = jnp.asarray

    def _L0_attn_setup():
        import jax, jax.numpy as jnp
        import numpy as np
        D_MODEL = 128
        N_HEADS = 16
        HEAD_DIM = D_MODEL // N_HEADS
        N_EXPERTS = 4
        HIDDEN = 4 * D_MODEL
        B, T = (1, 256)

        def _apply_rope(x, sin, cos):
            x1, x2 = (x[..., ::2], x[..., 1::2])
            r1 = x1 * cos - x2 * sin
            r2 = x1 * sin + x2 * cos
            return jnp.stack((r1, r2), axis=-1).reshape(x.shape)
        key = jax.random.key(seed)
        ks = jax.random.split(key, 16)
        s = 0.02
        d, E, Hd = (D_MODEL, N_EXPERTS, HIDDEN)
        return {'x': jax.random.normal(ks[0], (B, T, d), dtype=jnp.float32), 'w_dw': jax.random.normal(ks[1], (d, 3), dtype=jnp.float32) * s, 'w_pw': jax.random.normal(ks[2], (d, d), dtype=jnp.float32) * s, 'w_qkv': jax.random.normal(ks[3], (3 * d, d), dtype=jnp.float32) * s, 'w_o': jax.random.normal(ks[4], (d, d), dtype=jnp.float32) * s, 'w_gate': jax.random.normal(ks[5], (d, d), dtype=jnp.float32) * s, 'b_gate': jnp.zeros((d,), dtype=jnp.float32), 'ln_g': jnp.ones((d,), dtype=jnp.float32), 'ln_b': jnp.zeros((d,), dtype=jnp.float32), 'w_moe_gate': jax.random.normal(ks[6], (E, d), dtype=jnp.float32) * s, 'w1': jax.random.normal(ks[7], (E, Hd, d), dtype=jnp.float32) * s, 'b1': jnp.zeros((E, Hd), dtype=jnp.float32), 'w2': jax.random.normal(ks[8], (E, d, Hd), dtype=jnp.float32) * s, 'b2': jnp.zeros((E, d), dtype=jnp.float32)}
    _L0_attn_in = _L0_attn_setup()

    def _L0_ffn_setup():
        import jax, jax.numpy as jnp
        import numpy as np
        B, S, D, E, F = (4, 256, 128, 8, 512)
        key = jax.random.key(seed)
        k0, k1, k2, k3 = jax.random.split(key, 4)
        x = jax.random.normal(k0, (B, S, D), dtype=jnp.float32)
        wg = jax.random.normal(k1, (D, E), dtype=jnp.float32) * 0.02
        w_gate = jax.random.normal(k2, (E, D, F), dtype=jnp.float32) * 0.02
        w_down = jax.random.normal(k3, (E, F, D), dtype=jnp.float32) * 0.02
        return {'x': x, 'wg': wg, 'w_gate': w_gate, 'w_down': w_down}
    _L0_ffn_in = _L0_ffn_setup()
    _L0_c = _w((lambda *s: np.random.randn(*s).astype(np.float32) * 0.05)(2, 128))
    _L0_wmod = _w((lambda *s: np.random.randn(*s).astype(np.float32) * 0.05)(128, 6 * 128) * 128 ** (-0.5))
    _d = {'L0_attn_x': _L0_attn_in['x'], 'L0_attn_w_dw': _L0_attn_in['w_dw'], 'L0_attn_w_pw': _L0_attn_in['w_pw'], 'L0_attn_w_qkv': _L0_attn_in['w_qkv'], 'L0_attn_w_o': _L0_attn_in['w_o'], 'L0_attn_w_gate': _L0_attn_in['w_gate'], 'L0_attn_b_gate': _L0_attn_in['b_gate'], 'L0_attn_ln_g': _L0_attn_in['ln_g'], 'L0_attn_ln_b': _L0_attn_in['ln_b'], 'L0_attn_w_moe_gate': _L0_attn_in['w_moe_gate'], 'L0_attn_w1': _L0_attn_in['w1'], 'L0_attn_b1': _L0_attn_in['b1'], 'L0_attn_w2': _L0_attn_in['w2'], 'L0_attn_b2': _L0_attn_in['b2'], 'L0_ffn_wg': _L0_ffn_in['wg'], 'L0_ffn_w_gate': _L0_ffn_in['w_gate'], 'L0_ffn_w_down': _L0_ffn_in['w_down'], 'L0_c': _L0_c, 'L0_wmod': _L0_wmod}
    _x0 = _d['L0_attn_x']
    _d['L0_attn_x'] = jax.random.normal(jax.random.fold_in(jax.random.key(seed), 1), (2, 1024, 128), dtype=_x0.dtype)
    del _x0
    return _d

def reference(L0_attn_x, L0_attn_w_dw, L0_attn_w_pw, L0_attn_w_qkv, L0_attn_w_o, L0_attn_w_gate, L0_attn_b_gate, L0_attn_ln_g, L0_attn_ln_b, L0_attn_w_moe_gate, L0_attn_w1, L0_attn_b1, L0_attn_w2, L0_attn_b2, L0_ffn_wg, L0_ffn_w_gate, L0_ffn_w_down, L0_c, L0_wmod):

    def _L0_attn_ref(x, w_dw, w_pw, w_qkv, w_o, w_gate, b_gate, ln_g, ln_b, w_moe_gate, w1, b1, w2, b2):
        import jax, jax.numpy as jnp
        import numpy as np
        D_MODEL = 128
        N_HEADS = 16
        HEAD_DIM = D_MODEL // N_HEADS
        N_EXPERTS = 4
        HIDDEN = 4 * D_MODEL
        B, T = (1, 256)

        def _apply_rope(x, sin, cos):
            x1, x2 = (x[..., ::2], x[..., 1::2])
            r1 = x1 * cos - x2 * sin
            r2 = x1 * sin + x2 * cos
            return jnp.stack((r1, r2), axis=-1).reshape(x.shape)
        Bv, Tv, d = x.shape
        H, Dh = (N_HEADS, HEAD_DIM)
        dt = x.dtype
        xp = jnp.pad(x, ((0, 0), (2, 0), (0, 0)))
        y = xp[:, 0:Tv] * w_dw[:, 0] + xp[:, 1:Tv + 1] * w_dw[:, 1] + xp[:, 2:Tv + 2] * w_dw[:, 2]
        y = jnp.einsum('btd,ed->bte', y, w_pw)
        x = x + y
        qkv = jnp.einsum('btd,ed->bte', x, w_qkv).reshape(Bv, Tv, 3, H, Dh)
        q, k, v = (qkv[:, :, 0], qkv[:, :, 1], qkv[:, :, 2])
        inv_freq = 1.0 / 10000.0 ** (jnp.arange(0, Dh, 2, dtype=dt) / Dh)
        pos = jnp.arange(Tv, dtype=dt)
        theta = pos[:, None] * inv_freq[None, :]
        sin = jnp.sin(theta)[None, :, None, :]
        cos = jnp.cos(theta)[None, :, None, :]
        q = _apply_rope(q, sin, cos)
        k = _apply_rope(k, sin, cos)
        q_phi = jax.nn.elu(q) + 1.0
        k_phi = jax.nn.elu(k) + 1.0
        kv = k_phi[..., :, None] * v[..., None, :]
        kv_prefix = jnp.cumsum(kv, axis=1)
        k_prefix = jnp.cumsum(k_phi, axis=1)
        num = jnp.einsum('bthd,bthdm->bthm', q_phi, kv_prefix)
        denom = jnp.sum(q_phi * k_prefix, axis=-1, keepdims=True)
        attn = num / (denom + 1e-06)
        attn = attn.reshape(Bv, Tv, d)
        attn = jnp.einsum('btd,ed->bte', attn, w_o)
        delta = x - jnp.concatenate([x[:, :1], x[:, :-1]], axis=1)
        gate = jax.nn.sigmoid(jnp.einsum('btd,ed->bte', delta, w_gate) + b_gate)
        x = x + gate * attn
        mu = jnp.mean(x, axis=-1, keepdims=True)
        var = jnp.mean((x - mu) ** 2, axis=-1, keepdims=True)
        h = (x - mu) / jnp.sqrt(var + 1e-05) * ln_g + ln_b
        gw = jax.nn.softmax(jnp.einsum('btd,ed->bte', h, w_moe_gate), axis=-1)
        hid = jax.nn.silu(jnp.einsum('btd,efd->btef', h, w1) + b1)
        eo = jnp.einsum('btef,edf->bted', hid, w2) + b2
        ffn = jnp.einsum('bte,bted->btd', gw, eo)
        return x + ffn

    def _L0_ffn_ref(x, wg, w_gate, w_down):
        import jax, jax.numpy as jnp
        import numpy as np
        B, S, D, E, F = (4, 256, 128, 8, 512)
        Bb, Ss, Dd = x.shape
        Ee = wg.shape[1]
        T = Bb * Ss
        C = 2 * T // Ee
        tokens = x.reshape(T, Dd)
        logits = tokens.astype(jnp.float32) @ wg.astype(jnp.float32)
        gates = jax.nn.softmax(logits, axis=-1)
        idx1 = jnp.argmax(gates, axis=-1)
        mask1 = jax.nn.one_hot(idx1, Ee, dtype=jnp.int32)
        logits_no1 = jnp.where(mask1 > 0, -jnp.inf, logits)
        idx2 = jnp.argmax(logits_no1, axis=-1)
        mask2 = jax.nn.one_hot(idx2, Ee, dtype=jnp.int32)
        g1 = jnp.take_along_axis(gates, idx1[:, None], axis=-1)[:, 0]
        g2 = jnp.take_along_axis(gates, idx2[:, None], axis=-1)[:, 0]
        denom = jnp.clip(g1 + g2, 1e-09, None)
        g1, g2 = (g1 / denom, g2 / denom)
        loc1 = jnp.cumsum(mask1, axis=0) - mask1
        loc2 = jnp.cumsum(mask2, axis=0) - mask2 + jnp.sum(mask1, axis=0, keepdims=True)
        loc1_s = jnp.sum(loc1 * mask1, axis=-1)
        loc2_s = jnp.sum(loc2 * mask2, axis=-1)
        keep1 = (loc1_s < C).astype(x.dtype)
        keep2 = (loc2_s < C).astype(x.dtype)
        f1 = idx1 * C + jnp.minimum(loc1_s, C - 1)
        f2 = idx2 * C + jnp.minimum(loc2_s, C - 1)
        disp = jnp.zeros((Ee * C, Dd), dtype=x.dtype)
        disp = disp.at[f1].add(tokens * keep1[:, None])
        disp = disp.at[f2].add(tokens * keep2[:, None])
        disp = disp.reshape(Ee, C, Dd)
        h = jax.nn.gelu(jnp.einsum('ecd,edf->ecf', disp, w_gate), approximate=False)
        eo = jnp.einsum('ecf,efd->ecd', h, w_down).reshape(Ee * C, Dd)
        out = (g1 * keep1)[:, None].astype(x.dtype) * eo[f1] + (g2 * keep2)[:, None].astype(x.dtype) * eo[f2]
        return out.reshape(Bb, Ss, Dd)
    x = L0_attn_x
    mod = (_silu(L0_c) @ L0_wmod).reshape(L0_c.shape[0], 6, 1, -1)
    sa, ca, ga, sb, cb, gb = (mod[:, 0], mod[:, 1], mod[:, 2], mod[:, 3], mod[:, 4], mod[:, 5])
    ga = (2 * (ga >= 0) - 1) * jnp.maximum(jnp.abs(ga), 0.25)
    gb = (2 * (gb >= 0) - 1) * jnp.maximum(jnp.abs(gb), 0.25)
    h = _layernorm(x, axis=-1) * (1 + ca) + sa
    x = x + ga * _L0_attn_ref(h, L0_attn_w_dw, L0_attn_w_pw, L0_attn_w_qkv, L0_attn_w_o, L0_attn_w_gate, L0_attn_b_gate, L0_attn_ln_g, L0_attn_ln_b, L0_attn_w_moe_gate, L0_attn_w1, L0_attn_b1, L0_attn_w2, L0_attn_b2)
    h = _layernorm(x, axis=-1) * (1 + cb) + sb
    x = x + gb * _L0_ffn_ref(h, L0_ffn_wg, L0_ffn_w_gate, L0_ffn_w_down)
    return x

_drawn_inputs = setup_inputs


def setup_inputs(seed=0):
    import zlib

    import numpy as np

    out = dict(_drawn_inputs(seed))
    spreads = {'L0_attn_b_gate': (0.0, 0.8),
     'L0_attn_ln_g': (1.0, 0.6),
     'L0_attn_ln_b': (0.0, 0.8),
     'L0_attn_b1': (0.0, 0.8),
     'L0_attn_b2': (0.0, 0.562)}
    factors = {'L0_attn_w_dw': 8.0,
     'L0_attn_w_pw': 8.0,
     'L0_attn_w_qkv': 8.0,
     'L0_attn_w_o': 8.0,
     'L0_attn_w_gate': 8.0,
     'L0_attn_w_moe_gate': 8.0,
     'L0_attn_w1': 8.0,
     'L0_attn_w2': 7.455,
     'L0_ffn_wg': 6.978,
     'L0_ffn_w_gate': 6.259,
     'L0_ffn_w_down': 6.146}
    for name, (base, spread) in spreads.items():
        noise = np.random.default_rng([zlib.crc32(name.encode()), seed]).standard_normal(out[name].shape)
        drawn = base * np.exp(spread * noise) if base else spread * noise
        out[name] = jnp.asarray(drawn.astype(out[name].dtype))
    for name, factor in factors.items():
        out[name] = (out[name] * factor).astype(out[name].dtype)
    return out
```

```python
from contextlib import ExitStack

import concourse.bass as bass
from concourse import mybir

F32 = mybir.dt.float32
F32R = mybir.dt.float32r
BF16 = mybir.dt.bfloat16
U32 = mybir.dt.uint32
ALU = mybir.AluOpType
ACT = mybir.ActivationFunctionType
AX = mybir.AxisListType

P = 128
BATCH, SEQ, D = 2, 1024, 128
TOKENS = BATCH * SEQ
TILES = TOKENS // P
BT = 4
NBLK = TILES // BT
W = BT * P
TPB = SEQ // P
BPB = SEQ // W
HEADS = 16
DH = D // HEADS
M1 = DH + 1
CH = M1 * D
NH9 = M1 * HEADS
E1 = 4
FC = 4
E2 = 8
CAP = 2 * TOKENS // E2
SLOTS = E2 * CAP
LN_EPS = 1e-5
DEN_EPS = 1e-6
BIG = 3.0e38
MOD = 6

S_DW, S_BG, S_LG, S_LB, S_MG, S_B1, S_WG, S_C = 0, 3, 4, 5, 6, 10, 26, 34
N_SMALL = 36
C_ID, C_TRI, C_BD, C_COS, C_SIN, C_REV, C_TR = 0, 128, 256, 400, 464, 528, 536
N_CONST = C_TR + 2 * TILES


def block_kernel(nc, x, small, proj, wmod, w1, w2, b2, w_up, w_down, const, cmask, out):
    with ExitStack() as ctx:
        def sb(name, shape, dt=F32):
            return ctx.enter_context(nc.sbuf_tensor(name, shape, dt))

        def sem(name):
            return ctx.enter_context(nc.semaphore(name))

        table = nc.dram_tensor("slot_table", (2 * SLOTS, D), F32).ap()
        expert_out = nc.dram_tensor("expert_out", (SLOTS, D), F32).ap()

        ps = ctx.enter_context(nc.psum_tensor("ps", [P, 8, 512], F32))
        B_D, B_Q, B_KV, B_M, B_UP, B_DN = 0, 1, 2, 4, (5, 6), 7

        c_sb = sb("c_sb", [P, N_CONST])
        cm_sb = sb("cm_sb", [P, 2, P], BF16)
        s_sb = sb("s_sb", [P, N_SMALL])
        proj_sb = sb("proj_sb", [P, 6 * P])
        ident = c_sb[:, C_ID:C_ID + P]
        tri = c_sb[:, C_TRI:C_TRI + P]
        headmask = c_sb[:, C_BD:C_BD + NH9]
        strict, ones = cm_sb[:, 0, :], cm_sb[:, 1, :]
        wmod_sb = sb("wmod_sb", [P, MOD * D])
        w2_sb = sb("w2_sb", [P, E1, FC, D])
        b2_sb = sb("b2_sb", [P, BT, D])
        wd_sb = sb("wd_sb", [P, E2, FC, D])
        wst = sb("wst", [P, E1, W])
        w1h, w1l = sb("w1h", [P, E1, W], F32R), sb("w1l", [P, E1, W], F32R)
        wuh, wul = sb("wuh", [P, E1, W], F32R), sb("wul", [P, E1, W], F32R)
        x_sb = sb("x_sb", [P, TILES, D])
        x2 = sb("x2", [P, TILES, D])
        h3 = sb("h3", [P, TILES, D])
        wide = sb("wide", [P, BATCH * (3 + 2 * SEQ)])
        hT = wide[:, 0:BATCH * (2 + SEQ)].rearrange("p (b s) -> p b s", b=BATCH)
        x1T = wide[:, BATCH * (2 + SEQ):].rearrange("p (b s) -> p b s", b=BATCH)
        xh = sb("xh", [P, BT, D])
        xm = sb("xm", [P, BT, D])
        conv = sb("conv", [P, W])
        diff = sb("diff", [P, W])
        qk = sb("qk", [P, BT, 2 * D])
        vx = sb("vx", [P, 2, BT, NH9])
        rot_b = sb("rot_b", [P, BT, 2 * D])
        phi = sb("phi", [P, 2, BT, 2 * D])
        kv = sb("kv", [P, 2, CH])
        qp = sb("qp", [P, CH])
        qT = sb("qT", [P, 2, D])
        state = sb("state", [P, NH9])
        nd = sb("nd", [P, 2, NH9])
        rden = sb("rden", [P, 2, HEADS])
        att = sb("att", [P, 2, D])
        attT = sb("attT", [P, W])
        gate = wmod_sb[:, 0:W]
        x2T = attT
        h2T = sb("h2T", [P, W])
        h2h, h2l = sb("h2h", [P, 2, W], F32R), sb("h2l", [P, 2, W], F32R)
        hid = sb("hid", [P, 2, FC, W])
        acc = sb("acc", [P, BT, D])
        gwT = sb("gwT", [P, P])
        gwp = sb("gwp", [P, 2, P])
        h3T = sb("h3T", [P, W])
        st = sb("st", [P, BT, 6])
        mv = [sb(f"mv{i}", [P, TILES, 2]) for i in range(3)]
        ve = [sb(f"ve{i}", [P, TILES]) for i in range(3)]
        rstd = [sb(f"rstd{i}", [P, TILES]) for i in range(3)]
        mhalf = sb("mhalf", [P, BT])
        zero = wuh[:, 0:2, :].bitcast(F32).rearrange("p e f -> p (e f)")
        scT = sb("scT", [P, 2])
        scb = sb("scb", [P, 2, P])
        modT = sb("modT", [P, 2, 2])
        hbg = sb("hbg", [P, 1])
        modb = sb("modb", [P, BATCH, 4, D])
        gtmp = sb("gtmp", [P, 2, BATCH, D])
        sm = sb("sm", [P, BT, 4])
        sm_r = sb("sm_r", [P, 2, BT])
        lg = sb("lg", [P, BT, E2])
        gt_ = sb("gt_", [P, BT, E2])
        rt = sb("rt", [P, 4, BT, E2])
        rs = sb("rs", [P, 10, BT])
        oh = sb("oh", [P, TILES, 2 * E2])
        ohb = sb("ohb", [P, TILES, 2 * E2], BF16)
        before = sb("before", [P, TILES + 1, 2 * E2], BF16)
        exps = sb("exps", [P, TILES, 2])
        loc = sb("loc", [P, TILES, 2])
        gk = sb("gk", [P, TILES, 2])
        lt = sb("lt", [P, TILES, E2])
        over = sb("over", [P, TILES, 2])
        slot = sb("slot", [P, TILES, 2])
        dest = sb("dest", [P, TILES, 2])
        slot_i = sb("slot_i", [P, 2, TILES], U32)
        dest_i = sb("dest_i", [P, 2, TILES], U32)
        rows = phi[:, 0]
        back = wide[:, 0:TILES * 2 * D].rearrange("p (t k d) -> p t k d", t=TILES, k=2)

        L = lambda n: [sem(f"{n}_{i}") for i in range(NBLK)]
        x_in = L("x_in")
        small_in, mod_in, proj_in, w2_in, wd_in = (sem(n) for n in ("small_in", "mod_in", "proj_in", "w2_in", "wd_in"))
        wst_in = [sem(f"wst_in_{i}") for i in range(3)]
        w_split = sem("w_split")
        zero_ready, table_zero = sem("zero_ready"), sem("table_zero")
        sc_ready, scb_ready, mod_ps, mod_ready = (sem(n) for n in ("sc_ready", "scb_ready", "mod_ps", "mod_ready"))
        pads_ready, v_ones = sem("pads_ready"), sem("v_ones")
        dve_step, pool_step, act_step = sem("dve_step"), sem("pool_step"), sem("act_step")
        var_ready = [sem(f"var{i}_ready") for i in range(3)]
        rstd_ready = [sem(f"rstd{i}_ready") for i in range(3)]
        xh_ready, hT_ps, hT_ready, conv0_ready, conv_ready, pw_ps, x1_ready, diff_ready = (
            sem(n) for n in ("xh_ready", "hT_ps", "hT_ready", "conv0_ready", "conv_ready", "pw_ps", "x1_ready",
                             "diff_ready"))
        qkv_ps, qkv_ready, rot_parts, rot_ready, exp_ready, phi_ready = (
            sem(n) for n in ("qkv_ps", "qkv_ready", "rot_parts", "rot_ready", "exp_ready", "phi_ready"))
        kv_ready, cum_ps, tail_ps, qT_ps, qT_ready, cum_read, tail_read, state_ready, att_ready, attT_ps, attT_ready = (
            sem(n) for n in ("kv_ready", "cum_ps", "tail_ps", "qT_ps", "qT_ready", "cum_read", "tail_read",
                             "state_ready", "att_ready", "attT_ps", "attT_ready"))
        og_ps, gate_ready, x2T_ready, x2_ps, x2_ready, xm_ready, h2T_ps, h2T_ready, h2_split = (
            sem(n) for n in ("og_ps", "gate_ready", "x2T_ready", "x2_ps", "x2_ready", "xm_ready", "h2T_ps",
                             "h2T_ready", "h2_split"))
        mix_ps, mix_shift, mix_exp, mix_ready, gwT_ps, gwT_ready, b2_ps, acc_ready = (
            sem(n) for n in ("mix_ps", "mix_shift", "mix_exp", "mix_ready", "gwT_ps", "gwT_ready", "b2_ps",
                             "acc_ready"))
        up_ps, hid_ready, down_ps, down_added = (sem(n) for n in ("up_ps", "hid_ready", "down_ps", "down_added"))
        h3_ready, h3T_ps, h3T_ready, route_ps, route_shift, route_exp, onehot_ready, pos_ps, first_ready = (
            sem(n) for n in ("h3_ready", "h3T_ps", "h3T_ready", "route_ps", "route_shift", "route_exp",
                             "onehot_ready", "pos_ps", "first_ready"))
        pos_read, total_ps, second_ready, scattered = (
            sem(n) for n in ("pos_read", "total_ps", "second_ready", "scattered"))
        rows_in = [sem(f"rows_in_{e}") for e in range(E2)]
        rowsT_ps, rowsT_hi, rowsT_lo, eup_ps, ehid_ready, edown_ps, eout_ready = (
            sem(n) for n in ("rowsT_ps", "rowsT_hi", "rowsT_lo", "eup_ps", "ehid_ready", "edown_ps", "eout_ready"))
        eout_stored = [sem(f"eout_stored_{i}") for i in range(2)]
        gathered = [sem(f"gathered_{i}") for i in range(TILES)]
        comb0, comb_ready, stored = sem("comb0"), sem("comb_ready"), sem("stored")

        LAG = BT + 2
        STEPS = (NBLK + 3) * BT

        def live(blk):
            return 0 <= blk < NBLK

        def cols(ap, blk, pad):
            o = pad + (blk % BPB) * W
            return ap[:, blk // BPB, o:o + W]

        def up_weights(k):
            return (wuh, wul) if k // E1 == 1 else (w1h, w1l)

        def tiles(ap, blk):
            return ap[:, blk * BT:(blk + 1) * BT]

        def store_expert(sp, e):
            sp.wait_ge(eout_ready, e + 1)
            sp.dma_start(expert_out[e * CAP:(e + 1) * CAP, :].rearrange("(t p) d -> p t d", p=P),
                         xstage(e)).then_inc(eout_stored[e % 2], 16)

        def xstage(e):
            return (xh if e % 2 == 0 else xm)[:]

        def gelus(act, e):
            for c in range(FC):
                u = e * FC + c
                act.wait_ge(eup_ps, u + 1)
                if e >= 2 and c == 0:
                    act.wait_ge(edown_ps, e - 1)
                if e < 2 and c == 0:
                    act.wait_ge(down_ps, NBLK * E1)
                nc.scalar.activation(hid[:, e % 2, c, :], ps[:, 2 + u % 2, :], ACT.Gelu).then_inc(ehid_ready, 1)

        block = ctx.enter_context(nc.Block())

        @block.sync
        def _(sp):
            xv = x.rearrange("b (t p) d -> p (b t) d", p=P)
            ov = out.rearrange("b (t p) d -> p (b t) d", p=P)
            sp.dma_start(tiles(x_sb, 0), tiles(xv, 0)).then_inc(x_in[0], 16)
            sp.dma_start(s_sb[:], small).then_inc(small_in, 16)
            sp.dma_start(c_sb[:], const).then_inc(small_in, 16)
            sp.dma_start(cm_sb[:], cmask).then_inc(small_in, 16)
            sp.dma_start(wmod_sb[:], wmod).then_inc(mod_in, 16)
            sp.dma_start(proj_sb[:], proj).then_inc(proj_in, 16)
            sp.dma_start(wst[:], w1).then_inc(wst_in[0], 16)
            for b in range(1, NBLK):
                sp.dma_start(tiles(x_sb, b), tiles(xv, b)).then_inc(x_in[b], 16)
            sp.dma_start(w2_sb[:], w2).then_inc(w2_in, 16)
            sp.dma_start(b2_sb[:], b2).then_inc(w2_in, 16)
            sp.dma_start(wd_sb[:], w_down).then_inc(wd_in, 16)
            tz = table[0:SLOTS, :].rearrange("(p r) d -> p (r d)", p=P)
            sp.wait_ge(zero_ready, 1)
            for i in range(SLOTS * D // P // 1024):
                sp.dma_start(tz[:, i * 1024:(i + 1) * 1024], zero).then_inc(table_zero, 16)
            for half in range(2):
                sp.wait_ge(w_split, E1 * (half + 1))
                sp.dma_start(wst[:], w_up[:, half * E1:(half + 1) * E1, :]).then_inc(wst_in[1 + half], 16)
            sp.wait_ge(scattered, 16 * 2 * TILES)
            sp.wait_ge(table_zero, 64)
            for e in range(E2):
                if e >= 2:
                    sp.wait_ge(rowsT_ps, e - 1)
                buf = rows[:, :, (e % 2) * D:(e % 2 + 1) * D]
                sp.dma_start(buf, table[e * CAP:(e + 1) * CAP, :].rearrange("(t p) d -> p t d", p=P)) \
                    .then_inc(rows_in[e], 16)
                if e >= 2:
                    store_expert(sp, e - 2)
            store_expert(sp, E2 - 2)
            store_expert(sp, E2 - 1)
            for b in range(NBLK):
                sp.wait_ge(comb_ready, b + 1)
                sp.dma_start(tiles(ov, b), tiles(x_sb, b)).then_inc(stored, 16)
            sp.wait_ge(stored, 16 * NBLK)

        @block.gpsimd
        def _(pool):
            g = nc.gpsimd
            n = [0]

            def step(ins):
                n[0] += 1
                ins.then_inc(pool_step, 1)
                return n[0]

            g.memset(zero, 0.0).then_inc(zero_ready, 1)
            a = step(g.memset(mhalf[:], -0.5))
            g.memset(gwp[:], 0.0)
            g.memset(before[:, 0, :], 0.0)
            for par in range(2):
                for j in range(BT):
                    last = g.memset(vx[:, par, j, DH * HEADS:NH9], 1.0)
            last.then_inc(v_ones, 1)
            pool.wait_ge(pool_step, a)

            def inv_std(i, blk):
                pool.wait_ge(var_ready[i], blk + 1)
                a = step(g.tensor_scalar(tiles(ve[i], blk), tiles(mv[i], blk)[:, :, 1], LN_EPS, None, ALU.add))
                pool.wait_ge(pool_step, a)
                g.tensor_tensor(tiles(rstd[i], blk), tiles(ve[i], blk), mhalf[:], ALU.pow) \
                    .then_inc(rstd_ready[i], 1)

            def split(k):
                hi, lo = (w[:, k % E1, :] for w in up_weights(k))
                pool.wait_ge(wst_in[k // E1], 16)
                if k == E1:
                    pool.wait_ge(table_zero, 64)
                if k == 2 * E1:
                    pool.wait_ge(up_ps, NBLK * E1 * FC)
                a = step(g.tensor_copy(hi, wst[:, k % E1, :]))
                pool.wait_ge(pool_step, a)
                g.tensor_tensor(lo, wst[:, k % E1, :], hi.bitcast(F32), ALU.subtract).then_inc(w_split, 1)

            def difference(blk):
                pool.wait_ge(x1_ready, blk + 1)
                if blk >= 1:
                    pool.wait_ge(og_ps, blk)
                g.tensor_tensor(diff[:], cols(x1T, blk, 1), cols(x1T, blk, 0), ALU.subtract) \
                    .then_inc(diff_ready, 1)

            def rotate_sum(blk):
                pool.wait_ge(rot_parts, blk + 1)
                a = phi[:, blk % 2]
                g.tensor_tensor(a, a, rot_b[:], ALU.add).then_inc(rot_ready, 1)

            def outer(t):
                blk, j = t // BT, t % BT
                pool.wait_ge(phi_ready, blk + 1)
                if j == 0 and blk == 0:
                    pool.wait_ge(v_ones, 1)
                pool.wait_ge(qkv_ready, BT * blk + BT)
                if t >= 2:
                    pool.wait_ge(tail_ps, t - 1)
                k_ = phi[:, blk % 2, j, D:2 * D].rearrange("p (h d) -> p h d", h=HEADS)[:, None, :, :] \
                    .broadcast_to([P, M1, HEADS, DH])
                v_ = vx[:, blk % 2, j, :].rearrange("p (m h) -> p m h", m=M1)[:, :, :, None] \
                    .broadcast_to([P, M1, HEADS, DH])
                o_ = kv[:, t % 2, :].rearrange("p (m h d) -> p m h d", m=M1, h=HEADS)
                g.tensor_tensor(o_, k_, v_, ALU.mult).then_inc(kv_ready, 1)

            def scatter(k, t):
                g.indirect_dma_start(out=table, out_offset=bass.IndirectOffsetOnAxis(dest_i[:, k, t:t + 1], 0),
                                     in_=h3[:, t, :], in_offset=None).then_inc(scattered, 16)

            inv_std(0, 0)
            rotate_sum(0)
            outer(0)
            for s in range(STEPS):
                b, f = divmod(s, BT)
                if f == 0 and live(b + 1):
                    inv_std(0, b + 1)
                if f == 1 and live(b - 1):
                    inv_std(1, b - 1)
                if f == 3 and live(b + 1):
                    rotate_sum(b + 1)
                if s + 1 < TILES:
                    outer(s + 1)
                if f == 2 and live(b - 2):
                    inv_std(2, b - 2)
                if f == 3 and live(b):
                    difference(b)
                if s < 2 * E1:
                    split(s)
                if f == 3 and live(b - 3):
                    pool.wait_ge(first_ready, b - 2)
                    for j in range(BT):
                        scatter(0, BT * (b - 3) + j)
            pool.wait_ge(second_ready, 1)
            for t in range(TILES):
                scatter(1, t)
            for e in range(E1):
                split(2 * E1 + e)
            for half in eout_stored:
                pool.wait_ge(half, 16 * E2 // 2)
            for t in range(TILES):
                for k in range(2):
                    g.indirect_dma_start(out=back[:, t, k, :], out_offset=None, in_=expert_out,
                                         in_offset=bass.IndirectOffsetOnAxis(slot_i[:, k, t:t + 1], 0)) \
                        .then_inc(gathered[t], 16)

        @block.scalar
        def _(act):
            a_ = nc.scalar
            n = [0]

            act.wait_ge(small_in, 48)
            a_.activation(scT[:], s_sb[:, S_C:S_C + 2], ACT.Silu).then_inc(sc_ready, 1)

            def hT_evac(blk):
                b = blk // BPB
                act.wait_ge(hT_ps, blk + 1)
                if blk == 0:
                    act.wait_ge(mod_ready, 1)
                    act.wait_ge(pads_ready, 1)
                a_.activation(cols(hT, blk, 2), ps[:, B_D, :], ACT.Identity, bias=modT[:, 0, b:b + 1],
                              scale=modT[:, 1, b:b + 1]).then_inc(hT_ready, 1)
                act.wait_ge(hT_ready, blk + 1)
                if blk >= 1:
                    act.wait_ge(pw_ps, blk)
                a_.activation(conv[:], cols(hT, blk, 0), ACT.Copy, scale=s_sb[:, S_DW:S_DW + 1]) \
                    .then_inc(conv0_ready, 1)

            def qkv_evac(t):
                blk, j = t // BT, t % BT
                act.wait_ge(qkv_ps, t + 1)
                if j == 0 and blk >= 1:
                    act.wait_ge(rot_parts, blk)
                if j == 0 and blk >= 2:
                    act.wait_ge(kv_ready, BT * (blk - 1))
                    act.wait_ge(tail_ps, BT * (blk - 1))
                a_.activation(qk[:, j, :], ps[:, B_Q, 0:2 * D], ACT.Copy)
                a_.activation(vx[:, blk % 2, j, 0:D].rearrange("p (m h) -> p m h", m=DH),
                              ps[:, B_Q, 2 * D:3 * D].rearrange("p (h m) -> p m h", m=DH), ACT.Copy) \
                    .then_inc(qkv_ready, 1)

            def phi_exp(blk):
                act.wait_ge(rot_ready, blk + 1)
                if blk >= 1:
                    act.wait_ge(phi_ready, blk)
                a_.activation(rot_b[:], phi[:, blk % 2], ACT.Exp)
                a_.activation(qk[:], phi[:, blk % 2], ACT.Relu).then_inc(exp_ready, 1)

            def qT_evac(t):
                act.wait_ge(qT_ps, t + 1)
                if t >= 2:
                    act.wait_ge(tail_ps, t - 1)
                a_.activation(qT[:, t % 2, :], ps[:, B_Q, 384:512], ACT.Copy).then_inc(qT_ready, 1)

            def attT_evac(t):
                blk, j = t // BT, t % BT
                act.wait_ge(attT_ps, t + 1)
                if j == 0 and blk >= 1:
                    act.wait_ge(x2_ps, blk)
                a_.activation(attT[:, j * P:(j + 1) * P], ps[:, B_Q, 384:512], ACT.Copy).then_inc(attT_ready, 1)

            def gate_evac(blk):
                act.wait_ge(og_ps, blk + 1)
                if blk >= 1:
                    act.wait_ge(x2T_ready, blk)
                a_.activation(gate[:], ps[:, B_Q, :], ACT.Tanh, bias=hbg[:, 0:1], scale=0.5) \
                    .then_inc(gate_ready, 1)

            def x2_evac(blk):
                act.wait_ge(x2_ps, blk + 1)
                a_.activation(tiles(x2, blk), ps[:, B_D, :].rearrange("p (t d) -> p t d", t=BT), ACT.Copy) \
                    .then_inc(x2_ready, 1)

            def h2T_evac(blk):
                act.wait_ge(h2T_ps, blk + 1)
                if blk >= 1:
                    act.wait_ge(h2_split, blk)
                    act.wait_ge(mix_ps, blk)
                a_.activation(h2T[:], ps[:, B_D, :], ACT.Identity, bias=s_sb[:, S_LB:S_LB + 1],
                              scale=s_sb[:, S_LG:S_LG + 1]).then_inc(h2T_ready, 1)

            def mix_exps(blk):
                act.wait_ge(mix_shift, blk + 1)
                a_.activation(sm[:], sm[:], ACT.Exp).then_inc(mix_exp, 1)

            def gwT_evac(blk):
                act.wait_ge(gwT_ps, blk + 1)
                if blk >= 1:
                    act.wait_ge(b2_ps, blk)
                a_.activation(gwT[:], ps[:, B_D, 0:P], ACT.Copy).then_inc(gwT_ready, 1)

            def silu(u):
                e = u // FC
                act.wait_ge(up_ps, u + 1)
                if e >= 2:
                    act.wait_ge(down_ps, e - 1)
                c = S_B1 + u % (E1 * FC)
                a_.activation(hid[:, e % 2, u % FC, :], ps[:, B_UP[u % 2], :], ACT.Silu,
                              bias=s_sb[:, c:c + 1]).then_inc(hid_ready, 1)

            def h3T_evac(blk):
                act.wait_ge(h3T_ps, blk + 1)
                if blk >= 1:
                    act.wait_ge(route_ps, blk)
                a_.activation(h3T[:], ps[:, B_D, :], ACT.Copy).then_inc(h3T_ready, 1)

            def route_exps(blk):
                act.wait_ge(route_shift, blk + 1)
                a_.activation(gt_[:], gt_[:], ACT.Exp).then_inc(route_exp, 1)

            hT_evac(0)
            for j in range(BT):
                qkv_evac(j)
            phi_exp(0)
            for s in range(STEPS):
                b, f = divmod(s, BT)
                if s < TILES:
                    qT_evac(s)
                if 1 <= s <= TILES:
                    attT_evac(s - 1)
                if f == 0 and live(b - 3):
                    h3T_evac(b - 3)
                if f == 1 and live(b + 1):
                    hT_evac(b + 1)
                if f == 2:
                    if live(b - 1):
                        mix_exps(b - 1)
                    if live(b - 3):
                        route_exps(b - 3)
                if 0 <= s - LAG < NBLK * E1:
                    for c in range(FC):
                        silu((s - LAG) * FC + c)
                if f == 0 and live(b - 1):
                    gate_evac(b - 1)
                    x2_evac(b - 1)
                if f == 1 and live(b - 1):
                    h2T_evac(b - 1)
                if f == 2:
                    if live(b - 1):
                        gwT_evac(b - 1)
                    if live(b + 1):
                        for j in range(BT):
                            qkv_evac(BT * (b + 1) + j)
                if f == 3 and live(b + 1):
                    phi_exp(b + 1)

            for e in range(E2):
                act.wait_ge(rowsT_ps, e + 1)
                if e >= 2:
                    act.wait_ge(eup_ps, FC * (e - 1))
                a_.activation(h2h[:, e % 2, :], ps[:, e % 2, :], ACT.Copy).then_inc(rowsT_hi, 1)
                if e >= 1:
                    gelus(act, e - 1)
            gelus(act, E2 - 1)
            for t in range(TILES):
                act.wait_ge(gathered[t], 32)
                a_.activation(h3[:, t, :], back[:, t, 0, :], ACT.Copy, scale=gk[:, t, 0:1]).then_inc(comb0, 1)

        @block.vector
        def _(dve):
            v = nc.vector
            n = [0]

            def step(ins):
                n[0] += 1
                ins.then_inc(dve_step, 1)
                return n[0]

            def after(k=None):
                dve.wait_ge(dve_step, n[0] if k is None else k)

            v.memset(hT[:, :, 0:2], 0.0).then_inc(pads_ready, 1)

            statistics = []

            def stats(i, blk, src):
                if statistics:
                    dve.wait_ge(*statistics[-1])
                statistics.append((var_ready[i], blk + 1))
                for j in range(BT):
                    step(v.bn_stats(st[:, j, :], src[:, j, :]))
                after()
                for j in range(BT):
                    last = v.bn_aggr(tiles(mv[i], blk)[:, j, :], st[:, j, :])
                last.then_inc(var_ready[i], 1)

            def normalise(i, blk, src, dst, done):
                dve.wait_ge(rstd_ready[i], blk + 1)
                for j in range(BT):
                    t = BT * blk + j
                    last = v.tensor_scalar(dst[:, j, :], src[:, j, :], mv[i][:, t, 0:1], rstd[i][:, t:t + 1],
                                           ALU.subtract, ALU.mult)
                last.then_inc(done, 1)

            def modulation():
                dve.wait_ge(sc_ready, 1)
                v.tensor_copy(scb[:], scT[:, :, None].broadcast_to([P, 2, P])).then_inc(scb_ready, 1)
                v.tensor_scalar(hbg[:], s_sb[:, S_BG:S_BG + 1], 0.5, None, ALU.mult)
                dve.wait_ge(mod_ps, 1)
                v.tensor_copy(modT[:, 0, :], ps[:, B_D, 0:2])
                v.tensor_scalar(modT[:, 1, :], ps[:, B_D, 2:4], 1.0, None, ALU.add).then_inc(mod_ready, 1)

            def modulation_rows():
                dve.wait_ge(mod_ps, 2)
                for b in range(BATCH):
                    step(v.tensor_copy(modb[:, b].rearrange("p m d -> p (m d)"), ps[:, B_UP[b], :]))
                after()
                v.tensor_scalar(modb[:, :, 2, :], modb[:, :, 2, :], 1.0, None, ALU.add)
                for m in (0, 3):
                    s = modb[:, :, m, :]
                    t0, t1 = gtmp[:, 0], gtmp[:, 1]
                    step(v.tensor_scalar(t0, s, -1.0, None, ALU.mult))
                    after()
                    step(v.tensor_tensor(t1, t0, s, ALU.max))
                    after()
                    v.tensor_scalar(t1, t1, 0.25, None, ALU.max)
                    step(v.tensor_scalar(t0, s, 0.0, 2.0, ALU.is_ge, ALU.mult))
                    after()
                    step(v.tensor_scalar(t0, t0, -1.0, None, ALU.add))
                    after()
                    step(v.tensor_tensor(s, t0, t1, ALU.mult))
                    after()

            def ln1(blk):
                dve.wait_ge(x_in[blk], 16)
                stats(0, blk, tiles(x_sb, blk))

            def xhat(blk):
                if blk >= 1:
                    dve.wait_ge(hT_ps, blk)
                normalise(0, blk, tiles(x_sb, blk), xh, xh_ready)

            def conv_taps(blk):
                dve.wait_ge(conv0_ready, blk + 1)
                h = hT[:, blk // BPB, (blk % BPB) * W:(blk % BPB) * W + W + 2]
                step(v.scalar_tensor_tensor(conv[:], h[:, 1:1 + W], s_sb[:, S_DW + 1:S_DW + 2], conv[:],
                                            ALU.mult, ALU.add))
                after()
                v.scalar_tensor_tensor(conv[:], h[:, 2:2 + W], s_sb[:, S_DW + 2:S_DW + 3], conv[:],
                                       ALU.mult, ALU.add).then_inc(conv_ready, 1)

            def residual1(blk):
                dve.wait_ge(pw_ps, blk + 1)
                ins = v.tensor_tensor(cols(x1T, blk, 1), ps[:, B_D, :], cols(hT, blk, 2), ALU.add)
                if blk % BPB == 0:
                    step(ins)
                    after()
                    ins = v.tensor_copy(x1T[:, blk // BPB, 0:1], x1T[:, blk // BPB, 1:2])
                ins.then_inc(x1_ready, 1)

            def rotate(blk):
                dve.wait_ge(qkv_ready, BT * blk + BT)
                if blk >= 1:
                    dve.wait_ge(phi_ready, blk)
                if blk >= 2:
                    dve.wait_ge(tail_ps, BT * (blk - 1))
                    dve.wait_ge(kv_ready, BT * (blk - 1))
                i = blk % BPB * BT * DH
                cs, sn = (c_sb[:, c + i:c + i + BT * DH].rearrange("p (t e) -> p t e", t=BT)[:, :, None, :]
                          .broadcast_to([P, BT, 2 * HEADS, DH]) for c in (C_COS, C_SIN))
                q4 = qk[:].rearrange("p t (h e) -> p t h e", e=DH)
                v.tensor_tensor(phi[:, blk % 2].rearrange("p t (h e) -> p t h e", e=DH), q4, cs, ALU.mult)
                pair = lambda ap: ap.rearrange("p t h (f two) -> p t h f two", two=2)
                v.tensor_tensor(pair(rot_b[:].rearrange("p t (h e) -> p t h e", e=DH)), pair(q4)[:, :, :, :, ::-1],
                                pair(sn), ALU.mult).then_inc(rot_parts, 1)

            def feature(blk):
                dve.wait_ge(exp_ready, blk + 1)
                v.scalar_tensor_tensor(phi[:, blk % 2], rot_b[:], 1.0, qk[:], ALU.min, ALU.add).then_inc(phi_ready, 1)

            def attend(t):
                j, first, lastt = t % BT, t % TPB == 0, t % TPB == TPB - 1
                q_ = phi[:, t // BT % 2, j, 0:D]
                dve.wait_ge(cum_ps, t + 1)
                if t >= 1:
                    dve.wait_ge(att_ready, t)
                v.tensor_tensor(qp[:, 0:DH * D].rearrange("p (m c) -> p m c", m=DH),
                                ps[:, B_KV:B_KV + 2, :].rearrange("p b (m c) -> p (b m) c", m=4),
                                q_[:, None, :].broadcast_to([P, DH, D]), ALU.mult).then_inc(cum_read, 1)
                dve.wait_ge(tail_ps, t + 1)
                a = step(v.tensor_tensor(qp[:, DH * D:CH], ps[:, B_M, 0:D], q_, ALU.mult))
                if not lastt:
                    v.tensor_tensor(state[:], ps[:, B_M, 2 * D + 16:2 * D + 16 + NH9], headmask, ALU.mult) \
                        .then_inc(state_ready, 1) if first else state_add(t)
                else:
                    v.tensor_copy(state[0:1, 0:1], state[0:1, 0:1]).then_inc(state_ready, 1)
                dve.wait_ge(cum_read, t + 1)
                after(a)
                a = step(v.tensor_reduce(nd[:, 0, :], qp[:].rearrange("p (c d) -> p c d", d=DH), AX.X, ALU.add))
                after(a)
                if first:
                    r, ins = 0, v.tensor_copy(rden[:, 1, 0:1], nd[:, 0, 0:1])
                else:
                    r, ins = 1, v.tensor_tensor(nd[:, 1, :], ps[:, B_M, D:D + NH9], nd[:, 0, :], ALU.add)
                ins.then_inc(tail_read, 1)
                dve.wait_ge(tail_read, t + 1)
                a = step(v.tensor_scalar(rden[:, 0, :], nd[:, r, DH * HEADS:NH9], DEN_EPS, None, ALU.add))
                after(a)
                a = step(v.reciprocal(rden[:, 1, :], rden[:, 0, :]))
                after(a)
                if t >= 2:
                    dve.wait_ge(attT_ps, t - 1)
                v.tensor_tensor(att[:, t % 2, :].rearrange("p (h m) -> p m h", m=DH),
                                nd[:, r, 0:D].rearrange("p (m h) -> p m h", m=DH),
                                rden[:, 1, None, :].broadcast_to([P, DH, HEADS]), ALU.mult).then_inc(att_ready, 1)

            def state_add(t):
                a = step(v.tensor_tensor(gtmp[:, 0, 0:2].rearrange("p a d -> p (a d)")[:, 0:NH9],
                                         ps[:, B_M, 2 * D + 16:2 * D + 16 + NH9], headmask, ALU.mult))
                after(a)
                v.tensor_tensor(state[:], gtmp[:, 0, 0:2].rearrange("p a d -> p (a d)")[:, 0:NH9], state[:],
                                ALU.add).then_inc(state_ready, 1)

            def residual2(blk):
                dve.wait_ge(gate_ready, blk + 1)
                if blk >= 1:
                    dve.wait_ge(x2_ps, blk)
                step(v.scalar_tensor_tensor(x2T[:], gate[:], 1.0, ps[:, B_D, :], ALU.add, ALU.mult))
                after()
                v.scalar_tensor_tensor(x2T[:], x2T[:], 0.5, cols(x1T, blk, 1), ALU.mult, ALU.add) \
                    .then_inc(x2T_ready, 1)

            def ln2(blk):
                dve.wait_ge(x2_ready, blk + 1)
                stats(1, blk, tiles(x2, blk))

            def xhat2(blk):
                if blk >= 1:
                    dve.wait_ge(h2T_ps, blk)
                normalise(1, blk, tiles(x2, blk), xm, xm_ready)

            def split2(blk):
                dve.wait_ge(h2T_ready, blk + 1)
                if blk >= 2:
                    dve.wait_ge(up_ps, (blk - 1) * E1 * FC)
                i = blk % 2
                step(v.tensor_copy(h2h[:, i, :], h2T[:]))
                after()
                v.tensor_tensor(h2l[:, i, :], h2T[:], h2h[:, i, :].bitcast(F32), ALU.subtract).then_inc(h2_split, 1)

            def mix_a(blk):
                dve.wait_ge(mix_ps, blk + 1)
                lp = ps[:, B_D, 0:BT * E1].rearrange("p (t e) -> p t e", t=BT)
                step(v.tensor_reduce(sm_r[:, 0, :], lp, AX.X, ALU.max))
                after()
                v.tensor_tensor(sm[:], lp, sm_r[:, 0, :, None].broadcast_to([P, BT, E1]), ALU.subtract) \
                    .then_inc(mix_shift, 1)

            def mix_b(blk):
                dve.wait_ge(mix_exp, blk + 1)
                step(v.tensor_reduce(sm_r[:, 0, :], sm[:], AX.X, ALU.add))
                after()
                step(v.reciprocal(sm_r[:, 1, :], sm_r[:, 0, :]))
                after()
                if blk == 0:
                    dve.wait_ge(v_ones, 1)
                v.tensor_tensor(gwp[:, blk % 2, 0:BT * E1].rearrange("p (t e) -> p t e", t=BT), sm[:],
                                sm_r[:, 1, :, None].broadcast_to([P, BT, E1]), ALU.mult).then_inc(mix_ready, 1)

            def acc_start(blk):
                dve.wait_ge(b2_ps, blk + 1)
                v.tensor_tensor(acc[:], ps[:, B_D, :].rearrange("p (t d) -> p t d", t=BT), tiles(x2, blk),
                                ALU.add).then_inc(acc_ready, 1)
                dve.wait_ge(acc_ready, blk + 1)

            def add_expert(e):
                dve.wait_ge(down_ps, e + 1)
                for j in range(BT):
                    c = j * E1 + e % E1
                    last = v.scalar_tensor_tensor(acc[:, j, :], ps[:, B_DN, j * D:(j + 1) * D], gwp[:, e // E1 % 2, c:c + 1],
                                                  acc[:, j, :], ALU.mult, ALU.add)
                last.then_inc(down_added, 1)
                dve.wait_ge(down_added, e + 1)

            def residual3(blk):
                b = blk // BPB
                step(v.tensor_tensor(acc[:], acc[:], modb[:, b, 0, None, :].broadcast_to([P, BT, D]), ALU.mult))
                after()
                step(v.tensor_tensor(tiles(x_sb, blk), acc[:], tiles(x_sb, blk), ALU.add))
                after()

            def norm3(blk):
                b = blk // BPB
                dve.wait_ge(rstd_ready[2], blk + 1)
                for j in range(BT):
                    t = BT * blk + j
                    step(v.scalar_tensor_tensor(h3[:, t, :], x_sb[:, t, :], mv[2][:, t, 0:1], modb[:, b, 2, :],
                                                ALU.subtract, ALU.mult))
                after()
                for j in range(BT):
                    t = BT * blk + j
                    last = v.scalar_tensor_tensor(h3[:, t, :], h3[:, t, :], rstd[2][:, t:t + 1], modb[:, b, 1, :],
                                                  ALU.mult, ALU.add)
                last.then_inc(h3_ready, 1)

            def bc(ap):
                return ap[:, :, None].broadcast_to([P, BT, E2])

            def route_a(blk):
                dve.wait_ge(route_ps, blk + 1)
                step(v.tensor_copy(lg[:], ps[:, B_D, 0:BT * E2].rearrange("p (t e) -> p t e", t=BT)))
                after()
                step(v.tensor_reduce(rs[:, 0, :], lg[:], AX.X, ALU.max))
                after()
                v.tensor_tensor(gt_[:], lg[:], bc(rs[:, 0, :]), ALU.subtract).then_inc(route_shift, 1)

            def first_of_max(src, mx, rank, onehot):
                rev = c_sb[:, None, C_REV:C_REV + E2].broadcast_to([P, BT, E2])
                step(v.tensor_reduce(mx, src, AX.X, ALU.max))
                after()
                step(v.tensor_tensor(rt[:, 0], src, bc(mx), ALU.is_equal))
                after()
                step(v.tensor_tensor(rt[:, 1], rt[:, 0], rev, ALU.mult))
                after()
                step(v.tensor_reduce(rank, rt[:, 1], AX.X, ALU.max))
                after()
                step(v.tensor_tensor(onehot, rt[:, 1], bc(rank), ALU.is_equal))
                after()

            def route_b(blk):
                dve.wait_ge(route_exp, blk + 1)
                o = tiles(oh, blk)
                step(v.tensor_reduce(rs[:, 1, :], gt_[:], AX.X, ALU.add))
                after()
                step(v.reciprocal(rs[:, 2, :], rs[:, 1, :]))
                after()
                step(v.tensor_tensor(gt_[:], gt_[:], bc(rs[:, 2, :]), ALU.mult))
                after()
                first_of_max(gt_[:], rs[:, 3, :], rs[:, 4, :], o[:, :, 0:E2])
                step(v.scalar_tensor_tensor(lg[:], o[:, :, 0:E2], -BIG, lg[:], ALU.mult, ALU.add))
                after()
                first_of_max(lg[:], rs[:, 5, :], rs[:, 6, :], o[:, :, E2:2 * E2])
                step(v.tensor_copy(tiles(ohb, blk), o))
                after()
                if blk == 0:
                    dve.wait_ge(v_ones, 1)
                for j in range(BT):
                    t = BT * blk + j
                    ins = v.tensor_tensor(before[:, t + 1, :], before[:, t, :], ohb[:, t, :], ALU.add)
                    if j == BT - 1:
                        ins.then_inc(onehot_ready, 1)
                    else:
                        step(ins)
                        after()
                step(v.tensor_tensor(rt[:, 2], gt_[:], o[:, :, E2:2 * E2], ALU.mult))
                after()
                step(v.tensor_reduce(rs[:, 7, :], rt[:, 2], AX.X, ALU.add))
                after()
                step(v.tensor_tensor(rs[:, 8, :], rs[:, 3, :], rs[:, 7, :], ALU.add))
                after()
                step(v.tensor_scalar(rs[:, 8, :], rs[:, 8, :], 1e-9, None, ALU.max))
                after()
                step(v.reciprocal(rs[:, 9, :], rs[:, 8, :]))
                after()
                for k, gsrc, rsrc in ((0, 3, 4), (1, 7, 6)):
                    v.tensor_tensor(tiles(gk, blk)[:, :, k], rs[:, gsrc, :], rs[:, 9, :], ALU.mult)
                    step(v.tensor_scalar(tiles(exps, blk)[:, :, k], rs[:, rsrc, :], -float(CAP), float(SLOTS),
                                         ALU.mult, ALU.add))
                after()

            def route_c(blk):
                dve.wait_ge(pos_ps, blk + 1)
                o = tiles(oh, blk)
                pp = ps[:, B_D, 0:BT * 2 * E2].rearrange("p (t e) -> p t e", t=BT)
                for k in range(2):
                    step(v.tensor_tensor(rt[:, k], pp[:, :, k * E2:(k + 1) * E2], o[:, :, k * E2:(k + 1) * E2],
                                         ALU.mult))
                after()
                for k in range(2):
                    step(v.tensor_reduce(tiles(loc, blk)[:, :, k], rt[:, k], AX.X, ALU.add))
                after()
                place(0, blk * BT, BT, first_ready)

            def place(k, t0, nt, done):
                r = lambda ap: ap[:, t0:t0 + nt, k]
                step(v.tensor_scalar(r(over), r(loc), float(CAP), None, ALU.is_ge))
                step(v.scalar_tensor_tensor(r(slot), r(loc), float(CAP - 1), r(exps), ALU.min, ALU.add))
                after()
                tr = c_sb[:, C_TR + k * TILES + t0:C_TR + k * TILES + t0 + nt]
                step(v.tensor_tensor(r(dest), tr, r(slot), ALU.subtract))
                after()
                step(v.tensor_tensor(r(dest), r(dest), r(over), ALU.mult))
                after()
                step(v.tensor_tensor(r(dest), r(dest), r(slot), ALU.add))
                after()
                step(v.tensor_copy(slot_i[:, k, t0:t0 + nt], r(slot)))
                v.tensor_copy(dest_i[:, k, t0:t0 + nt], r(dest)).then_inc(done, 1)
                step(v.tensor_tensor(r(over), r(gk), r(over), ALU.mult))
                after()
                step(v.tensor_tensor(r(gk), r(gk), r(over), ALU.subtract))
                after()

            def route_d():
                dve.wait_ge(total_ps, 1)
                step(v.tensor_tensor(lt[:], oh[:, :, E2:2 * E2],
                                     ps[:, B_D, None, 0:E2].broadcast_to([P, TILES, E2]), ALU.mult))
                after()
                step(v.tensor_reduce(over[:, :, 1], lt[:], AX.X, ALU.add))
                after()
                step(v.tensor_tensor(loc[:, :, 1], loc[:, :, 1], over[:, :, 1], ALU.add))
                after()
                place(1, 0, TILES, second_ready)

            ln1(0)
            dve.wait_ge(small_in, 48)
            modulation()
            xhat(0)
            conv_taps(0)
            modulation_rows()
            residual1(0)
            rotate(0)
            feature(0)
            for s in range(STEPS):
                b, f = divmod(s, BT)
                if 0 <= s - LAG - 1 < NBLK * E1:
                    add_expert(s - LAG - 1)
                if f == 0 and live(b + 1):
                    ln1(b + 1)
                if f == 1 and live(b - 1):
                    ln2(b - 1)
                if f == 2 and live(b - 1):
                    mix_a(b - 1)
                if f == 3 and live(b + 1):
                    rotate(b + 1)
                if s < TILES:
                    attend(s)
                if f == 0:
                    if live(b - 1):
                        residual2(b - 1)
                    if live(b - 3):
                        route_a(b - 3)
                    if live(b + 1):
                        xhat(b + 1)
                if f == 1:
                    if live(b + 1):
                        conv_taps(b + 1)
                    if live(b - 1):
                        xhat2(b - 1)
                    if live(b + 1):
                        residual1(b + 1)
                    if live(b - 1):
                        split2(b - 1)
                if f == 2:
                    if live(b - 1):
                        mix_b(b - 1)
                    if live(b - 2):
                        residual3(b - 2)
                        stats(2, b - 2, tiles(x_sb, b - 2))
                    if live(b - 1):
                        acc_start(b - 1)
                    if live(b - 3):
                        route_b(b - 3)
                if f == 3:
                    if live(b - 2):
                        norm3(b - 2)
                    if live(b - 3):
                        route_c(b - 3)
                    if live(b + 1):
                        feature(b + 1)
            route_d()

            def low_part(e):
                dve.wait_ge(rowsT_hi, e + 1)
                if e >= 2:
                    dve.wait_ge(eup_ps, FC * (e - 1))
                v.tensor_tensor(h2l[:, e % 2, :], ps[:, e % 2, :], h2h[:, e % 2, :].bitcast(F32), ALU.subtract) \
                    .then_inc(rowsT_lo, 1)

            low_part(0)
            for e in range(E2):
                if e + 1 < E2:
                    low_part(e + 1)
                dve.wait_ge(edown_ps, e + 1)
                if e >= 2:
                    dve.wait_ge(eout_stored[e % 2], 16 * (e // 2))
                v.tensor_copy(xstage(e), ps[:, 6 + e % 2, :].rearrange("p (t d) -> p t d", t=BT)) \
                    .then_inc(eout_ready, 1)
            for blk in range(NBLK):
                for j in range(BT):
                    t = BT * blk + j
                    dve.wait_ge(comb0, t + 1)
                    step(v.scalar_tensor_tensor(h3[:, t, :], back[:, t, 1, :], gk[:, t, 1:2], h3[:, t, :],
                                                ALU.mult, ALU.add))
                after()
                step(v.tensor_tensor(tiles(h3, blk), tiles(h3, blk),
                                     modb[:, blk // BPB, 3, None, :].broadcast_to([P, BT, D]), ALU.mult))
                after()
                v.tensor_tensor(tiles(x_sb, blk), tiles(x_sb, blk), tiles(h3, blk), ALU.add).then_inc(comb_ready, 1)

        @block.tensor
        def _(pe):
            m = nc.tensor
            freed = {}

            def claim(bank, reader, count):
                if bank in freed:
                    pe.wait_ge(*freed[bank])
                freed[bank] = (reader, count)

            def mm(o, l, r, start=True, stop=True):
                return m.matmul(o, l, r, start=start, stop=stop)

            def modulation():
                pe.wait_ge(mod_in, 16)
                pe.wait_ge(sc_ready, 1)
                claim(B_D, mod_ready, 1)
                for i in range(2):
                    last = mm(ps[:, B_D, 2 * i:2 * i + 2], wmod_sb[:, i * D:(i + 1) * D], scT[:])
                last.then_inc(mod_ps, 1)

            def modulation_rows():
                pe.wait_ge(scb_ready, 1)
                for b in range(BATCH):
                    last = mm(ps[:, B_UP[b], :], scb[:, b, :], wmod_sb[:, 2 * D:6 * D])
                last.then_inc(mod_ps, 1)
                freed[B_UP[0]] = freed[B_UP[1]] = (x1_ready, 1)

            def transposes(bank, src, src_ready, count, done, reader):
                pe.wait_ge(src_ready, count)
                claim(bank, reader, count)
                for j in range(BT):
                    last = m.transpose(ps[:, bank, j * P:(j + 1) * P], src[:, j], ident)
                last.then_inc(done, 1)

            def pointwise(blk):
                pe.wait_ge(conv_ready, blk + 1)
                if blk == 0:
                    pe.wait_ge(proj_in, 16)
                claim(B_D, x1_ready, blk + 1)
                mm(ps[:, B_D, :], proj_sb[:, 0:P], conv[:]).then_inc(pw_ps, 1)

            def qkv(t):
                blk = t // BT
                pe.wait_ge(x1_ready, blk + 1)
                claim(B_Q, qkv_ready, t + 1)
                o = 1 + (t % TPB) * P
                mm(ps[:, B_Q, 0:3 * D], x1T[:, blk // BPB, o:o + P], proj_sb[:, P:4 * P]).then_inc(qkv_ps, 1)

            def q_transpose(t):
                pe.wait_ge(phi_ready, t // BT + 1)
                claim(B_Q, qT_ready, t + 1)
                m.transpose(ps[:, B_Q, 384:512], phi[:, t // BT % 2, t % BT, 0:D], ident).then_inc(qT_ps, 1)

            def prefix(t):
                blk, j = t // BT, t % BT
                kv_ = kv[:, t % 2, :]
                pe.wait_ge(kv_ready, t + 1)
                claim(B_KV, cum_read, t + 1)
                mm(ps[:, B_KV, :], tri, kv_[:, 0:512])
                mm(ps[:, B_KV + 1, :], tri, kv_[:, 512:1024]).then_inc(cum_ps, 1)
                claim(B_M, tail_read, t + 1)
                if t % TPB != TPB - 1:
                    mm(ps[:, B_M, 2 * D + 16:2 * D + 16 + NH9], phi[:, blk % 2, j, D:2 * D], vx[:, blk % 2, j, :])
                if t % TPB != 0:
                    pe.wait_ge(qT_ready, t + 1)
                    pe.wait_ge(state_ready, t)
                    mm(ps[:, B_M, D:D + NH9], qT[:, t % 2, :], state[:])
                mm(ps[:, B_M, 0:D], tri, kv_[:, 1024:CH]).then_inc(tail_ps, 1)

            def att_transpose(t):
                pe.wait_ge(att_ready, t + 1)
                claim(B_Q, attT_ready, t + 1)
                m.transpose(ps[:, B_Q, 384:512], att[:, t % 2, :], ident).then_inc(attT_ps, 1)

            def out_and_gate(blk):
                pe.wait_ge(attT_ready, BT * (blk + 1))
                pe.wait_ge(diff_ready, blk + 1)
                claim(B_D, x2T_ready, blk + 1)
                mm(ps[:, B_D, :], proj_sb[:, 4 * P:5 * P], attT[:])
                claim(B_Q, gate_ready, blk + 1)
                mm(ps[:, B_Q, :], proj_sb[:, 5 * P:6 * P], diff[:]).then_inc(og_ps, 1)

            def x2_transposes(blk):
                pe.wait_ge(x2T_ready, blk + 1)
                claim(B_D, x2_ready, blk + 1)
                for j in range(BT):
                    last = m.transpose(ps[:, B_D, j * P:(j + 1) * P], x2T[:, j * P:(j + 1) * P], ident)
                last.then_inc(x2_ps, 1)

            def mix_logits(blk):
                pe.wait_ge(h2T_ready, blk + 1)
                claim(B_D, mix_shift, blk + 1)
                for j in range(BT):
                    last = mm(ps[:, B_D, j * E1:(j + 1) * E1], h2T[:, j * P:(j + 1) * P], s_sb[:, S_MG:S_MG + E1])
                last.then_inc(mix_ps, 1)

            def mix_weights_transpose(blk):
                pe.wait_ge(mix_ready, blk + 1)
                claim(B_D, gwT_ready, blk + 1)
                m.transpose(ps[:, B_D, 0:P], gwp[:, blk % 2, :], ident).then_inc(gwT_ps, 1)

            def mix_bias(blk):
                pe.wait_ge(gwT_ready, blk + 1)
                if blk == 0:
                    pe.wait_ge(w2_in, 32)
                claim(B_D, acc_ready, blk + 1)
                for j in range(BT):
                    last = mm(ps[:, B_D, j * D:(j + 1) * D], gwT[:], b2_sb[:, j, :])
                last.then_inc(b2_ps, 1)

            def three_pass(o, wh, wl, ah, al):
                mm(o, wh, ah, stop=False)
                mm(o, wh, al, start=False, stop=False)
                return mm(o, wl, ah, start=False)

            def up(u):
                e = u // FC
                blk, c = e // E1, u % FC
                pe.wait_ge(h2_split, blk + 1)
                if blk == 0:
                    pe.wait_ge(w_split, e + 1)
                claim(B_UP[u % 2], hid_ready, u + 1)
                w_ = slice(c * P, (c + 1) * P)
                three_pass(ps[:, B_UP[u % 2], :], w1h[:, e % E1, w_], w1l[:, e % E1, w_], h2h[:, blk % 2, :],
                           h2l[:, blk % 2, :]).then_inc(up_ps, 1)

            def down(bank, w_, h, done, ready, count):
                for j in range(BT):
                    for c in range(FC):
                        if j == 0:
                            pe.wait_ge(ready, count + c + 1)
                        last = mm(ps[:, bank, j * D:(j + 1) * D], h[:, c, j * P:(j + 1) * P], w_[:, c, :],
                                  start=(c == 0), stop=(c == FC - 1))
                last.then_inc(done, 1)

            def route_logits(blk):
                pe.wait_ge(h3T_ready, blk + 1)
                claim(B_D, route_shift, blk + 1)
                for j in range(BT):
                    last = mm(ps[:, B_D, j * E2:(j + 1) * E2], h3T[:, j * P:(j + 1) * P], s_sb[:, S_WG:S_WG + E2])
                last.then_inc(route_ps, 1)

            def positions(blk):
                pe.wait_ge(onehot_ready, blk + 1)
                claim(B_D, first_ready, blk + 1)
                for j in range(BT):
                    t = BT * blk + j
                    o = ps[:, B_D, j * 2 * E2:(j + 1) * 2 * E2]
                    mm(o, strict, ohb[:, t, :], stop=False)
                    last = mm(o, ones, before[:, t, :], start=False)
                last.then_inc(pos_ps, 1)

            pe.wait_ge(small_in, 48)
            modulation()
            transposes(B_D, xh, xh_ready, 1, hT_ps, hT_ready)
            modulation_rows()
            pointwise(0)
            for j in range(BT):
                qkv(j)
            for s in range(STEPS):
                b, f = divmod(s, BT)
                e = s - LAG
                if s < TILES:
                    q_transpose(s)
                    prefix(s)
                if 1 <= s <= TILES:
                    att_transpose(s - 1)
                if 0 <= e < NBLK * E1:
                    for c in range(FC):
                        up(e * FC + c)
                if f == 0 and live(b - 1):
                    out_and_gate(b - 1)
                if f == 1:
                    if live(b + 1):
                        pointwise(b + 1)
                    if live(b - 1):
                        transposes(B_D, xm, xm_ready, b, h2T_ps, h2T_ready)
                if f == 2:
                    if live(b - 1):
                        mix_weights_transpose(b - 1)
                    if live(b + 1):
                        qkv(BT * (b + 1))
                        qkv(BT * (b + 1) + 1)
                if f == 3 and live(b - 3):
                    positions(b - 3)
                if 0 <= e < NBLK * E1:
                    claim(B_DN, down_added, e + 1)
                    down(B_DN, w2_sb[:, e % E1], hid[:, e % 2], down_ps, hid_ready, e * FC)
                if f == 0:
                    if live(b - 1):
                        x2_transposes(b - 1)
                    if live(b - 3):
                        route_logits(b - 3)
                    if live(b + 1):
                        transposes(B_D, xh, xh_ready, b + 2, hT_ps, hT_ready)
                if f == 1 and live(b - 1):
                    mix_logits(b - 1)
                if f == 2:
                    if live(b - 1):
                        mix_bias(b - 1)
                    if live(b + 1):
                        qkv(BT * (b + 1) + 2)
                        qkv(BT * (b + 1) + 3)
                if f == 3 and live(b - 2):
                    transposes(B_D, tiles(h3, b - 2), h3_ready, b - 1, h3T_ps, h3T_ready)
            claim(B_D, second_ready, 1)
            mm(ps[:, B_D, 0:2 * E2], ones, before[:, TILES, :]).then_inc(total_ps, 1)

            def rows_transpose(e):
                pe.wait_ge(rows_in[e], 16)
                claim(e % 2, rowsT_lo, e + 1)
                for j in range(BT):
                    last = m.transpose(ps[:, e % 2, j * P:(j + 1) * P], rows[:, j, (e % 2) * D:(e % 2 + 1) * D], ident)
                last.then_inc(rowsT_ps, 1)

            rows_transpose(0)
            pe.wait_ge(wd_in, 16)
            for e in range(E2):
                if e + 1 < E2:
                    rows_transpose(e + 1)
                pe.wait_ge(rowsT_lo, e + 1)
                pe.wait_ge(w_split, E1 + e + 1)
                wh, wl = up_weights(E1 + e)
                for c in range(FC):
                    u = e * FC + c
                    claim(2 + u % 2, ehid_ready, u + 1)
                    w_ = slice(c * P, (c + 1) * P)
                    three_pass(ps[:, 2 + u % 2, :], wh[:, e % E1, w_], wl[:, e % E1, w_], h2h[:, e % 2, :],
                               h2l[:, e % 2, :]).then_inc(eup_ps, 1)
                claim(6 + e % 2, eout_ready, e + 1)
                down(6 + e % 2, wd_sb[:, e], hid[:, e % 2], edown_ps, ehid_ready, e * FC)


def kernel(**inputs):
    import ml_dtypes
    import numpy as np
    import concourse.bacc as bacc
    from concourse.bass_utils import run_bass_kernel_spmd

    a = {k: np.asarray(v) for k, v in inputs.items()}
    f = np.float32
    col = lambda v: v.reshape(-1, P).T
    small = np.concatenate([
        a["L0_attn_w_dw"], col(a["L0_attn_b_gate"]), col(a["L0_attn_ln_g"]), col(a["L0_attn_ln_b"]),
        a["L0_attn_w_moe_gate"].T, col(a["L0_attn_b1"]), a["L0_ffn_wg"], a["L0_c"].T], axis=1)
    proj = np.concatenate([a["L0_attn_w_pw"].T, a["L0_attn_w_qkv"].T, a["L0_attn_w_o"].T, a["L0_attn_w_gate"].T],
                          axis=1)
    w1 = a["L0_attn_w1"].transpose(2, 0, 1)
    w2 = a["L0_attn_w2"].reshape(E1, D, FC, P).transpose(3, 0, 2, 1)
    b2 = np.zeros((P, BT, D), f)
    for j in range(BT):
        b2[j * E1:(j + 1) * E1, j, :] = a["L0_attn_b2"]
    w_up = a["L0_ffn_w_gate"].transpose(1, 0, 2)
    w_down = a["L0_ffn_w_down"].reshape(E2, FC, P, D).transpose(2, 0, 1, 3)

    const = np.zeros((P, N_CONST), f)
    i = np.arange(P)
    const[:, C_ID:C_ID + P] = i[:, None] == i
    const[:, C_TRI:C_TRI + P] = i[:, None] <= i
    const[:, C_BD:C_BD + NH9] = (i // DH)[:, None] == np.arange(NH9) % HEADS
    inv = (f(1) / f(10000) ** (np.arange(0, DH, 2, dtype=f) / f(DH))).astype(f)
    theta = (np.arange(SEQ, dtype=f)[:, None] * inv).astype(f)
    cos = np.repeat(np.cos(theta), 2, axis=1).reshape(TPB, P, DH).transpose(1, 0, 2)
    sin = (np.repeat(np.sin(theta), 2, axis=1) * np.tile([-1, 1], DH // 2)).reshape(TPB, P, DH).transpose(1, 0, 2)
    const[:, C_COS:C_COS + TPB * DH] = cos.reshape(P, -1)
    const[:, C_SIN:C_SIN + TPB * DH] = sin.reshape(P, -1)
    const[:, C_REV:C_REV + E2] = E2 - np.arange(E2)
    const[:, C_TR:] = SLOTS + np.arange(2 * TILES) * P + i[:, None]
    cmask = np.stack([i[:, None] < i, np.ones((P, P), bool)], axis=1).astype(ml_dtypes.bfloat16)

    arrays = {"x": a["L0_attn_x"], "small": small, "proj": proj, "wmod": a["L0_wmod"], "w1": w1, "w2": w2,
              "b2": b2, "w_up": w_up, "w_down": w_down, "const": const, "cmask": cmask}
    arrays = {f"in_{k}": np.ascontiguousarray(v) for k, v in arrays.items()}
    nc = bacc.Bacc("TRN2", target_bir_lowering=False, num_devices=1)
    args = [nc.dram_tensor(k, v.shape, mybir.dt.from_np(v.dtype), kind="ExternalInput").ap()
            for k, v in arrays.items()]
    args.append(nc.dram_tensor("out", (BATCH, SEQ, D), F32, kind="ExternalOutput").ap())
    block_kernel(nc, *args)
    r = run_bass_kernel_spmd(nc, [arrays], core_ids=[0])
    return r.results[0]["out"]
```

```python
from contextlib import ExitStack

import concourse.bass as bass
from concourse import mybir

F32 = mybir.dt.float32
F32R = mybir.dt.float32r
BF16 = mybir.dt.bfloat16
U32 = mybir.dt.uint32
ALU = mybir.AluOpType
ACT = mybir.ActivationFunctionType
AX = mybir.AxisListType

P = 128
BATCH, SEQ, D = 2, 1024, 128
TOKENS = BATCH * SEQ
TILES = TOKENS // P
BT = 4
NBLK = TILES // BT
W = BT * P
TPB = SEQ // P
BPB = SEQ // W
HEADS = 16
DH = D // HEADS
M1 = DH + 1
CH = M1 * D
NH9 = M1 * HEADS
E1 = 4
FC = 4
E2 = 8
CAP = 2 * TOKENS // E2
SLOTS = E2 * CAP
ROW = D + 3
LINE1 = TOKENS + CAP
LINE2 = TOKENS
LN_EPS = 1e-5
DEN_EPS = 1e-6
BIG = 3.0e38
MOD = 6

S_DW, S_BG, S_LG, S_LB, S_MG, S_B1, S_WG, S_C = 0, 3, 4, 5, 6, 10, 26, 34
N_SMALL = 36
C_ID, C_TRI, C_BD, C_COS, C_SIN, C_REV, C_TOK, C_SLOT, C_TRASH = 0, 128, 256, 400, 464, 528, 536, 552, 556
N_CONST = C_TRASH + E2 * BT


def block_kernel(nc, x, small, proj, wmod, w1, w2, b2, w_up, w_down, const, cmask, out):
    with ExitStack() as ctx:
        def sb(name, shape, dt=F32):
            return ctx.enter_context(nc.sbuf_tensor(name, shape, dt))

        def sem(name):
            return ctx.enter_context(nc.semaphore(name))

        line1 = nc.dram_tensor("line1", (E2 * LINE1, ROW), F32).ap()
        line2 = nc.dram_tensor("line2", (E2 * LINE2, ROW), F32).ap()
        chosen = nc.dram_tensor("chosen", (2 * TOKENS + SLOTS, D), F32).ap()

        ps = ctx.enter_context(nc.psum_tensor("ps", [P, 8, 512], F32))
        B_D, B_Q, B_KV, B_M, B_UP, B_DN = 0, 1, 2, 4, (5, 6), 7

        c_sb = sb("c_sb", [P, N_CONST])
        cm_sb = sb("cm_sb", [P, 2, P], BF16)
        s_sb = sb("s_sb", [P, N_SMALL])
        proj_sb = sb("proj_sb", [P, 6 * P])
        ident = c_sb[:, C_ID:C_ID + P]
        tri = c_sb[:, C_TRI:C_TRI + P]
        headmask = c_sb[:, C_BD:C_BD + NH9]
        strict, ones = cm_sb[:, 0, :], cm_sb[:, 1, :]
        wmod_sb = sb("wmod_sb", [P, MOD * D])
        w2_sb = sb("w2_sb", [P, E1, FC, D])
        b2_sb = sb("b2_sb", [P, BT, D])
        wd_sb = sb("wd_sb", [P, E2, FC, D])
        wst = sb("wst", [P, E1, W])
        w1h, w1l = sb("w1h", [P, E1, W], F32R), sb("w1l", [P, E1, W], F32R)
        wuh, wul = sb("wuh", [P, E1, W], F32R), sb("wul", [P, E1, W], F32R)
        x_sb = sb("x_sb", [P, TILES, D])
        x2 = sb("x2", [P, TILES, D])
        h3r = sb("h3r", [P, TILES, ROW])
        h3 = h3r[:, :, 0:D]
        wide = sb("wide", [P, BATCH * (3 + 2 * SEQ)])
        hT = wide[:, 0:BATCH * (2 + SEQ)].rearrange("p (b s) -> p b s", b=BATCH)
        x1T = wide[:, BATCH * (2 + SEQ):].rearrange("p (b s) -> p b s", b=BATCH)
        xh = sb("xh", [P, BT, D])
        xm = sb("xm", [P, BT, D])
        conv = sb("conv", [P, W])
        diff = sb("diff", [P, W])
        qk = sb("qk", [P, BT, 2 * D])
        vx = sb("vx", [P, 2, BT, NH9])
        rot_b = sb("rot_b", [P, BT, 2 * D])
        phi = sb("phi", [P, 2, BT, 2 * D])
        kv = sb("kv", [P, 2, CH])
        qp = sb("qp", [P, CH])
        qT = sb("qT", [P, 2, D])
        state = sb("state", [P, NH9])
        nd = sb("nd", [P, 2, NH9])
        rden = sb("rden", [P, 2, HEADS])
        att = sb("att", [P, 2, D])
        attT = sb("attT", [P, W])
        gate = wmod_sb[:, 0:W]
        x2T = attT
        h2T = sb("h2T", [P, W])
        h2h, h2l = sb("h2h", [P, 2, W], F32R), sb("h2l", [P, 2, W], F32R)
        hid = sb("hid", [P, 2, FC, W])
        acc = sb("acc", [P, BT, D])
        gwT = sb("gwT", [P, P])
        gwp = sb("gwp", [P, 2, P])
        h3T = sb("h3T", [P, W])
        st = sb("st", [P, BT, 6])
        mv = [sb(f"mv{i}", [P, TILES, 2]) for i in range(3)]
        ve = [sb(f"ve{i}", [P, TILES]) for i in range(3)]
        rstd = [sb(f"rstd{i}", [P, TILES]) for i in range(3)]
        mhalf = sb("mhalf", [P, BT])
        zero = wuh[:, 0:2, :].bitcast(F32).rearrange("p e f -> p (e f)")
        scT = sb("scT", [P, 2])
        scb = sb("scb", [P, 2, P])
        modT = sb("modT", [P, 2, 2])
        hbg = sb("hbg", [P, 1])
        modb = sb("modb", [P, BATCH, 4, D])
        gtmp = sb("gtmp", [P, 2, BATCH, D])
        sm = sb("sm", [P, BT, 4])
        sm_r = sb("sm_r", [P, 2, BT])
        lg = sb("lg", [P, BT, E2])
        gt_ = sb("gt_", [P, BT, E2])
        rt = sb("rt", [P, 4, BT, E2])
        rs = sb("rs", [P, 10, BT])
        oh = sb("oh", [P, TILES, 2 * E2])
        ohb = sb("ohb", [P, TILES, 2 * E2], BF16)
        before = sb("before", [P, TILES + 1, 2 * E2], BF16)
        exps = sb("exps", [P, TILES, 2])
        loc = sb("loc", [P, TILES, 2])
        dest = sb("dest", [P, TILES, 2])
        dest_i = sb("dest_i", [P, TILES, 2], U32)
        count = sb("count", [P, E2])
        count_i = sb("count_i", [P, E2], U32)
        second = sb("second", [P, E2, BT])
        trash = sb("trash", [P, E2, BT])
        addr = sb("addr", [P, 4, BT])
        row_w = sb("row_w", [P, E2, BT])
        back_i = sb("back_i", [P, E2, BT], U32)
        back = wide[:, 0:TILES * 2 * D].rearrange("p (k t d) -> p k t d", t=TILES, k=2)

        def rows(e):
            return phi[:, e % 2].rearrange("p t d -> p (t d)")[:, 0:BT * ROW].rearrange("p (t d) -> p t d", t=BT)

        L = lambda n: [sem(f"{n}_{i}") for i in range(NBLK)]
        x_in = L("x_in")
        small_in, mod_in, proj_in, w2_in, wd_in = (sem(n) for n in ("small_in", "mod_in", "proj_in", "w2_in", "wd_in"))
        wst_in = [sem(f"wst_in_{i}") for i in range(3)]
        w_split = sem("w_split")
        zero_ready, zeroed = sem("zero_ready"), sem("zeroed")
        sc_ready, scb_ready, mod_ps, mod_ready = (sem(n) for n in ("sc_ready", "scb_ready", "mod_ps", "mod_ready"))
        pads_ready, v_ones = sem("pads_ready"), sem("v_ones")
        dve_step, pool_step, act_step = sem("dve_step"), sem("pool_step"), sem("act_step")
        var_ready = [sem(f"var{i}_ready") for i in range(3)]
        rstd_ready = [sem(f"rstd{i}_ready") for i in range(3)]
        xh_ready, hT_ps, hT_ready, conv0_ready, conv_ready, pw_ps, x1_ready, diff_ready = (
            sem(n) for n in ("xh_ready", "hT_ps", "hT_ready", "conv0_ready", "conv_ready", "pw_ps", "x1_ready",
                             "diff_ready"))
        qkv_ps, qkv_ready, rot_parts, rot_ready, exp_ready, phi_ready = (
            sem(n) for n in ("qkv_ps", "qkv_ready", "rot_parts", "rot_ready", "exp_ready", "phi_ready"))
        kv_ready, cum_ps, tail_ps, qT_ps, qT_ready, cum_read, tail_read, state_ready, att_ready, attT_ps, attT_ready = (
            sem(n) for n in ("kv_ready", "cum_ps", "tail_ps", "qT_ps", "qT_ready", "cum_read", "tail_read",
                             "state_ready", "att_ready", "attT_ps", "attT_ready"))
        og_ps, gate_ready, x2T_ready, x2_ps, x2_ready, xm_ready, h2T_ps, h2T_ready, h2_split = (
            sem(n) for n in ("og_ps", "gate_ready", "x2T_ready", "x2_ps", "x2_ready", "xm_ready", "h2T_ps",
                             "h2T_ready", "h2_split"))
        mix_ps, mix_shift, mix_exp, mix_ready, gwT_ps, gwT_ready, b2_ps, acc_ready = (
            sem(n) for n in ("mix_ps", "mix_shift", "mix_exp", "mix_ready", "gwT_ps", "gwT_ready", "b2_ps",
                             "acc_ready"))
        up_ps, hid_ready, down_ps, down_added = (sem(n) for n in ("up_ps", "hid_ready", "down_ps", "down_added"))
        h3_ready, h3T_ps, h3T_ready, route_ps, route_shift, route_exp, onehot_ready, pos_ps, dest_ready = (
            sem(n) for n in ("h3_ready", "h3T_ps", "h3T_ready", "route_ps", "route_shift", "route_exp",
                             "onehot_ready", "pos_ps", "dest_ready"))
        total_ps, count_ready, scattered = (sem(n) for n in ("total_ps", "count_ready", "scattered"))
        moved = [sem(f"moved_{e}") for e in range(E2)]
        rows_in = [sem(f"rows_in_{e}") for e in range(E2)]
        rowsT_ps, rowsT_hi, rowsT_lo, eup_ps, ehid_ready, edown_ps, eout_ready, back_i_ready = (
            sem(n) for n in ("rowsT_ps", "rowsT_hi", "rowsT_lo", "eup_ps", "ehid_ready", "edown_ps", "eout_ready",
                             "back_i_ready"))
        chosen_written = [sem(f"chosen_written_{i}") for i in range(2)]
        back_in = L("back_in")
        comb_ready, stored = sem("comb_ready"), sem("stored")

        LAG = BT + 3
        STEPS = (NBLK + 3) * BT
        STEPS_MIX = NBLK * E1 + LAG - 1

        def live(blk):
            return 0 <= blk < NBLK

        def mix_bank(e):
            return B_KV if e == NBLK * E1 - 1 else B_DN

        def cols(ap, blk, pad):
            o = pad + (blk % BPB) * W
            return ap[:, blk // BPB, o:o + W]

        def up_weights(k):
            return (wuh, wul) if k // E1 == 1 else (w1h, w1l)

        def tiles(ap, blk):
            return ap[:, blk * BT:(blk + 1) * BT]

        def xstage(e):
            return (xh if e % 2 == 0 else xm)[:]

        def gelus(act, e):
            for c in range(FC):
                u = e * FC + c
                act.wait_ge(eup_ps, u + 1)
                if e >= 2 and c == 0:
                    act.wait_ge(edown_ps, e - 1)
                if e < 2 and c == 0:
                    act.wait_ge(down_ps, NBLK * E1)
                nc.scalar.activation(hid[:, e % 2, c, :], ps[:, 2 + c, :], ACT.Gelu).then_inc(ehid_ready, 1)

        block = ctx.enter_context(nc.Block())

        @block.sync
        def _(sp):
            xv = x.rearrange("b (t p) d -> p (b t) d", p=P)
            ov = out.rearrange("b (t p) d -> p (b t) d", p=P)
            sp.dma_start(tiles(x_sb, 0), tiles(xv, 0)).then_inc(x_in[0], 16)
            sp.dma_start(s_sb[:], small).then_inc(small_in, 16)
            sp.dma_start(c_sb[:], const).then_inc(small_in, 16)
            sp.dma_start(cm_sb[:], cmask).then_inc(small_in, 16)
            sp.dma_start(wmod_sb[:], wmod).then_inc(mod_in, 16)
            sp.dma_start(proj_sb[:], proj).then_inc(proj_in, 16)
            sp.dma_start(wst[:], w1).then_inc(wst_in[0], 16)
            for b in range(1, NBLK):
                sp.dma_start(tiles(x_sb, b), tiles(xv, b)).then_inc(x_in[b], 16)
            sp.dma_start(w2_sb[:], w2).then_inc(w2_in, 16)
            sp.dma_start(b2_sb[:], b2).then_inc(w2_in, 16)
            sp.dma_start(wd_sb[:], w_down).then_inc(wd_in, 16)
            sp.wait_ge(zero_ready, 1)
            for e in range(E2):
                sp.dma_start(line2[e * LINE2:e * LINE2 + CAP, :].rearrange("(p r) d -> p (r d)", p=P),
                             zero[:, 0:BT * ROW]).then_inc(zeroed, 16)
            cz = chosen[0:2 * TOKENS, :].rearrange("(p r) d -> p (r d)", p=P)
            for i in range(BT):
                sp.dma_start(cz[:, i * 1024:(i + 1) * 1024], zero).then_inc(zeroed, 16)
            for half in range(2):
                sp.wait_ge(w_split, E1 * (half + 1))
                sp.dma_start(wst[:], w_up[:, half * E1:(half + 1) * E1, :]).then_inc(wst_in[1 + half], 16)
            def append(e):
                first = sp.value_load(count_i[0:1, e:e + 1], min_val=0, max_val=CAP)
                sp.dma_start(line1[bass.ds(first + e * LINE1, CAP), :],
                             line2[e * LINE2:e * LINE2 + CAP, :]).then_inc(moved[e], 16)

            sp.wait_ge(count_ready, 1)
            sp.wait_ge(scattered, 16 * 2 * TILES)
            append(0)
            append(1)
            for e in range(E2):
                sp.wait_ge(moved[e], 16)
                if e + 2 < E2:
                    append(e + 2)
                if e >= 2:
                    sp.wait_ge(rowsT_ps, e - 1)
                    sp.wait_ge(back_i_ready, e - 1)
                sp.dma_start(rows(e), line1[e * LINE1:e * LINE1 + CAP, :].rearrange("(t p) d -> p t d", p=P)) \
                    .then_inc(rows_in[e], 16)
            cv = chosen[0:2 * TOKENS, :].rearrange("(k t p) d -> p k t d", k=2, p=P)
            for half in chosen_written:
                sp.wait_ge(half, 16 * BT * E2 // 2)
            for b in range(NBLK):
                for k in range(2):
                    sp.dma_start(tiles(back[:, k], b), tiles(cv[:, k], b)).then_inc(back_in[b], 16)
            for b in range(NBLK):
                sp.wait_ge(comb_ready, b + 1)
                sp.dma_start(tiles(ov, b), tiles(x_sb, b)).then_inc(stored, 16)
            sp.wait_ge(stored, 16 * NBLK)

        @block.gpsimd
        def _(pool):
            g = nc.gpsimd
            n = [0]

            def step(ins):
                n[0] += 1
                ins.then_inc(pool_step, 1)
                return n[0]

            g.memset(zero, 0.0).then_inc(zero_ready, 1)
            a = step(g.memset(mhalf[:], -0.5))
            g.memset(gwp[:], 0.0)
            g.memset(before[:, 0, :], 0.0)
            for par in range(2):
                for j in range(BT):
                    last = g.memset(vx[:, par, j, DH * HEADS:NH9], 1.0)
            last.then_inc(v_ones, 1)
            pool.wait_ge(pool_step, a)

            def inv_std(i, blk):
                pool.wait_ge(var_ready[i], blk + 1)
                a = step(g.tensor_scalar(tiles(ve[i], blk), tiles(mv[i], blk)[:, :, 1], LN_EPS, None, ALU.add))
                pool.wait_ge(pool_step, a)
                g.tensor_tensor(tiles(rstd[i], blk), tiles(ve[i], blk), mhalf[:], ALU.pow) \
                    .then_inc(rstd_ready[i], 1)

            def split(k):
                hi, lo = (w[:, k % E1, :] for w in up_weights(k))
                pool.wait_ge(wst_in[k // E1], 16)
                if k == E1:
                    pool.wait_ge(zeroed, 16 * (E2 + BT))
                if k == 2 * E1:
                    pool.wait_ge(up_ps, NBLK * E1 * FC)
                a = step(g.tensor_copy(hi, wst[:, k % E1, :]))
                pool.wait_ge(pool_step, a)
                g.tensor_tensor(lo, wst[:, k % E1, :], hi.bitcast(F32), ALU.subtract).then_inc(w_split, 1)

            def difference(blk):
                pool.wait_ge(x1_ready, blk + 1)
                if blk >= 1:
                    pool.wait_ge(og_ps, blk)
                g.tensor_tensor(diff[:], cols(x1T, blk, 1), cols(x1T, blk, 0), ALU.subtract) \
                    .then_inc(diff_ready, 1)

            def rotate_sum(blk):
                pool.wait_ge(rot_parts, blk + 1)
                a = phi[:, blk % 2]
                g.tensor_tensor(a, a, rot_b[:], ALU.add).then_inc(rot_ready, 1)

            def outer(t):
                blk, j = t // BT, t % BT
                pool.wait_ge(phi_ready, blk + 1)
                if j == 0 and blk == 0:
                    pool.wait_ge(v_ones, 1)
                pool.wait_ge(qkv_ready, BT * blk + BT)
                if t >= 2:
                    pool.wait_ge(tail_ps, t - 1)
                k_ = phi[:, blk % 2, j, D:2 * D].rearrange("p (h d) -> p h d", h=HEADS)[:, None, :, :] \
                    .broadcast_to([P, M1, HEADS, DH])
                v_ = vx[:, blk % 2, j, :].rearrange("p (m h) -> p m h", m=M1)[:, :, :, None] \
                    .broadcast_to([P, M1, HEADS, DH])
                o_ = kv[:, t % 2, :].rearrange("p (m h d) -> p m h d", m=M1, h=HEADS)
                g.tensor_tensor(o_, k_, v_, ALU.mult).then_inc(kv_ready, 1)

            def scatter(k, t):
                g.indirect_dma_start(out=(line1, line2)[k],
                                     out_offset=bass.IndirectOffsetOnAxis(dest_i[:, t, k:k + 1], 0),
                                     in_=h3r[:, t, :], in_offset=None).then_inc(scattered, 16)

            inv_std(0, 0)
            rotate_sum(0)
            outer(0)
            for s in range(STEPS):
                b, f = divmod(s, BT)
                if f == 3 and live(b + 1):
                    rotate_sum(b + 1)
                if s + 1 < TILES:
                    outer(s + 1)
                if f == 0 and live(b + 1):
                    inv_std(0, b + 1)
                if f == 0 and live(b - 3):
                    inv_std(2, b - 3)
                if s < 2 * E1:
                    split(s)
                if f == 1 and live(b - 1):
                    inv_std(1, b - 1)
                if f == 3 and live(b):
                    difference(b)
                if f == 3 and live(b - 3):
                    pool.wait_ge(dest_ready, b - 2)
                    for j in range(BT):
                        for k in range(2):
                            scatter(k, BT * (b - 3) + j)
            for e in range(E1):
                split(2 * E1 + e)
            for e in range(E2):
                pool.wait_ge(eout_ready, e + 1)
                for j in range(BT):
                    g.indirect_dma_start(out=chosen, out_offset=bass.IndirectOffsetOnAxis(back_i[:, e, j:j + 1], 0),
                                         in_=xstage(e)[:, j, :], in_offset=None).then_inc(chosen_written[e % 2], 16)

        @block.scalar
        def _(act):
            a_ = nc.scalar
            n = [0]

            act.wait_ge(small_in, 48)
            a_.activation(scT[:], s_sb[:, S_C:S_C + 2], ACT.Silu).then_inc(sc_ready, 1)

            def hT_evac(blk):
                b = blk // BPB
                act.wait_ge(hT_ps, blk + 1)
                if blk == 0:
                    act.wait_ge(mod_ready, 1)
                    act.wait_ge(pads_ready, 1)
                a_.activation(cols(hT, blk, 2), ps[:, B_D, :], ACT.Identity, bias=modT[:, 0, b:b + 1],
                              scale=modT[:, 1, b:b + 1]).then_inc(hT_ready, 1)
                act.wait_ge(hT_ready, blk + 1)
                if blk >= 1:
                    act.wait_ge(pw_ps, blk)
                a_.activation(conv[:], cols(hT, blk, 0), ACT.Copy, scale=s_sb[:, S_DW:S_DW + 1]) \
                    .then_inc(conv0_ready, 1)

            def qkv_evac(t):
                blk, j = t // BT, t % BT
                act.wait_ge(qkv_ps, t + 1)
                if j == 0 and blk >= 1:
                    act.wait_ge(rot_parts, blk)
                if j == 0 and blk >= 2:
                    act.wait_ge(kv_ready, BT * (blk - 1))
                    act.wait_ge(tail_ps, BT * (blk - 1))
                a_.activation(qk[:, j, :], ps[:, B_Q, 0:2 * D], ACT.Copy)
                a_.activation(vx[:, blk % 2, j, 0:D].rearrange("p (m h) -> p m h", m=DH),
                              ps[:, B_Q, 2 * D:3 * D].rearrange("p (h m) -> p m h", m=DH), ACT.Copy) \
                    .then_inc(qkv_ready, 1)

            def phi_exp(blk):
                act.wait_ge(rot_ready, blk + 1)
                if blk >= 1:
                    act.wait_ge(phi_ready, blk)
                a_.activation(rot_b[:], phi[:, blk % 2], ACT.Exp)
                a_.activation(qk[:], phi[:, blk % 2], ACT.Relu).then_inc(exp_ready, 1)

            def qT_evac(t):
                act.wait_ge(qT_ps, t + 1)
                if t >= 2:
                    act.wait_ge(tail_ps, t - 1)
                a_.activation(qT[:, t % 2, :], ps[:, B_Q, 384:512], ACT.Copy).then_inc(qT_ready, 1)

            def attT_evac(t):
                blk, j = t // BT, t % BT
                act.wait_ge(attT_ps, t + 1)
                if j == 0 and blk >= 1:
                    act.wait_ge(x2_ps, blk)
                a_.activation(attT[:, j * P:(j + 1) * P], ps[:, B_Q, 384:512], ACT.Copy).then_inc(attT_ready, 1)

            def gate_evac(blk):
                act.wait_ge(og_ps, blk + 1)
                if blk >= 1:
                    act.wait_ge(x2T_ready, blk)
                a_.activation(gate[:], ps[:, B_Q, :], ACT.Tanh, bias=hbg[:, 0:1], scale=0.5) \
                    .then_inc(gate_ready, 1)

            def x2_evac(blk):
                act.wait_ge(x2_ps, blk + 1)
                a_.activation(tiles(x2, blk), ps[:, B_D, :].rearrange("p (t d) -> p t d", t=BT), ACT.Copy) \
                    .then_inc(x2_ready, 1)

            def h2T_evac(blk):
                act.wait_ge(h2T_ps, blk + 1)
                if blk >= 1:
                    act.wait_ge(h2_split, blk)
                    act.wait_ge(mix_ps, blk)
                a_.activation(h2T[:], ps[:, B_D, :], ACT.Identity, bias=s_sb[:, S_LB:S_LB + 1],
                              scale=s_sb[:, S_LG:S_LG + 1]).then_inc(h2T_ready, 1)

            def mix_exps(blk):
                act.wait_ge(mix_shift, blk + 1)
                a_.activation(sm[:], sm[:], ACT.Exp).then_inc(mix_exp, 1)

            def gwT_evac(blk):
                act.wait_ge(gwT_ps, blk + 1)
                if blk >= 1:
                    act.wait_ge(b2_ps, blk)
                a_.activation(gwT[:], ps[:, B_D, 0:P], ACT.Copy).then_inc(gwT_ready, 1)

            def silu(u):
                e = u // FC
                act.wait_ge(up_ps, u + 1)
                if e >= 2:
                    act.wait_ge(down_ps, e - 1)
                c = S_B1 + u % (E1 * FC)
                a_.activation(hid[:, e % 2, u % FC, :], ps[:, B_UP[u % 2], :], ACT.Silu,
                              bias=s_sb[:, c:c + 1]).then_inc(hid_ready, 1)

            def h3T_evac(blk):
                act.wait_ge(h3T_ps, blk + 1)
                if blk >= 1:
                    act.wait_ge(route_ps, blk)
                a_.activation(h3T[:], ps[:, B_D, :], ACT.Copy).then_inc(h3T_ready, 1)

            def route_exps(blk):
                act.wait_ge(route_shift, blk + 1)
                a_.activation(gt_[:], gt_[:], ACT.Exp).then_inc(route_exp, 1)

            hT_evac(0)
            for j in range(BT):
                qkv_evac(j)
            phi_exp(0)
            for s in range(STEPS):
                b, f = divmod(s, BT)
                e = s - LAG

                def silus(c0):
                    if 0 <= e < NBLK * E1:
                        for c in range(c0, c0 + 2):
                            silu(e * FC + c)

                def query(s):
                    if s < TILES:
                        qT_evac(s)

                def attended(s):
                    if 1 <= s <= TILES:
                        attT_evac(s - 1)

                if f == 0:
                    silus(0)
                    query(s)
                    if live(b - 2):
                        gwT_evac(b - 2)
                    attended(s)
                    if live(b - 1):
                        gate_evac(b - 1)
                    silus(2)
                if f == 1:
                    silus(0)
                    if live(b + 1):
                        hT_evac(b + 1)
                    query(s)
                    if live(b - 1):
                        x2_evac(b - 1)
                    silus(2)
                    if live(b - 3):
                        h3T_evac(b - 3)
                    attended(s)
                if f == 2:
                    query(s)
                    silus(0)
                    if live(b + 1):
                        qkv_evac(BT * (b + 1))
                        qkv_evac(BT * (b + 1) + 1)
                    if live(b - 1):
                        h2T_evac(b - 1)
                    silus(2)
                    if live(b + 1):
                        qkv_evac(BT * (b + 1) + 2)
                    attended(s)
                    if live(b + 1):
                        qkv_evac(BT * (b + 1) + 3)
                    if live(b - 3):
                        route_exps(b - 3)
                if f == 3:
                    query(s)
                    if live(b - 1):
                        mix_exps(b - 1)
                    silus(0)
                    silus(2)
                    attended(s)
                    if live(b + 1):
                        phi_exp(b + 1)

            for e in range(E2):
                act.wait_ge(rowsT_ps, e + 1)
                if e >= 2:
                    act.wait_ge(eup_ps, FC * (e - 1))
                a_.activation(h2h[:, e % 2, :], ps[:, e % 2, :], ACT.Copy).then_inc(rowsT_hi, 1)
                if e >= 1:
                    gelus(act, e - 1)
            gelus(act, E2 - 1)
        @block.vector
        def _(dve):
            v = nc.vector
            n = [0]

            def step(ins):
                n[0] += 1
                ins.then_inc(dve_step, 1)
                return n[0]

            def after(k=None):
                dve.wait_ge(dve_step, n[0] if k is None else k)

            v.memset(hT[:, :, 0:2], 0.0).then_inc(pads_ready, 1)

            statistics = []

            def stats(i, blk, src):
                if statistics:
                    dve.wait_ge(*statistics[-1])
                statistics.append((var_ready[i], blk + 1))
                for j in range(BT):
                    step(v.bn_stats(st[:, j, :], src[:, j, :]))
                after()
                for j in range(BT):
                    last = v.bn_aggr(tiles(mv[i], blk)[:, j, :], st[:, j, :])
                last.then_inc(var_ready[i], 1)

            def normalise(i, blk, src, dst, done):
                dve.wait_ge(rstd_ready[i], blk + 1)
                for j in range(BT):
                    t = BT * blk + j
                    last = v.tensor_scalar(dst[:, j, :], src[:, j, :], mv[i][:, t, 0:1], rstd[i][:, t:t + 1],
                                           ALU.subtract, ALU.mult)
                last.then_inc(done, 1)

            def modulation():
                dve.wait_ge(sc_ready, 1)
                v.tensor_copy(scb[:], scT[:, :, None].broadcast_to([P, 2, P])).then_inc(scb_ready, 1)
                v.tensor_scalar(hbg[:], s_sb[:, S_BG:S_BG + 1], 0.5, None, ALU.mult)
                dve.wait_ge(mod_ps, 1)
                v.tensor_copy(modT[:, 0, :], ps[:, B_D, 0:2])
                v.tensor_scalar(modT[:, 1, :], ps[:, B_D, 2:4], 1.0, None, ALU.add).then_inc(mod_ready, 1)

            def modulation_rows():
                dve.wait_ge(mod_ps, 2)
                for b in range(BATCH):
                    step(v.tensor_copy(modb[:, b].rearrange("p m d -> p (m d)"), ps[:, B_UP[b], :]))
                after()
                v.tensor_scalar(modb[:, :, 2, :], modb[:, :, 2, :], 1.0, None, ALU.add)
                for m in (0, 3):
                    s = modb[:, :, m, :]
                    t0, t1 = gtmp[:, 0], gtmp[:, 1]
                    step(v.tensor_scalar(t0, s, -1.0, None, ALU.mult))
                    after()
                    step(v.tensor_tensor(t1, t0, s, ALU.max))
                    after()
                    v.tensor_scalar(t1, t1, 0.25, None, ALU.max)
                    step(v.tensor_scalar(t0, s, 0.0, 2.0, ALU.is_ge, ALU.mult))
                    after()
                    step(v.tensor_scalar(t0, t0, -1.0, None, ALU.add))
                    after()
                    step(v.tensor_tensor(s, t0, t1, ALU.mult))
                    after()

            def ln1(blk):
                dve.wait_ge(x_in[blk], 16)
                stats(0, blk, tiles(x_sb, blk))

            def xhat(blk):
                if blk >= 1:
                    dve.wait_ge(hT_ps, blk)
                normalise(0, blk, tiles(x_sb, blk), xh, xh_ready)

            def conv_taps(blk):
                dve.wait_ge(conv0_ready, blk + 1)
                h = hT[:, blk // BPB, (blk % BPB) * W:(blk % BPB) * W + W + 2]
                step(v.scalar_tensor_tensor(conv[:], h[:, 1:1 + W], s_sb[:, S_DW + 1:S_DW + 2], conv[:],
                                            ALU.mult, ALU.add))
                after()
                v.scalar_tensor_tensor(conv[:], h[:, 2:2 + W], s_sb[:, S_DW + 2:S_DW + 3], conv[:],
                                       ALU.mult, ALU.add).then_inc(conv_ready, 1)

            def residual1(blk):
                dve.wait_ge(pw_ps, blk + 1)
                ins = v.tensor_tensor(cols(x1T, blk, 1), ps[:, B_D, :], cols(hT, blk, 2), ALU.add)
                if blk % BPB == 0:
                    step(ins)
                    after()
                    ins = v.tensor_copy(x1T[:, blk // BPB, 0:1], x1T[:, blk // BPB, 1:2])
                ins.then_inc(x1_ready, 1)

            def rotate(blk):
                dve.wait_ge(qkv_ready, BT * blk + BT)
                if blk >= 1:
                    dve.wait_ge(phi_ready, blk)
                if blk >= 2:
                    dve.wait_ge(tail_ps, BT * (blk - 1))
                    dve.wait_ge(kv_ready, BT * (blk - 1))
                i = blk % BPB * BT * DH
                cs, sn = (c_sb[:, c + i:c + i + BT * DH].rearrange("p (t e) -> p t e", t=BT)[:, :, None, :]
                          .broadcast_to([P, BT, 2 * HEADS, DH]) for c in (C_COS, C_SIN))
                q4 = qk[:].rearrange("p t (h e) -> p t h e", e=DH)
                v.tensor_tensor(phi[:, blk % 2].rearrange("p t (h e) -> p t h e", e=DH), q4, cs, ALU.mult)
                pair = lambda ap: ap.rearrange("p t h (f two) -> p t h f two", two=2)
                v.tensor_tensor(pair(rot_b[:].rearrange("p t (h e) -> p t h e", e=DH)), pair(q4)[:, :, :, :, ::-1],
                                pair(sn), ALU.mult).then_inc(rot_parts, 1)

            def feature(blk):
                dve.wait_ge(exp_ready, blk + 1)
                v.scalar_tensor_tensor(phi[:, blk % 2], rot_b[:], 1.0, qk[:], ALU.min, ALU.add).then_inc(phi_ready, 1)

            def attend(t):
                j, first, lastt = t % BT, t % TPB == 0, t % TPB == TPB - 1
                q_ = phi[:, t // BT % 2, j, 0:D]
                dve.wait_ge(cum_ps, t + 1)
                if t >= 1:
                    dve.wait_ge(att_ready, t)
                v.tensor_tensor(qp[:, 0:DH * D].rearrange("p (m c) -> p m c", m=DH),
                                ps[:, B_KV:B_KV + 2, :].rearrange("p b (m c) -> p (b m) c", m=4),
                                q_[:, None, :].broadcast_to([P, DH, D]), ALU.mult).then_inc(cum_read, 1)
                dve.wait_ge(tail_ps, t + 1)
                a = step(v.tensor_tensor(qp[:, DH * D:CH], ps[:, B_M, 0:D], q_, ALU.mult))
                if not lastt:
                    v.tensor_tensor(state[:], ps[:, B_M, 2 * D + 16:2 * D + 16 + NH9], headmask, ALU.mult) \
                        .then_inc(state_ready, 1) if first else state_add(t)
                else:
                    v.tensor_copy(state[0:1, 0:1], state[0:1, 0:1]).then_inc(state_ready, 1)
                dve.wait_ge(cum_read, t + 1)
                after(a)
                a = step(v.tensor_reduce(nd[:, 0, :], qp[:].rearrange("p (c d) -> p c d", d=DH), AX.X, ALU.add))
                after(a)
                if first:
                    r, ins = 0, v.tensor_copy(rden[:, 1, 0:1], nd[:, 0, 0:1])
                else:
                    r, ins = 1, v.tensor_tensor(nd[:, 1, :], ps[:, B_M, D:D + NH9], nd[:, 0, :], ALU.add)
                ins.then_inc(tail_read, 1)
                dve.wait_ge(tail_read, t + 1)
                a = step(v.tensor_scalar(rden[:, 0, :], nd[:, r, DH * HEADS:NH9], DEN_EPS, None, ALU.add))
                after(a)
                a = step(v.reciprocal(rden[:, 1, :], rden[:, 0, :]))
                after(a)
                if t >= 2:
                    dve.wait_ge(attT_ps, t - 1)
                v.tensor_tensor(att[:, t % 2, :].rearrange("p (h m) -> p m h", m=DH),
                                nd[:, r, 0:D].rearrange("p (m h) -> p m h", m=DH),
                                rden[:, 1, None, :].broadcast_to([P, DH, HEADS]), ALU.mult).then_inc(att_ready, 1)

            def state_add(t):
                a = step(v.tensor_tensor(gtmp[:, 0, 0:2].rearrange("p a d -> p (a d)")[:, 0:NH9],
                                         ps[:, B_M, 2 * D + 16:2 * D + 16 + NH9], headmask, ALU.mult))
                after(a)
                v.tensor_tensor(state[:], gtmp[:, 0, 0:2].rearrange("p a d -> p (a d)")[:, 0:NH9], state[:],
                                ALU.add).then_inc(state_ready, 1)

            def residual2(blk):
                dve.wait_ge(gate_ready, blk + 1)
                if blk >= 1:
                    dve.wait_ge(x2_ps, blk)
                step(v.scalar_tensor_tensor(x2T[:], gate[:], 1.0, ps[:, B_D, :], ALU.add, ALU.mult))
                after()
                v.scalar_tensor_tensor(x2T[:], x2T[:], 0.5, cols(x1T, blk, 1), ALU.mult, ALU.add) \
                    .then_inc(x2T_ready, 1)

            def ln2(blk):
                dve.wait_ge(x2_ready, blk + 1)
                stats(1, blk, tiles(x2, blk))

            def xhat2(blk):
                if blk >= 1:
                    dve.wait_ge(h2T_ps, blk)
                normalise(1, blk, tiles(x2, blk), xm, xm_ready)

            def split2(blk):
                dve.wait_ge(h2T_ready, blk + 1)
                if blk >= 2:
                    dve.wait_ge(up_ps, (blk - 1) * E1 * FC)
                i = blk % 2
                step(v.tensor_copy(h2h[:, i, :], h2T[:]))
                after()
                v.tensor_tensor(h2l[:, i, :], h2T[:], h2h[:, i, :].bitcast(F32), ALU.subtract).then_inc(h2_split, 1)

            def mix_a(blk):
                dve.wait_ge(mix_ps, blk + 1)
                lp = ps[:, B_D, 0:BT * E1].rearrange("p (t e) -> p t e", t=BT)
                step(v.tensor_reduce(sm_r[:, 0, :], lp, AX.X, ALU.max))
                after()
                v.tensor_tensor(sm[:], lp, sm_r[:, 0, :, None].broadcast_to([P, BT, E1]), ALU.subtract) \
                    .then_inc(mix_shift, 1)

            def mix_b(blk):
                dve.wait_ge(mix_exp, blk + 1)
                step(v.tensor_reduce(sm_r[:, 0, :], sm[:], AX.X, ALU.add))
                after()
                step(v.reciprocal(sm_r[:, 1, :], sm_r[:, 0, :]))
                after()
                if blk == 0:
                    dve.wait_ge(v_ones, 1)
                v.tensor_tensor(gwp[:, blk % 2, 0:BT * E1].rearrange("p (t e) -> p t e", t=BT), sm[:],
                                sm_r[:, 1, :, None].broadcast_to([P, BT, E1]), ALU.mult).then_inc(mix_ready, 1)

            def acc_start(blk):
                dve.wait_ge(b2_ps, blk + 1)
                v.tensor_tensor(acc[:], ps[:, B_Q, :].rearrange("p (t d) -> p t d", t=BT), tiles(x2, blk),
                                ALU.add).then_inc(acc_ready, 1)
                dve.wait_ge(acc_ready, blk + 1)

            def add_expert(e):
                dve.wait_ge(down_ps, e + 1)
                for j in range(BT):
                    c = j * E1 + e % E1
                    last = v.scalar_tensor_tensor(acc[:, j, :], ps[:, mix_bank(e), j * D:(j + 1) * D], gwp[:, e // E1 % 2, c:c + 1],
                                                  acc[:, j, :], ALU.mult, ALU.add)
                last.then_inc(down_added, 1)
                dve.wait_ge(down_added, e + 1)

            def residual3(blk):
                b = blk // BPB
                step(v.tensor_tensor(acc[:], acc[:], modb[:, b, 0, None, :].broadcast_to([P, BT, D]), ALU.mult))
                after()
                step(v.tensor_tensor(tiles(x_sb, blk), acc[:], tiles(x_sb, blk), ALU.add))
                after()

            def norm3(blk):
                b = blk // BPB
                dve.wait_ge(rstd_ready[2], blk + 1)
                for j in range(BT):
                    t = BT * blk + j
                    step(v.scalar_tensor_tensor(h3[:, t, :], x_sb[:, t, :], mv[2][:, t, 0:1], modb[:, b, 2, :],
                                                ALU.subtract, ALU.mult))
                after()
                for j in range(BT):
                    t = BT * blk + j
                    last = v.scalar_tensor_tensor(h3[:, t, :], h3[:, t, :], rstd[2][:, t:t + 1], modb[:, b, 1, :],
                                                  ALU.mult, ALU.add)
                last.then_inc(h3_ready, 1)

            def bc(ap):
                return ap[:, :, None].broadcast_to([P, BT, E2])

            def route_a(blk):
                dve.wait_ge(route_ps, blk + 1)
                step(v.tensor_copy(lg[:], ps[:, B_D, 0:BT * E2].rearrange("p (t e) -> p t e", t=BT)))
                after()
                step(v.tensor_reduce(rs[:, 0, :], lg[:], AX.X, ALU.max))
                after()
                v.tensor_tensor(gt_[:], lg[:], bc(rs[:, 0, :]), ALU.subtract).then_inc(route_shift, 1)

            def first_of_max(src, mx, rank, onehot):
                rev = c_sb[:, None, C_REV:C_REV + E2].broadcast_to([P, BT, E2])
                step(v.tensor_reduce(mx, src, AX.X, ALU.max))
                after()
                step(v.tensor_tensor(rt[:, 0], src, bc(mx), ALU.is_equal))
                after()
                step(v.tensor_tensor(rt[:, 1], rt[:, 0], rev, ALU.mult))
                after()
                step(v.tensor_reduce(rank, rt[:, 1], AX.X, ALU.max))
                after()
                step(v.tensor_tensor(onehot, rt[:, 1], bc(rank), ALU.is_equal))
                after()

            def route_b(blk):
                dve.wait_ge(route_exp, blk + 1)
                o = tiles(oh, blk)
                step(v.tensor_reduce(rs[:, 1, :], gt_[:], AX.X, ALU.add))
                after()
                step(v.reciprocal(rs[:, 2, :], rs[:, 1, :]))
                after()
                step(v.tensor_tensor(gt_[:], gt_[:], bc(rs[:, 2, :]), ALU.mult))
                after()
                first_of_max(gt_[:], rs[:, 3, :], rs[:, 4, :], o[:, :, 0:E2])
                step(v.scalar_tensor_tensor(lg[:], o[:, :, 0:E2], -BIG, lg[:], ALU.mult, ALU.add))
                after()
                first_of_max(lg[:], rs[:, 5, :], rs[:, 6, :], o[:, :, E2:2 * E2])
                step(v.tensor_copy(tiles(ohb, blk), o))
                after()
                if blk == 0:
                    dve.wait_ge(v_ones, 1)
                for j in range(BT):
                    t = BT * blk + j
                    ins = v.tensor_tensor(before[:, t + 1, :], before[:, t, :], ohb[:, t, :], ALU.add)
                    if j == BT - 1:
                        ins.then_inc(onehot_ready, 1)
                    else:
                        step(ins)
                        after()
                step(v.tensor_tensor(rt[:, 2], gt_[:], o[:, :, E2:2 * E2], ALU.mult))
                after()
                step(v.tensor_reduce(rs[:, 7, :], rt[:, 2], AX.X, ALU.add))
                after()
                step(v.tensor_tensor(rs[:, 8, :], rs[:, 3, :], rs[:, 7, :], ALU.add))
                after()
                step(v.tensor_scalar(rs[:, 8, :], rs[:, 8, :], 1e-9, None, ALU.max))
                after()
                step(v.reciprocal(rs[:, 9, :], rs[:, 8, :]))
                after()
                tail = tiles(h3r, blk)
                v.tensor_copy(tail[:, :, D], tiles(c_sb[:, C_TOK:C_TOK + TILES], blk))
                v.tensor_tensor(tail[:, :, D + 1], rs[:, 3, :], rs[:, 9, :], ALU.mult)
                step(v.tensor_tensor(rs[:, 8, :], rs[:, 7, :], rs[:, 3, :], ALU.subtract))
                for k, rsrc, length in ((0, 4, LINE1), (1, 6, LINE2)):
                    v.tensor_scalar(tiles(exps, blk)[:, :, k], rs[:, rsrc, :], -float(length), float(E2 * length),
                                    ALU.mult, ALU.add)
                after()
                step(v.tensor_tensor(tail[:, :, D + 2], rs[:, 8, :], rs[:, 9, :], ALU.mult))
                after()

            def route_c(blk):
                dve.wait_ge(pos_ps, blk + 1)
                o = tiles(oh, blk)
                pp = ps[:, B_D, 0:BT * 2 * E2].rearrange("p (t e) -> p t e", t=BT)
                for k in range(2):
                    step(v.tensor_tensor(rt[:, k], pp[:, :, k * E2:(k + 1) * E2], o[:, :, k * E2:(k + 1) * E2],
                                         ALU.mult))
                after()
                for k in range(2):
                    step(v.tensor_reduce(tiles(loc, blk)[:, :, k], rt[:, k], AX.X, ALU.add))
                after()
                step(v.tensor_tensor(tiles(dest, blk), tiles(loc, blk), tiles(exps, blk), ALU.add))
                after()
                v.tensor_copy(tiles(dest_i, blk), tiles(dest, blk)).then_inc(dest_ready, 1)

            def counts():
                dve.wait_ge(total_ps, 1)
                step(v.tensor_scalar(count[:], ps[:, B_D, 0:E2], float(CAP), None, ALU.min))
                after()
                v.tensor_copy(count_i[:], count[:]).then_inc(count_ready, 1)
                slot = c_sb[:, None, C_SLOT:C_SLOT + BT].broadcast_to([P, E2, BT])
                step(v.tensor_tensor(second[:], slot, count[:, :, None].broadcast_to([P, E2, BT]), ALU.is_ge))
                after()
                step(v.scalar_tensor_tensor(trash[:], second[:], -float(TOKENS),
                                            c_sb[:, C_TRASH:].rearrange("p (e t) -> p e t", e=E2), ALU.mult, ALU.add))
                after()

            def row_addresses(e):
                dve.wait_ge(rows_in[e], 16)
                number, w_first, w_diff = (rows(e)[:, :, D + i] for i in range(3))
                step(v.scalar_tensor_tensor(addr[:, 0, :], second[:, e, :], float(TOKENS), number, ALU.mult, ALU.add))
                step(v.scalar_tensor_tensor(addr[:, 1, :], number, 0.0, trash[:, e, :], ALU.is_equal, ALU.mult))
                step(v.tensor_tensor(addr[:, 2, :], second[:, e, :], w_diff, ALU.mult))
                after()
                step(v.scalar_tensor_tensor(addr[:, 3, :], addr[:, 0, :], -1.0, addr[:, 1, :], ALU.add, ALU.add))
                step(v.tensor_tensor(row_w[:, e, :], addr[:, 2, :], w_first, ALU.add))
                after()
                v.tensor_copy(back_i[:, e, :], addr[:, 3, :]).then_inc(back_i_ready, 1)
                dve.wait_ge(back_i_ready, e + 1)

            ln1(0)
            dve.wait_ge(small_in, 48)
            modulation()
            xhat(0)
            conv_taps(0)
            modulation_rows()
            residual1(0)
            rotate(0)
            feature(0)
            for s in range(STEPS):
                b, f = divmod(s, BT)
                if f == 1 and live(b - 2):
                    acc_start(b - 2)
                if f == 3 and live(b - 1):
                    mix_a(b - 1)
                if 0 <= s - LAG - 2 < NBLK * E1 - 1:
                    add_expert(s - LAG - 2)
                if s == STEPS_MIX + 1:
                    add_expert(s - LAG - 1)
                    residual3(NBLK - 1)
                    stats(2, NBLK - 1, tiles(x_sb, NBLK - 1))
                if f == 0:
                    if live(b - 3) and b - 3 < NBLK - 1:
                        residual3(b - 3)
                        stats(2, b - 3, tiles(x_sb, b - 3))
                    if live(b + 1):
                        ln1(b + 1)
                if f == 1:
                    if live(b - 3):
                        norm3(b - 3)
                    if live(b + 1):
                        conv_taps(b + 1)
                if f == 2:
                    if live(b - 3):
                        route_a(b - 3)
                    if live(b - 1):
                        xhat2(b - 1)
                if f == 3 and live(b + 1):
                    rotate(b + 1)
                if s < TILES:
                    attend(s)
                if f == 0:
                    if live(b - 1):
                        residual2(b - 1)
                    if live(b + 1):
                        xhat(b + 1)
                if f == 1:
                    if live(b + 1):
                        residual1(b + 1)
                    if live(b - 1):
                        ln2(b - 1)
                if f == 2:
                    if live(b - 1):
                        split2(b - 1)
                    if live(b - 3):
                        route_b(b - 3)
                if f == 3:
                    if live(b + 1):
                        feature(b + 1)
                    if live(b - 1):
                        mix_b(b - 1)
                    if live(b - 3):
                        route_c(b - 3)
            counts()

            def low_part(e):
                dve.wait_ge(rowsT_hi, e + 1)
                if e >= 2:
                    dve.wait_ge(eup_ps, FC * (e - 1))
                v.tensor_tensor(h2l[:, e % 2, :], ps[:, e % 2, :], h2h[:, e % 2, :].bitcast(F32), ALU.subtract) \
                    .then_inc(rowsT_lo, 1)

            for e in range(2):
                row_addresses(e)
                low_part(e)
            for e in range(E2):
                if e + 2 < E2:
                    row_addresses(e + 2)
                    low_part(e + 2)
                dve.wait_ge(edown_ps, e + 1)
                if e >= 2:
                    dve.wait_ge(chosen_written[e % 2], 16 * BT * (e // 2))
                for j in range(BT):
                    last = v.tensor_scalar(xstage(e)[:, j, :], ps[:, 6 + e % 2, j * D:(j + 1) * D],
                                           row_w[:, e, j:j + 1], None, ALU.mult)
                last.then_inc(eout_ready, 1)
            for blk in range(NBLK):
                dve.wait_ge(back_in[blk], 32)
                a, b_ = tiles(back[:, 0], blk), tiles(back[:, 1], blk)
                step(v.tensor_tensor(a, a, b_, ALU.add))
                after()
                step(v.tensor_tensor(a, a, modb[:, blk // BPB, 3, None, :].broadcast_to([P, BT, D]), ALU.mult))
                after()
                v.tensor_tensor(tiles(x_sb, blk), tiles(x_sb, blk), a, ALU.add).then_inc(comb_ready, 1)

        @block.tensor
        def _(pe):
            m = nc.tensor
            freed = {}

            def claim(bank, reader, count):
                if bank in freed:
                    pe.wait_ge(*freed[bank])
                freed[bank] = (reader, count)

            def mm(o, l, r, start=True, stop=True):
                return m.matmul(o, l, r, start=start, stop=stop)

            def modulation():
                pe.wait_ge(mod_in, 16)
                pe.wait_ge(sc_ready, 1)
                claim(B_D, mod_ready, 1)
                for i in range(2):
                    last = mm(ps[:, B_D, 2 * i:2 * i + 2], wmod_sb[:, i * D:(i + 1) * D], scT[:])
                last.then_inc(mod_ps, 1)

            def modulation_rows():
                pe.wait_ge(scb_ready, 1)
                for b in range(BATCH):
                    last = mm(ps[:, B_UP[b], :], scb[:, b, :], wmod_sb[:, 2 * D:6 * D])
                last.then_inc(mod_ps, 1)
                freed[B_UP[0]] = freed[B_UP[1]] = (x1_ready, 1)

            def transposes(bank, src, src_ready, count, done, reader):
                pe.wait_ge(src_ready, count)
                claim(bank, reader, count)
                for j in range(BT):
                    last = m.transpose(ps[:, bank, j * P:(j + 1) * P], src[:, j], ident)
                last.then_inc(done, 1)

            def pointwise(blk):
                pe.wait_ge(conv_ready, blk + 1)
                if blk == 0:
                    pe.wait_ge(proj_in, 16)
                claim(B_D, x1_ready, blk + 1)
                mm(ps[:, B_D, :], proj_sb[:, 0:P], conv[:]).then_inc(pw_ps, 1)

            def qkv(t):
                blk = t // BT
                pe.wait_ge(x1_ready, blk + 1)
                claim(B_Q, qkv_ready, t + 1)
                o = 1 + (t % TPB) * P
                mm(ps[:, B_Q, 0:3 * D], x1T[:, blk // BPB, o:o + P], proj_sb[:, P:4 * P]).then_inc(qkv_ps, 1)

            def q_transpose(t):
                pe.wait_ge(phi_ready, t // BT + 1)
                claim(B_Q, qT_ready, t + 1)
                m.transpose(ps[:, B_Q, 384:512], phi[:, t // BT % 2, t % BT, 0:D], ident).then_inc(qT_ps, 1)

            def prefix(t):
                blk, j = t // BT, t % BT
                kv_ = kv[:, t % 2, :]
                pe.wait_ge(kv_ready, t + 1)
                claim(B_KV, cum_read, t + 1)
                mm(ps[:, B_KV, :], tri, kv_[:, 0:512])
                mm(ps[:, B_KV + 1, :], tri, kv_[:, 512:1024]).then_inc(cum_ps, 1)
                claim(B_M, tail_read, t + 1)
                if t % TPB != TPB - 1:
                    mm(ps[:, B_M, 2 * D + 16:2 * D + 16 + NH9], phi[:, blk % 2, j, D:2 * D], vx[:, blk % 2, j, :])
                if t % TPB != 0:
                    pe.wait_ge(qT_ready, t + 1)
                    pe.wait_ge(state_ready, t)
                    mm(ps[:, B_M, D:D + NH9], qT[:, t % 2, :], state[:])
                mm(ps[:, B_M, 0:D], tri, kv_[:, 1024:CH]).then_inc(tail_ps, 1)

            def att_transpose(t):
                pe.wait_ge(att_ready, t + 1)
                claim(B_Q, attT_ready, t + 1)
                m.transpose(ps[:, B_Q, 384:512], att[:, t % 2, :], ident).then_inc(attT_ps, 1)

            def out_and_gate(blk):
                pe.wait_ge(attT_ready, BT * (blk + 1))
                pe.wait_ge(diff_ready, blk + 1)
                claim(B_D, x2T_ready, blk + 1)
                mm(ps[:, B_D, :], proj_sb[:, 4 * P:5 * P], attT[:])
                claim(B_Q, gate_ready, blk + 1)
                mm(ps[:, B_Q, :], proj_sb[:, 5 * P:6 * P], diff[:]).then_inc(og_ps, 1)

            def x2_transposes(blk):
                pe.wait_ge(x2T_ready, blk + 1)
                claim(B_D, x2_ready, blk + 1)
                for j in range(BT):
                    last = m.transpose(ps[:, B_D, j * P:(j + 1) * P], x2T[:, j * P:(j + 1) * P], ident)
                last.then_inc(x2_ps, 1)

            def mix_logits(blk):
                pe.wait_ge(h2T_ready, blk + 1)
                claim(B_D, mix_shift, blk + 1)
                for j in range(BT):
                    last = mm(ps[:, B_D, j * E1:(j + 1) * E1], h2T[:, j * P:(j + 1) * P], s_sb[:, S_MG:S_MG + E1])
                last.then_inc(mix_ps, 1)

            def mix_weights_transpose(blk):
                pe.wait_ge(mix_ready, blk + 1)
                claim(B_D, gwT_ready, blk + 1)
                m.transpose(ps[:, B_D, 0:P], gwp[:, blk % 2, :], ident).then_inc(gwT_ps, 1)

            def mix_bias(blk):
                pe.wait_ge(gwT_ready, blk + 1)
                if blk == 0:
                    pe.wait_ge(w2_in, 32)
                claim(B_Q, acc_ready, blk + 1)
                for j in range(BT):
                    last = mm(ps[:, B_Q, j * D:(j + 1) * D], gwT[:], b2_sb[:, j, :])
                last.then_inc(b2_ps, 1)

            def three_pass(o, wh, wl, ah, al):
                mm(o, wh, ah, stop=False)
                mm(o, wh, al, start=False, stop=False)
                return mm(o, wl, ah, start=False)

            def up(u):
                e = u // FC
                blk, c = e // E1, u % FC
                pe.wait_ge(h2_split, blk + 1)
                if blk == 0:
                    pe.wait_ge(w_split, e + 1)
                claim(B_UP[u % 2], hid_ready, u + 1)
                w_ = slice(c * P, (c + 1) * P)
                three_pass(ps[:, B_UP[u % 2], :], w1h[:, e % E1, w_], w1l[:, e % E1, w_], h2h[:, blk % 2, :],
                           h2l[:, blk % 2, :]).then_inc(up_ps, 1)

            def down(bank, w_, h, done, ready, count):
                for j in range(BT):
                    for c in range(FC):
                        if j == 0:
                            pe.wait_ge(ready, count + c + 1)
                        last = mm(ps[:, bank, j * D:(j + 1) * D], h[:, c, j * P:(j + 1) * P], w_[:, c, :],
                                  start=(c == 0), stop=(c == FC - 1))
                last.then_inc(done, 1)

            def route_logits(blk):
                pe.wait_ge(h3T_ready, blk + 1)
                claim(B_D, route_shift, blk + 1)
                for j in range(BT):
                    last = mm(ps[:, B_D, j * E2:(j + 1) * E2], h3T[:, j * P:(j + 1) * P], s_sb[:, S_WG:S_WG + E2])
                last.then_inc(route_ps, 1)

            def positions(blk):
                pe.wait_ge(onehot_ready, blk + 1)
                claim(B_D, dest_ready, blk + 1)
                for j in range(BT):
                    t = BT * blk + j
                    o = ps[:, B_D, j * 2 * E2:(j + 1) * 2 * E2]
                    mm(o, strict, ohb[:, t, :], stop=False)
                    last = mm(o, ones, before[:, t, :], start=False)
                last.then_inc(pos_ps, 1)

            pe.wait_ge(small_in, 48)
            modulation()
            transposes(B_D, xh, xh_ready, 1, hT_ps, hT_ready)
            modulation_rows()
            pointwise(0)
            for j in range(BT):
                qkv(j)
            for s in range(STEPS):
                b, f = divmod(s, BT)
                e = s - LAG

                def ups(c0):
                    if 0 <= e < NBLK * E1:
                        for c in range(c0, c0 + 2):
                            up(e * FC + c)

                def downs(ahead=0):
                    k = e - 1 + ahead
                    if 0 <= k < NBLK * E1:
                        bank = mix_bank(k)
                        claim(bank, down_added, k + 1)
                        down(bank, w2_sb[:, k % E1], hid[:, k % 2], down_ps, hid_ready, k * FC)

                def attention(order):
                    for part in order:
                        if part == "q" and s < TILES:
                            q_transpose(s)
                        if part == "a" and 1 <= s <= TILES:
                            att_transpose(s - 1)
                        if part == "p" and s < TILES:
                            prefix(s)

                if f == 0:
                    ups(0)
                    attention("q")
                    if live(b - 2):
                        mix_weights_transpose(b - 2)
                    downs()
                    attention("pa")
                    if live(b - 1):
                        out_and_gate(b - 1)
                    ups(2)
                    if live(b - 2):
                        mix_bias(b - 2)
                if f == 1:
                    ups(0)
                    if live(b + 1):
                        transposes(B_D, xh, xh_ready, b + 2, hT_ps, hT_ready)
                    attention("qp")
                    if live(b - 1):
                        x2_transposes(b - 1)
                    ups(2)
                    if live(b - 3):
                        transposes(B_D, tiles(h3, b - 3), h3_ready, b - 2, h3T_ps, h3T_ready)
                    downs()
                    attention("a")
                    if live(b + 1):
                        pointwise(b + 1)
                if f == 2:
                    attention("q")
                    if live(b - 3):
                        route_logits(b - 3)
                    ups(0)
                    if live(b + 1):
                        qkv(BT * (b + 1))
                    attention("p")
                    if live(b + 1):
                        qkv(BT * (b + 1) + 1)
                    if live(b - 1):
                        transposes(B_D, xm, xm_ready, b, h2T_ps, h2T_ready)
                    ups(2)
                    if live(b + 1):
                        qkv(BT * (b + 1) + 2)
                    downs()
                    if s == STEPS_MIX:
                        downs(1)
                    attention("a")
                    if live(b + 1):
                        qkv(BT * (b + 1) + 3)
                if f == 3:
                    attention("q")
                    if live(b - 1):
                        mix_logits(b - 1)
                    ups(0)
                    attention("p")
                    ups(2)
                    if s < STEPS_MIX:
                        downs()
                    if live(b - 3):
                        positions(b - 3)
                    attention("a")
            claim(B_D, count_ready, 1)
            mm(ps[:, B_D, 0:2 * E2], ones, before[:, TILES, :]).then_inc(total_ps, 1)

            def rows_transpose(e):
                pe.wait_ge(rows_in[e], 16)
                claim(e % 2, rowsT_lo, e + 1)
                for j in range(BT):
                    last = m.transpose(ps[:, e % 2, j * P:(j + 1) * P], rows(e)[:, j, 0:D], ident)
                last.then_inc(rowsT_ps, 1)

            def expert_up(e):
                pe.wait_ge(rowsT_lo, e + 1)
                pe.wait_ge(w_split, E1 + e + 1)
                wh, wl = up_weights(E1 + e)
                for c in range(FC):
                    u = e * FC + c
                    claim(2 + c, ehid_ready, u + 1)
                    w_ = slice(c * P, (c + 1) * P)
                    three_pass(ps[:, 2 + c, :], wh[:, e % E1, w_], wl[:, e % E1, w_], h2h[:, e % 2, :],
                               h2l[:, e % 2, :]).then_inc(eup_ps, 1)

            rows_transpose(0)
            rows_transpose(1)
            expert_up(0)
            pe.wait_ge(wd_in, 16)
            for e in range(E2):
                if e + 2 < E2:
                    rows_transpose(e + 2)
                if e + 1 < E2:
                    expert_up(e + 1)
                claim(6 + e % 2, eout_ready, e + 1)
                down(6 + e % 2, wd_sb[:, e], hid[:, e % 2], edown_ps, ehid_ready, e * FC)


def kernel(**inputs):
    import ml_dtypes
    import numpy as np
    import concourse.bacc as bacc
    from concourse.bass_utils import run_bass_kernel_spmd

    a = {k: np.asarray(v) for k, v in inputs.items()}
    f = np.float32
    col = lambda v: v.reshape(-1, P).T
    small = np.concatenate([
        a["L0_attn_w_dw"], col(a["L0_attn_b_gate"]), col(a["L0_attn_ln_g"]), col(a["L0_attn_ln_b"]),
        a["L0_attn_w_moe_gate"].T, col(a["L0_attn_b1"]), a["L0_ffn_wg"], a["L0_c"].T], axis=1)
    proj = np.concatenate([a["L0_attn_w_pw"].T, a["L0_attn_w_qkv"].T, a["L0_attn_w_o"].T, a["L0_attn_w_gate"].T],
                          axis=1)
    w1 = a["L0_attn_w1"].transpose(2, 0, 1)
    w2 = a["L0_attn_w2"].reshape(E1, D, FC, P).transpose(3, 0, 2, 1)
    b2 = np.zeros((P, BT, D), f)
    for j in range(BT):
        b2[j * E1:(j + 1) * E1, j, :] = a["L0_attn_b2"]
    w_up = a["L0_ffn_w_gate"].transpose(1, 0, 2)
    w_down = a["L0_ffn_w_down"].reshape(E2, FC, P, D).transpose(2, 0, 1, 3)

    const = np.zeros((P, N_CONST), f)
    i = np.arange(P)
    const[:, C_ID:C_ID + P] = i[:, None] == i
    const[:, C_TRI:C_TRI + P] = i[:, None] <= i
    const[:, C_BD:C_BD + NH9] = (i // DH)[:, None] == np.arange(NH9) % HEADS
    inv = (f(1) / f(10000) ** (np.arange(0, DH, 2, dtype=f) / f(DH))).astype(f)
    theta = (np.arange(SEQ, dtype=f)[:, None] * inv).astype(f)
    cos = np.repeat(np.cos(theta), 2, axis=1).reshape(TPB, P, DH).transpose(1, 0, 2)
    sin = (np.repeat(np.sin(theta), 2, axis=1) * np.tile([-1, 1], DH // 2)).reshape(TPB, P, DH).transpose(1, 0, 2)
    const[:, C_COS:C_COS + TPB * DH] = cos.reshape(P, -1)
    const[:, C_SIN:C_SIN + TPB * DH] = sin.reshape(P, -1)
    const[:, C_REV:C_REV + E2] = E2 - np.arange(E2)
    const[:, C_TOK:C_TOK + TILES] = np.arange(TILES) * P + i[:, None] + 1
    const[:, C_SLOT:C_SLOT + BT] = np.arange(BT) * P + i[:, None]
    const[:, C_TRASH:] = 2 * TOKENS + 1 + np.arange(E2 * BT) * P + i[:, None]
    cmask = np.stack([i[:, None] < i, np.ones((P, P), bool)], axis=1).astype(ml_dtypes.bfloat16)

    arrays = {"x": a["L0_attn_x"], "small": small, "proj": proj, "wmod": a["L0_wmod"], "w1": w1, "w2": w2,
              "b2": b2, "w_up": w_up, "w_down": w_down, "const": const, "cmask": cmask}
    arrays = {f"in_{k}": np.ascontiguousarray(v) for k, v in arrays.items()}
    nc = bacc.Bacc("TRN2", target_bir_lowering=False, num_devices=1)
    args = [nc.dram_tensor(k, v.shape, mybir.dt.from_np(v.dtype), kind="ExternalInput").ap()
            for k, v in arrays.items()]
    args.append(nc.dram_tensor("out", (BATCH, SEQ, D), F32, kind="ExternalOutput").ap())
    block_kernel(nc, *args)
    r = run_bass_kernel_spmd(nc, [arrays], core_ids=[0])
    return r.results[0]["out"]
```

```python
from contextlib import ExitStack

import concourse.bass as bass
from concourse import mybir

F32 = mybir.dt.float32
F32R = mybir.dt.float32r
BF16 = mybir.dt.bfloat16
U32 = mybir.dt.uint32
ALU = mybir.AluOpType
ACT = mybir.ActivationFunctionType
AX = mybir.AxisListType

P = 128
BATCH, SEQ, D = 2, 1024, 128
TOKENS = BATCH * SEQ
TILES = TOKENS // P
BT = 4
NBLK = TILES // BT
W = BT * P
TPB = SEQ // P
BPB = SEQ // W
HEADS = 16
DH = D // HEADS
M1 = DH + 1
CH = M1 * D
NH9 = M1 * HEADS
E1 = 4
FC = 4
E2 = 8
CAP = 2 * TOKENS // E2
SLOTS = E2 * CAP
ROW = D + 3
LINE1 = TOKENS + CAP
LINE2 = TOKENS
LN_EPS = 1e-5
DEN_EPS = 1e-6
BIG = 3.0e38
MOD = 6

S_DW, S_BG, S_LG, S_LB, S_MG, S_B1, S_WG, S_C = 0, 3, 4, 5, 6, 10, 26, 34
N_SMALL = 36
C_ID, C_TRI, C_BD, C_COS, C_SIN, C_REV, C_TOK, C_SLOT, C_TRASH = 0, 128, 256, 400, 464, 528, 536, 552, 556
N_CONST = C_TRASH + E2 * BT


def block_kernel(nc, x, small, proj, wmod, w1, w2, b2, w_up, w_down, const, cmask, out):
    with ExitStack() as ctx:
        def sb(name, shape, dt=F32):
            return ctx.enter_context(nc.sbuf_tensor(name, shape, dt))

        def sem(name):
            return ctx.enter_context(nc.semaphore(name))

        line1 = nc.dram_tensor("line1", (E2 * LINE1, ROW), F32).ap()
        line2 = nc.dram_tensor("line2", (E2 * LINE2, ROW), F32).ap()
        chosen = nc.dram_tensor("chosen", (2 * TOKENS + SLOTS, D), F32).ap()

        ps = ctx.enter_context(nc.psum_tensor("ps", [P, 8, 512], F32))
        B_D, B_Q, B_KV, B_M, B_UP, B_DN = 0, 1, 2, 4, (5, 6), 7

        c_sb = sb("c_sb", [P, N_CONST])
        cm_sb = sb("cm_sb", [P, 2, P], BF16)
        s_sb = sb("s_sb", [P, N_SMALL])
        proj_sb = sb("proj_sb", [P, 6 * P])
        ident = c_sb[:, C_ID:C_ID + P]
        tri = c_sb[:, C_TRI:C_TRI + P]
        headmask = c_sb[:, C_BD:C_BD + NH9]
        strict, ones = cm_sb[:, 0, :], cm_sb[:, 1, :]
        wmod_sb = sb("wmod_sb", [P, MOD * D])
        w2_sb = sb("w2_sb", [P, E1, FC, D])
        b2_sb = sb("b2_sb", [P, BT, D])
        wd_sb = sb("wd_sb", [P, E2, FC, D])
        wst = sb("wst", [P, E1, W])
        w1h, w1l = sb("w1h", [P, E1, W], F32R), sb("w1l", [P, E1, W], F32R)
        wuh, wul = sb("wuh", [P, E1, W], F32R), sb("wul", [P, E1, W], F32R)
        x_sb = sb("x_sb", [P, TILES, D])
        x2 = sb("x2", [P, TILES, D])
        h3r = sb("h3r", [P, TILES, ROW])
        h3 = h3r[:, :, 0:D]
        wide = sb("wide", [P, BATCH * (3 + 2 * SEQ)])
        hT = wide[:, 0:BATCH * (2 + SEQ)].rearrange("p (b s) -> p b s", b=BATCH)
        x1T = wide[:, BATCH * (2 + SEQ):].rearrange("p (b s) -> p b s", b=BATCH)
        xh = sb("xh", [P, BT, D])
        xm = sb("xm", [P, BT, D])
        conv = sb("conv", [P, W])
        diff = sb("diff", [P, W])
        qk = sb("qk", [P, BT, 2 * D])
        vx = sb("vx", [P, 2, BT, NH9])
        rot_b = sb("rot_b", [P, BT, 2 * D])
        phi = sb("phi", [P, 2, BT, 2 * D])
        kv = sb("kv", [P, 2, CH])
        qp = sb("qp", [P, CH])
        qT = sb("qT", [P, 2, D])
        state = sb("state", [P, NH9])
        nd = sb("nd", [P, 2, NH9])
        rden = sb("rden", [P, 2, HEADS])
        att = sb("att", [P, 2, D])
        attT = sb("attT", [P, W])
        gate = wmod_sb[:, 0:W]
        x2T = attT
        h2T = sb("h2T", [P, W])
        h2h, h2l = sb("h2h", [P, 2, W], F32R), sb("h2l", [P, 2, W], F32R)
        hid = sb("hid", [P, 2, FC, W])
        acc = sb("acc", [P, BT, D])
        gwT = sb("gwT", [P, P])
        gwp = sb("gwp", [P, 2, P])
        h3T = sb("h3T", [P, W])
        st = sb("st", [P, BT, 6])
        mv = [sb(f"mv{i}", [P, TILES, 2]) for i in range(3)]
        ve = [sb(f"ve{i}", [P, TILES]) for i in range(3)]
        rstd = [sb(f"rstd{i}", [P, TILES]) for i in range(3)]
        shift = [sb(f"shift{i}", [P, TILES]) for i in range(2)]
        mhalf = sb("mhalf", [P, BT])
        zero = wuh[:, 0:2, :].bitcast(F32).rearrange("p e f -> p (e f)")
        scT = sb("scT", [P, 2])
        scb = sb("scb", [P, 2, P])
        modT = sb("modT", [P, 2, 2])
        hbg = sb("hbg", [P, 1])
        modb = sb("modb", [P, BATCH, 4, D])
        gtmp = sb("gtmp", [P, 2, BATCH, D])
        sm = sb("sm", [P, BT, 4])
        sm_r = sb("sm_r", [P, 2, BT])
        lg = sb("lg", [P, BT, E2])
        gt_ = sb("gt_", [P, BT, E2])
        rt = sb("rt", [P, 4, BT, E2])
        rs = sb("rs", [P, 10, BT])
        oh = sb("oh", [P, TILES, 2 * E2])
        ohb = sb("ohb", [P, TILES, 2 * E2], BF16)
        before = sb("before", [P, NBLK, 2 * E2], BF16)
        chose = sb("chose", [P, 2 * E2])
        exps = sb("exps", [P, TILES, 2])
        loc = sb("loc", [P, TILES, 2])
        dest = sb("dest", [P, TILES, 2])
        past = sb("past", [P, BT])
        dest_i = sb("dest_i", [P, TILES, 2], U32)
        count = sb("count", [P, E2])
        count_i = sb("count_i", [P, E2], U32)
        second = sb("second", [P, E2, BT])
        trash = sb("trash", [P, E2, BT])
        addr = sb("addr", [P, 4, BT])
        row_w = sb("row_w", [P, E2, BT])
        back_i = sb("back_i", [P, E2, BT], U32)
        back = wide[:, 0:TILES * 2 * D].rearrange("p (k t d) -> p k t d", t=TILES, k=2)

        def rows(e):
            return phi[:, e % 2].rearrange("p t d -> p (t d)")[:, 0:BT * ROW].rearrange("p (t d) -> p t d", t=BT)

        L = lambda n: [sem(f"{n}_{i}") for i in range(NBLK)]
        x_in = L("x_in")
        small_in, mod_in, proj_in, w2_in, wd_in = (sem(n) for n in ("small_in", "mod_in", "proj_in", "w2_in", "wd_in"))
        wst_in = [sem(f"wst_in_{i}") for i in range(3)]
        w_high, w_split = sem("w_high"), sem("w_split")
        zero_ready, zeroed = sem("zero_ready"), sem("zeroed")
        sc_ready, scb_ready, mod_ps, mod_ready = (sem(n) for n in ("sc_ready", "scb_ready", "mod_ps", "mod_ready"))
        pads_ready, v_ones = sem("pads_ready"), sem("v_ones")
        modb_ready, rot0_ready, exp0_ready, phi0_ready = (
            sem(n) for n in ("modb_ready", "rot0_ready", "exp0_ready", "phi0_ready"))
        dve_step, pool_step = sem("dve_step"), sem("pool_step")
        var_ready = [sem(f"var{i}_ready") for i in range(3)]
        rstd_ready = [sem(f"rstd{i}_ready") for i in range(3)]
        xh_ready, hT_ps, hT_ready, conv0_ready, conv_ready, pw_ps, x1_ready, diff_ready = (
            sem(n) for n in ("xh_ready", "hT_ps", "hT_ready", "conv0_ready", "conv_ready", "pw_ps", "x1_ready",
                             "diff_ready"))
        qkv_ps, qkv_ready, rot_parts, rot_ready, exp_ready, phi_ready = (
            sem(n) for n in ("qkv_ps", "qkv_ready", "rot_parts", "rot_ready", "exp_ready", "phi_ready"))
        kv_ready, cum_ps, tail_ps, qT_ps, qT_ready, cum_read, tail_read, state_ready, att_ready, attT_ps, attT_ready = (
            sem(n) for n in ("kv_ready", "cum_ps", "tail_ps", "qT_ps", "qT_ready", "cum_read", "tail_read",
                             "state_ready", "att_ready", "attT_ps", "attT_ready"))
        og_ps, gate_ready, x2T_ready, x2_ps, x2_ready, xm_ready, h2T_ps, h2T_ready, h2_split = (
            sem(n) for n in ("og_ps", "gate_ready", "x2T_ready", "x2_ps", "x2_ready", "xm_ready", "h2T_ps",
                             "h2T_ready", "h2_split"))
        mix_ps, mix_shift, mix_exp, mix_ready, gwT_ps, gwT_ready, b2_ps, acc_ready, x3_ready, h2_high = (
            sem(n) for n in ("mix_ps", "mix_shift", "mix_exp", "mix_ready", "gwT_ps", "gwT_ready", "b2_ps",
                             "acc_ready", "x3_ready", "h2_high"))
        up_ps, hid_ready, down_ps, down_added = (sem(n) for n in ("up_ps", "hid_ready", "down_ps", "down_added"))
        h3_ready, h3T_ps, h3T_ready, route_ps, route_shift, route_exp, onehot_ready, pos_ps, dest_ready = (
            sem(n) for n in ("h3_ready", "h3T_ps", "h3T_ready", "route_ps", "route_shift", "route_exp",
                             "onehot_ready", "pos_ps", "dest_ready"))
        count_ready, scattered = sem("count_ready"), [sem(f"scattered_{k}") for k in range(2)]
        moved = [sem(f"moved_{e}") for e in range(E2)]
        rows_in = [sem(f"rows_in_{e}") for e in range(E2)]
        rowsT_ps, rowsT_hi, rowsT_lo, eup_ps, ehid_ready, edown_ps, eout_ready, back_i_ready = (
            sem(n) for n in ("rowsT_ps", "rowsT_hi", "rowsT_lo", "eup_ps", "ehid_ready", "edown_ps", "eout_ready",
                             "back_i_ready"))
        chosen_written = [sem(f"chosen_written_{i}") for i in range(2)]
        back_in = L("back_in")
        both_ready, comb_ready, stored = sem("both_ready"), sem("comb_ready"), sem("stored")

        LAG = BT + 3
        STEPS = NBLK * E1 + LAG
        LAST = NBLK - 1
        LAST_BANKS = (7, 0, 1, 2)

        def live(blk):
            return 0 <= blk < NBLK

        def qkv_bank(t):
            blk, j = divmod(t, BT)
            return ((B_Q, B_KV, B_KV + 1, B_M), (B_Q, B_UP[0], B_UP[1], B_Q))[min(blk, 1)][j] if blk < 3 else B_Q

        def pw_bank(blk):
            return B_DN if 1 <= blk <= 2 else B_D

        def mix_bank(e):
            return B_KV if e == NBLK * E1 - 1 else B_DN

        def cols(ap, blk, pad):
            o = pad + (blk % BPB) * W
            return ap[:, blk // BPB, o:o + W]

        def wait_phi(engine, t):
            if t == 0:
                engine.wait_ge(phi0_ready, 1)
            else:
                engine.wait_ge(phi_ready, t // BT + 1)

        def up_weights(k):
            return (wuh, wul) if k // E1 == 1 else (w1h, w1l)

        def tiles(ap, blk):
            return ap[:, blk * BT:(blk + 1) * BT]

        def xstage(e):
            return (xh if e % 2 == 0 else xm)[:]

        def gelus(act, e):
            for c in range(FC):
                u = e * FC + c
                act.wait_ge(eup_ps, u + 1)
                if e >= 2 and c == 0:
                    act.wait_ge(edown_ps, e - 1)
                if e < 2 and c == 0:
                    act.wait_ge(down_ps, NBLK * E1)
                nc.scalar.activation(hid[:, e % 2, c, :], ps[:, 2 + c, :], ACT.Gelu).then_inc(ehid_ready, 1)

        block = ctx.enter_context(nc.Block())

        @block.sync
        def _(sp):
            xv = x.rearrange("b (t p) d -> p (b t) d", p=P)
            ov = out.rearrange("b (t p) d -> p (b t) d", p=P)
            sp.dma_start(tiles(x_sb, 0), tiles(xv, 0)).then_inc(x_in[0], 16)
            sp.dma_start(s_sb[:], small).then_inc(small_in, 16)
            sp.dma_start(c_sb[:], const).then_inc(small_in, 16)
            sp.dma_start(cm_sb[:], cmask).then_inc(small_in, 16)
            sp.dma_start(wmod_sb[:], wmod).then_inc(mod_in, 16)
            sp.dma_start(tiles(x_sb, 1), tiles(xv, 1)).then_inc(x_in[1], 16)
            sp.dma_start(proj_sb[:], proj).then_inc(proj_in, 16)
            sp.dma_start(wst[:], w1).then_inc(wst_in[0], 16)
            for b in range(2, NBLK):
                sp.dma_start(tiles(x_sb, b), tiles(xv, b)).then_inc(x_in[b], 16)
            sp.dma_start(w2_sb[:], w2).then_inc(w2_in, 16)
            sp.dma_start(b2_sb[:], b2).then_inc(w2_in, 16)
            sp.dma_start(wd_sb[:], w_down).then_inc(wd_in, 16)
            sp.wait_ge(zero_ready, 1)
            for e in range(E2):
                sp.dma_start(line2[e * LINE2:e * LINE2 + CAP, :].rearrange("(p r) d -> p (r d)", p=P),
                             zero[:, 0:BT * ROW]).then_inc(zeroed, 16)
            cz = chosen[0:2 * TOKENS, :].rearrange("(p r) d -> p (r d)", p=P)
            for i in range(BT):
                sp.dma_start(cz[:, i * 1024:(i + 1) * 1024], zero).then_inc(zeroed, 16)
            for half in range(2):
                sp.wait_ge(w_split, E1 * (half + 1))
                sp.dma_start(wst[:], w_up[:, half * E1:(half + 1) * E1, :]).then_inc(wst_in[1 + half], 16)
            def append(e):
                sp.dma_start(line1[bass.ds(first[e] + e * LINE1, CAP), :],
                             line2[e * LINE2:e * LINE2 + CAP, :]).then_inc(moved[e], 16)

            sp.wait_ge(count_ready, 1)
            first = [sp.value_load(count_i[0:1, e:e + 1], min_val=0, max_val=CAP) for e in range(E2)]
            sp.wait_ge(scattered[1], 16 * TILES)
            append(0)
            append(1)
            sp.wait_ge(scattered[0], 16 * TILES)
            for e in range(E2):
                sp.wait_ge(moved[e], 16)
                if 1 <= e < E2 - 1:
                    append(e + 1)
                if e >= 2:
                    sp.wait_ge(rowsT_ps, e - 1)
                    sp.wait_ge(back_i_ready, e - 1)
                sp.dma_start(rows(e), line1[e * LINE1:e * LINE1 + CAP, :].rearrange("(t p) d -> p t d", p=P)) \
                    .then_inc(rows_in[e], 16)
            cv = chosen[0:2 * TOKENS, :].rearrange("(k t p) d -> p k t d", k=2, p=P)
            for half in chosen_written:
                sp.wait_ge(half, 16 * BT * E2 // 2)
            for b in range(NBLK):
                for k in range(2):
                    sp.dma_start(tiles(back[:, k], b), tiles(cv[:, k], b)).then_inc(back_in[b], 16)
            for b in range(NBLK):
                sp.wait_ge(comb_ready, b + 1)
                sp.dma_start(tiles(ov, b), tiles(x_sb, b)).then_inc(stored, 16)
            sp.wait_ge(stored, 16 * NBLK)

        @block.gpsimd
        def _(pool):
            g = nc.gpsimd
            n = [0]

            def step(ins):
                n[0] += 1
                ins.then_inc(pool_step, 1)
                return n[0]

            g.memset(zero, 0.0).then_inc(zero_ready, 1)
            a = step(g.memset(mhalf[:], -0.5))
            g.memset(gwp[:], 0.0)
            g.memset(before[:, 0, :], 0.0)
            for par in range(2):
                for j in range(BT):
                    last = g.memset(vx[:, par, j, DH * HEADS:NH9], 1.0)
            last.then_inc(v_ones, 1)
            pool.wait_ge(pool_step, a)

            def inv_std(i, blk):
                pool.wait_ge(var_ready[i], blk + 1)
                a = step(g.tensor_scalar(tiles(ve[i], blk), tiles(mv[i], blk)[:, :, 1], LN_EPS, None, ALU.add))
                if i < 2:
                    a = step(g.tensor_scalar(tiles(shift[i], blk), tiles(mv[i], blk)[:, :, 0], -1.0, None, ALU.mult))
                pool.wait_ge(pool_step, a)
                ins = g.tensor_tensor(tiles(rstd[i], blk), tiles(ve[i], blk), mhalf[:], ALU.pow)
                if i == 2:
                    ins.then_inc(rstd_ready[i], 1)
                    return
                pool.wait_ge(pool_step, step(ins))
                g.tensor_tensor(tiles(shift[i], blk), tiles(shift[i], blk), tiles(rstd[i], blk), ALU.mult) \
                    .then_inc(rstd_ready[i], 1)

            def split(k):
                hi, lo = (w[:, k % E1, :] for w in up_weights(k))
                pool.wait_ge(w_high, k + 1)
                g.tensor_tensor(lo, wst[:, k % E1, :], hi.bitcast(F32), ALU.subtract).then_inc(w_split, 1)

            def difference(blk):
                pool.wait_ge(x1_ready, blk + 1)
                if blk >= 1:
                    pool.wait_ge(og_ps, blk)
                g.tensor_tensor(diff[:], cols(x1T, blk, 1), cols(x1T, blk, 0), ALU.subtract) \
                    .then_inc(diff_ready, 1)

            def residual3(blk):
                pool.wait_ge(down_added, (blk + 1) * E1)
                ga = modb[:, blk // BPB, 0, None, :].broadcast_to([P, BT, D])
                pool.wait_ge(pool_step, step(g.tensor_tensor(acc[:], acc[:], ga, ALU.mult)))
                g.tensor_tensor(tiles(x_sb, blk), acc[:], tiles(x_sb, blk), ALU.add).then_inc(x3_ready, 1)

            def rotate_sum(blk):
                pool.wait_ge(rot_parts, blk)
                a = phi[:, blk % 2]
                g.tensor_tensor(a, a, rot_b[:], ALU.add).then_inc(rot_ready, 1)

            def outer(t):
                blk, j = t // BT, t % BT
                wait_phi(pool, t)
                if t == 0:
                    pool.wait_ge(v_ones, 1)
                    pool.wait_ge(qkv_ready, 1)
                else:
                    pool.wait_ge(qkv_ready, BT * blk + BT)
                if t >= 2:
                    pool.wait_ge(tail_ps, t - 1)
                k_ = phi[:, blk % 2, j, D:2 * D].rearrange("p (h d) -> p h d", h=HEADS)[:, None, :, :] \
                    .broadcast_to([P, M1, HEADS, DH])
                v_ = vx[:, blk % 2, j, :].rearrange("p (m h) -> p m h", m=M1)[:, :, :, None] \
                    .broadcast_to([P, M1, HEADS, DH])
                o_ = kv[:, t % 2, :].rearrange("p (m h d) -> p m h d", m=M1, h=HEADS)
                g.tensor_tensor(o_, k_, v_, ALU.mult).then_inc(kv_ready, 1)

            def scatter(k, t):
                g.indirect_dma_start(out=(line1, line2)[k],
                                     out_offset=bass.IndirectOffsetOnAxis(dest_i[:, t, k:k + 1], 0),
                                     in_=h3r[:, t, :], in_offset=None).then_inc(scattered[k], 16)

            def scatters(blk):
                pool.wait_ge(dest_ready, blk + 1)
                for k in (1, 0):
                    for j in range(BT):
                        scatter(k, BT * blk + j)

            inv_std(0, 0)
            inv_std(0, 1)
            outer(0)
            for s in range(STEPS):
                b, f = divmod(s, BT)
                if f == 3 and b >= 2 and live(b + 1):
                    rotate_sum(b + 1)
                if f == 2 and live(b - 1):
                    inv_std(1, b - 1)
                if s + 1 < TILES:
                    outer(s + 1)
                if f == 2 and b < 2:
                    rotate_sum(b + 1)
                if f == 0 and live(b - 3):
                    residual3(b - 3)
                if f == 1 and live(b - 3):
                    inv_std(2, b - 3)
                if f == 2 and live(b + 2):
                    inv_std(0, b + 2)
                if f == 3 and live(b):
                    difference(b)
                if s < 2 * E1:
                    split(s)
                if f == 2 and live(b - 4):
                    scatters(b - 4)
            inv_std(2, LAST)
            scatters(LAST - 1)
            scatters(LAST)
            for e in range(E1):
                split(2 * E1 + e)
            for e in range(E2):
                for j in range(BT):
                    pool.wait_ge(eout_ready, BT * e + j + 1)
                    g.indirect_dma_start(out=chosen, out_offset=bass.IndirectOffsetOnAxis(back_i[:, e, j:j + 1], 0),
                                         in_=xstage(e)[:, j, :], in_offset=None).then_inc(chosen_written[e % 2], 16)

            for blk in range(NBLK):
                pool.wait_ge(back_in[blk], 32)
                a, b_ = tiles(back[:, 0], blk), tiles(back[:, 1], blk)
                g.tensor_tensor(a, a, b_, ALU.add).then_inc(both_ready, 1)

        @block.scalar
        def _(act):
            a_ = nc.scalar

            act.wait_ge(small_in, 48)
            a_.activation(scT[:], s_sb[:, S_C:S_C + 2], ACT.Silu).then_inc(sc_ready, 1)

            def normalise(i, blk, src, dst, done):
                act.wait_ge(rstd_ready[i], blk + 1)
                for j in range(BT):
                    t = BT * blk + j
                    last = a_.activation(dst[:, j, :], src[:, t, :], ACT.Identity, bias=shift[i][:, t:t + 1],
                                         scale=rstd[i][:, t:t + 1])
                last.then_inc(done, 1)

            def modulation_rows():
                act.wait_ge(mod_ps, 2)
                for b in range(BATCH):
                    last = a_.activation(modb[:, b].rearrange("p m d -> p (m d)"), ps[:, B_UP[b], :], ACT.Copy)
                last.then_inc(modb_ready, 1)

            def high_part(k):
                act.wait_ge(wst_in[k // E1], 16)
                if k == E1:
                    act.wait_ge(zeroed, 16 * (E2 + BT))
                if k == 2 * E1:
                    act.wait_ge(up_ps, NBLK * E1 * FC)
                a_.activation(up_weights(k)[0][:, k % E1, :], wst[:, k % E1, :], ACT.Copy).then_inc(w_high, 1)

            def xhat(blk):
                if blk >= 1:
                    act.wait_ge(hT_ps, blk)
                normalise(0, blk, x_sb, xh, xh_ready)

            def xhat2(blk):
                if blk >= 1:
                    act.wait_ge(h2T_ps, blk)
                normalise(1, blk, x2, xm, xm_ready)

            def hT_evac(blk):
                b = blk // BPB
                act.wait_ge(hT_ps, blk + 1)
                if blk == 0:
                    act.wait_ge(mod_ready, 1)
                    act.wait_ge(pads_ready, 1)
                a_.activation(cols(hT, blk, 2), ps[:, B_D, :], ACT.Identity, bias=modT[:, 0, b:b + 1],
                              scale=modT[:, 1, b:b + 1]).then_inc(hT_ready, 1)
                act.wait_ge(hT_ready, blk + 1)
                if blk >= 1:
                    act.wait_ge(pw_ps, blk)
                a_.activation(conv[:], cols(hT, blk, 0), ACT.Copy, scale=s_sb[:, S_DW:S_DW + 1]) \
                    .then_inc(conv0_ready, 1)

            def qkv_evac(t):
                blk, j = t // BT, t % BT
                act.wait_ge(qkv_ps, t + 1)
                if j == 0 and blk >= 1:
                    act.wait_ge(phi_ready, blk)
                if j == 0 and blk >= 2:
                    act.wait_ge(kv_ready, BT * (blk - 1))
                    act.wait_ge(tail_ps, BT * (blk - 1))
                a_.activation(qk[:, j, :], ps[:, qkv_bank(t), 0:2 * D], ACT.Copy)
                a_.activation(vx[:, blk % 2, j, 0:D].rearrange("p (m h) -> p m h", m=DH),
                              ps[:, qkv_bank(t), 2 * D:3 * D].rearrange("p (h m) -> p m h", m=DH), ACT.Copy) \
                    .then_inc(qkv_ready, 1)

            def phi_exp(blk):
                act.wait_ge(rot_ready, blk + 1)
                if blk >= 1:
                    act.wait_ge(phi_ready, blk)
                a_.activation(rot_b[:], phi[:, blk % 2], ACT.Exp)
                a_.activation(qk[:], phi[:, blk % 2], ACT.Relu).then_inc(exp_ready, 1)

            def qT_evac(t):
                act.wait_ge(qT_ps, t + 1)
                if t >= 2:
                    act.wait_ge(tail_ps, t - 1)
                a_.activation(qT[:, t % 2, :], ps[:, B_Q, 384:512], ACT.Copy).then_inc(qT_ready, 1)

            def attT_evac(t):
                blk, j = t // BT, t % BT
                act.wait_ge(attT_ps, t + 1)
                if j == 0 and blk >= 1:
                    act.wait_ge(x2_ps, blk)
                a_.activation(attT[:, j * P:(j + 1) * P], ps[:, B_Q, 384:512], ACT.Copy).then_inc(attT_ready, 1)

            def gate_evac(blk):
                act.wait_ge(og_ps, blk + 1)
                if blk >= 1:
                    act.wait_ge(x2T_ready, blk)
                a_.activation(gate[:], ps[:, B_Q, :], ACT.Tanh, bias=hbg[:, 0:1], scale=0.5) \
                    .then_inc(gate_ready, 1)

            def x2_evac(blk):
                act.wait_ge(x2_ps, blk + 1)
                a_.activation(tiles(x2, blk), ps[:, B_D, :].rearrange("p (t d) -> p t d", t=BT), ACT.Copy) \
                    .then_inc(x2_ready, 1)

            def h2T_evac(blk):
                act.wait_ge(h2T_ps, blk + 1)
                if blk >= 1:
                    act.wait_ge(h2_split, blk)
                    act.wait_ge(mix_ps, blk)
                if blk >= 2:
                    act.wait_ge(up_ps, (blk - 1) * E1 * FC)
                a_.activation(h2T[:], ps[:, B_D, :], ACT.Identity, bias=s_sb[:, S_LB:S_LB + 1],
                              scale=s_sb[:, S_LG:S_LG + 1]).then_inc(h2T_ready, 1)
                act.wait_ge(h2T_ready, blk + 1)
                a_.activation(h2h[:, blk % 2, :], h2T[:], ACT.Copy).then_inc(h2_high, 1)

            def mix_exps(blk):
                act.wait_ge(mix_shift, blk + 1)
                a_.activation(sm[:], sm[:], ACT.Exp).then_inc(mix_exp, 1)

            def gwT_evac(blk):
                act.wait_ge(gwT_ps, blk + 1)
                if blk >= 1:
                    act.wait_ge(b2_ps, blk)
                a_.activation(gwT[:], ps[:, B_D, 0:P], ACT.Copy).then_inc(gwT_ready, 1)

            def silu(u):
                e = u // FC
                act.wait_ge(up_ps, u + 1)
                if e >= 2:
                    act.wait_ge(down_ps, e - 1)
                c = S_B1 + u % (E1 * FC)
                a_.activation(hid[:, e % 2, u % FC, :], ps[:, B_UP[u % 2], :], ACT.Silu,
                              bias=s_sb[:, c:c + 1]).then_inc(hid_ready, 1)

            def h3T_evac(blk):
                act.wait_ge(h3T_ps, blk + 1)
                if blk >= 1:
                    act.wait_ge(route_ps, blk)
                a_.activation(h3T[:], ps[:, B_D, :], ACT.Copy).then_inc(h3T_ready, 1)

            def route_exps(blk):
                act.wait_ge(route_shift, blk + 1)
                a_.activation(gt_[:], gt_[:], ACT.Exp).then_inc(route_exp, 1)

            xhat(0)
            hT_evac(0)
            xhat(1)
            a_.preload_act_table(ACT.Exp)
            modulation_rows()
            qkv_evac(0)
            qkv_evac(1)
            act.wait_ge(rot0_ready, 1)
            a_.activation(rot_b[:, 0], phi[:, 0, 0], ACT.Exp)
            a_.activation(qk[:, 0], phi[:, 0, 0], ACT.Relu).then_inc(exp0_ready, 1)
            qkv_evac(2)
            qkv_evac(3)
            act.wait_ge(rot_ready, 1)
            a_.activation(rot_b[:, 1:], phi[:, 0, 1:], ACT.Exp)
            a_.activation(qk[:, 1:], phi[:, 0, 1:], ACT.Relu).then_inc(exp_ready, 1)
            for s in range(STEPS):
                b, f = divmod(s, BT)
                e = s - LAG

                def silus(c0):
                    if 0 <= e < NBLK * E1:
                        for c in range(c0, c0 + 2):
                            silu(e * FC + c)

                def query(s):
                    if s < TILES:
                        qT_evac(s)

                def attended(s):
                    if 1 <= s <= TILES:
                        attT_evac(s - 1)

                if f == 0:
                    if live(b + 1):
                        hT_evac(b + 1)
                    silus(0)
                    query(s)
                    if live(b - 2):
                        gwT_evac(b - 2)
                    attended(s)
                    if live(b - 1):
                        gate_evac(b - 1)
                    silus(2)
                if f == 1:
                    silus(0)
                    query(s)
                    if live(b - 1):
                        x2_evac(b - 1)
                    if live(b + 1):
                        qkv_evac(BT * (b + 1))
                    silus(2)
                    if live(b + 1):
                        qkv_evac(BT * (b + 1) + 1)
                        qkv_evac(BT * (b + 1) + 2)
                    attended(s)
                if f == 2:
                    if live(b + 1):
                        qkv_evac(BT * (b + 1) + 3)
                    if b >= 2 and live(b - 1):
                        xhat2(b - 1)
                    silus(0)
                    if live(b - 3):
                        h3T_evac(b - 3)
                    query(s)
                    if b == 1:
                        xhat2(0)
                    if live(b - 1):
                        h2T_evac(b - 1)
                    silus(2)
                    attended(s)
                if f == 3:
                    query(s)
                    silus(0)
                    if live(b - 3):
                        route_exps(b - 3)
                    if live(b + 1):
                        phi_exp(b + 1)
                    if live(b - 1):
                        mix_exps(b - 1)
                    silus(2)
                    attended(s)
                    if live(b + 2):
                        xhat(b + 2)
                if s < 2 * E1:
                    high_part(s)
            route_exps(LAST - 1)
            h3T_evac(LAST)
            route_exps(LAST)
            for e in range(E1):
                high_part(2 * E1 + e)

            for e in range(E2):
                act.wait_ge(rowsT_ps, e + 1)
                if e >= 2:
                    act.wait_ge(eup_ps, FC * (e - 1))
                a_.activation(h2h[:, e % 2, :], ps[:, e % 2, :], ACT.Copy).then_inc(rowsT_hi, 1)
                if e >= 1:
                    gelus(act, e - 1)
            gelus(act, E2 - 1)
        @block.vector
        def _(dve):
            v = nc.vector
            n = [0]

            def step(ins):
                n[0] += 1
                ins.then_inc(dve_step, 1)
                return n[0]

            def after(k=None):
                dve.wait_ge(dve_step, n[0] if k is None else k)

            v.memset(hT[:, :, 0:2], 0.0).then_inc(pads_ready, 1)

            statistics = []

            def stats(i, blk, src):
                if statistics:
                    dve.wait_ge(*statistics[-1])
                statistics.append((var_ready[i], blk + 1))
                for j in range(BT):
                    step(v.bn_stats(st[:, j, :], src[:, j, :]))
                after()
                for j in range(BT):
                    last = v.bn_aggr(tiles(mv[i], blk)[:, j, :], st[:, j, :])
                last.then_inc(var_ready[i], 1)

            def modulation():
                dve.wait_ge(sc_ready, 1)
                v.tensor_copy(scb[:], scT[:, :, None].broadcast_to([P, 2, P])).then_inc(scb_ready, 1)
                v.tensor_scalar(hbg[:], s_sb[:, S_BG:S_BG + 1], 0.5, None, ALU.mult)
                dve.wait_ge(mod_ps, 1)
                v.tensor_copy(modT[:, 0, :], ps[:, B_D, 0:2])
                v.tensor_scalar(modT[:, 1, :], ps[:, B_D, 2:4], 1.0, None, ALU.add).then_inc(mod_ready, 1)

            def residual_scales():
                dve.wait_ge(modb_ready, 1)
                v.tensor_scalar(modb[:, :, 2, :], modb[:, :, 2, :], 1.0, None, ALU.add)
                for m in (0, 3):
                    s = modb[:, :, m, :]
                    t0, t1 = gtmp[:, 0], gtmp[:, 1]
                    step(v.tensor_scalar(t0, s, -1.0, None, ALU.mult))
                    after()
                    step(v.tensor_tensor(t1, t0, s, ALU.max))
                    after()
                    v.tensor_scalar(t1, t1, 0.25, None, ALU.max)
                    step(v.tensor_scalar(t0, s, 0.0, 2.0, ALU.is_ge, ALU.mult))
                    after()
                    step(v.tensor_scalar(t0, t0, -1.0, None, ALU.add))
                    after()
                    step(v.tensor_tensor(s, t0, t1, ALU.mult))
                    after()

            def ln1(blk):
                dve.wait_ge(x_in[blk], 16)
                stats(0, blk, tiles(x_sb, blk))

            def conv_taps(blk):
                dve.wait_ge(conv0_ready, blk + 1)
                h = hT[:, blk // BPB, (blk % BPB) * W:(blk % BPB) * W + W + 2]
                step(v.scalar_tensor_tensor(conv[:], h[:, 1:1 + W], s_sb[:, S_DW + 1:S_DW + 2], conv[:],
                                            ALU.mult, ALU.add))
                after()
                v.scalar_tensor_tensor(conv[:], h[:, 2:2 + W], s_sb[:, S_DW + 2:S_DW + 3], conv[:],
                                       ALU.mult, ALU.add).then_inc(conv_ready, 1)

            def residual1(blk):
                dve.wait_ge(pw_ps, blk + 1)
                ins = v.tensor_tensor(cols(x1T, blk, 1), ps[:, pw_bank(blk), :], cols(hT, blk, 2), ALU.add)
                if blk % BPB == 0:
                    step(ins)
                    after()
                    ins = v.tensor_copy(x1T[:, blk // BPB, 0:1], x1T[:, blk // BPB, 1:2])
                ins.then_inc(x1_ready, 1)

            def rotate(blk):
                dve.wait_ge(qkv_ready, BT * blk + BT)
                dve.wait_ge(phi_ready, blk)
                if blk >= 2:
                    dve.wait_ge(tail_ps, BT * (blk - 1))
                    dve.wait_ge(kv_ready, BT * (blk - 1))
                rotated(blk, 0, BT).then_inc(rot_parts, 1)

            def rotated(blk, j0, j1):
                nj = j1 - j0
                i = (blk % BPB * BT + j0) * DH
                cs, sn = (c_sb[:, c + i:c + i + nj * DH].rearrange("p (t e) -> p t e", t=nj)[:, :, None, :]
                          .broadcast_to([P, nj, 2 * HEADS, DH]) for c in (C_COS, C_SIN))
                q4 = qk[:, j0:j1].rearrange("p t (h e) -> p t h e", e=DH)
                v.tensor_tensor(phi[:, blk % 2, j0:j1].rearrange("p t (h e) -> p t h e", e=DH), q4, cs, ALU.mult)
                pair = lambda ap: ap.rearrange("p t h (f two) -> p t h f two", two=2)
                return v.tensor_tensor(pair(rot_b[:, j0:j1].rearrange("p t (h e) -> p t h e", e=DH)),
                                       pair(q4)[:, :, :, :, ::-1], pair(sn), ALU.mult)

            def first_features():
                dve.wait_ge(qkv_ready, 1)
                step(rotated(0, 0, 1))
                after()
                v.tensor_tensor(phi[:, 0, 0], phi[:, 0, 0], rot_b[:, 0], ALU.add).then_inc(rot0_ready, 1)
                dve.wait_ge(exp0_ready, 1)
                v.scalar_tensor_tensor(phi[:, 0, 0], rot_b[:, 0], 1.0, qk[:, 0], ALU.min, ALU.add) \
                    .then_inc(phi0_ready, 1)
                dve.wait_ge(qkv_ready, BT)
                step(rotated(0, 1, BT))
                after()
                v.tensor_tensor(phi[:, 0, 1:], phi[:, 0, 1:], rot_b[:, 1:], ALU.add).then_inc(rot_ready, 1)
                dve.wait_ge(exp_ready, 1)
                v.scalar_tensor_tensor(phi[:, 0, 1:], rot_b[:, 1:], 1.0, qk[:, 1:], ALU.min, ALU.add) \
                    .then_inc(phi_ready, 1)

            def feature(blk):
                dve.wait_ge(exp_ready, blk + 1)
                v.scalar_tensor_tensor(phi[:, blk % 2], rot_b[:], 1.0, qk[:], ALU.min, ALU.add).then_inc(phi_ready, 1)

            def attend(t):
                j, first, lastt = t % BT, t % TPB == 0, t % TPB == TPB - 1
                q_ = phi[:, t // BT % 2, j, 0:D]
                dve.wait_ge(cum_ps, t + 1)
                if t >= 1:
                    dve.wait_ge(att_ready, t)
                v.tensor_tensor(qp[:, 0:DH * D].rearrange("p (m c) -> p m c", m=DH),
                                ps[:, B_KV:B_KV + 2, :].rearrange("p b (m c) -> p (b m) c", m=4),
                                q_[:, None, :].broadcast_to([P, DH, D]), ALU.mult).then_inc(cum_read, 1)
                dve.wait_ge(tail_ps, t + 1)
                a = step(v.tensor_tensor(qp[:, DH * D:CH], ps[:, B_M, 0:D], q_, ALU.mult))
                if not lastt:
                    v.tensor_tensor(state[:], ps[:, B_M, 2 * D + 16:2 * D + 16 + NH9], headmask, ALU.mult) \
                        .then_inc(state_ready, 1) if first else state_add(t)
                else:
                    v.tensor_copy(state[0:1, 0:1], state[0:1, 0:1]).then_inc(state_ready, 1)
                dve.wait_ge(cum_read, t + 1)
                after(a)
                a = step(v.tensor_reduce(nd[:, 0, :], qp[:].rearrange("p (c d) -> p c d", d=DH), AX.X, ALU.add))
                after(a)
                if first:
                    r, ins = 0, v.tensor_copy(rden[:, 1, 0:1], nd[:, 0, 0:1])
                else:
                    r, ins = 1, v.tensor_tensor(nd[:, 1, :], ps[:, B_M, D:D + NH9], nd[:, 0, :], ALU.add)
                ins.then_inc(tail_read, 1)
                dve.wait_ge(tail_read, t + 1)
                a = step(v.tensor_scalar(rden[:, 0, :], nd[:, r, DH * HEADS:NH9], DEN_EPS, None, ALU.add))
                after(a)
                a = step(v.reciprocal(rden[:, 1, :], rden[:, 0, :]))
                after(a)
                if t >= 2:
                    dve.wait_ge(attT_ps, t - 1)
                v.tensor_tensor(att[:, t % 2, :].rearrange("p (h m) -> p m h", m=DH),
                                nd[:, r, 0:D].rearrange("p (m h) -> p m h", m=DH),
                                rden[:, 1, None, :].broadcast_to([P, DH, HEADS]), ALU.mult).then_inc(att_ready, 1)

            def state_add(t):
                a = step(v.tensor_tensor(gtmp[:, 0, 0:2].rearrange("p a d -> p (a d)")[:, 0:NH9],
                                         ps[:, B_M, 2 * D + 16:2 * D + 16 + NH9], headmask, ALU.mult))
                after(a)
                v.tensor_tensor(state[:], gtmp[:, 0, 0:2].rearrange("p a d -> p (a d)")[:, 0:NH9], state[:],
                                ALU.add).then_inc(state_ready, 1)

            def residual2(blk):
                dve.wait_ge(gate_ready, blk + 1)
                if blk >= 1:
                    dve.wait_ge(x2_ps, blk)
                step(v.scalar_tensor_tensor(x2T[:], gate[:], 1.0, ps[:, B_D, :], ALU.add, ALU.mult))
                after()
                v.scalar_tensor_tensor(x2T[:], x2T[:], 0.5, cols(x1T, blk, 1), ALU.mult, ALU.add) \
                    .then_inc(x2T_ready, 1)

            def ln2(blk):
                dve.wait_ge(x2_ready, blk + 1)
                stats(1, blk, tiles(x2, blk))

            def split2(blk):
                dve.wait_ge(h2_high, blk + 1)
                if blk >= 2:
                    dve.wait_ge(up_ps, (blk - 1) * E1 * FC)
                i = blk % 2
                v.tensor_tensor(h2l[:, i, :], h2T[:], h2h[:, i, :].bitcast(F32), ALU.subtract).then_inc(h2_split, 1)

            def mix_a(blk):
                dve.wait_ge(mix_ps, blk + 1)
                lp = ps[:, B_D, 0:BT * E1].rearrange("p (t e) -> p t e", t=BT)
                step(v.tensor_reduce(sm_r[:, 0, :], lp, AX.X, ALU.max))
                after()
                v.tensor_tensor(sm[:], lp, sm_r[:, 0, :, None].broadcast_to([P, BT, E1]), ALU.subtract) \
                    .then_inc(mix_shift, 1)

            def mix_b(blk):
                dve.wait_ge(mix_exp, blk + 1)
                step(v.tensor_reduce(sm_r[:, 0, :], sm[:], AX.X, ALU.add))
                after()
                step(v.reciprocal(sm_r[:, 1, :], sm_r[:, 0, :]))
                after()
                if blk == 0:
                    dve.wait_ge(v_ones, 1)
                v.tensor_tensor(gwp[:, blk % 2, 0:BT * E1].rearrange("p (t e) -> p t e", t=BT), sm[:],
                                sm_r[:, 1, :, None].broadcast_to([P, BT, E1]), ALU.mult).then_inc(mix_ready, 1)

            def acc_start(blk):
                dve.wait_ge(b2_ps, blk + 1)
                if blk >= 1:
                    dve.wait_ge(x3_ready, blk)
                v.tensor_tensor(acc[:], ps[:, B_Q, :].rearrange("p (t d) -> p t d", t=BT), tiles(x2, blk),
                                ALU.add).then_inc(acc_ready, 1)
                dve.wait_ge(acc_ready, blk + 1)

            def add_expert(e):
                dve.wait_ge(down_ps, e + 1)
                for j in range(BT):
                    c = j * E1 + e % E1
                    last = v.scalar_tensor_tensor(acc[:, j, :], ps[:, mix_bank(e), j * D:(j + 1) * D],
                                                  gwp[:, e // E1 % 2, c:c + 1], acc[:, j, :], ALU.mult, ALU.add)
                last.then_inc(down_added, 1)
                dve.wait_ge(down_added, e + 1)

            def residual3(blk):
                b = blk // BPB
                step(v.tensor_tensor(acc[:], acc[:], modb[:, b, 0, None, :].broadcast_to([P, BT, D]), ALU.mult))
                after()
                step(v.tensor_tensor(tiles(x_sb, blk), acc[:], tiles(x_sb, blk), ALU.add))
                after()

            def norm3(blk):
                b = blk // BPB
                dve.wait_ge(rstd_ready[2], blk + 1)
                for j in range(BT):
                    t = BT * blk + j
                    step(v.scalar_tensor_tensor(h3[:, t, :], x_sb[:, t, :], mv[2][:, t, 0:1], modb[:, b, 2, :],
                                                ALU.subtract, ALU.mult))
                after()
                for j in range(BT):
                    t = BT * blk + j
                    last = v.scalar_tensor_tensor(h3[:, t, :], h3[:, t, :], rstd[2][:, t:t + 1], modb[:, b, 1, :],
                                                  ALU.mult, ALU.add)
                last.then_inc(h3_ready, 1)

            def bc(ap):
                return ap[:, :, None].broadcast_to([P, BT, E2])

            def route_a(blk):
                dve.wait_ge(route_ps, blk + 1)
                step(v.tensor_copy(lg[:], ps[:, B_D, 0:BT * E2].rearrange("p (t e) -> p t e", t=BT)))
                after()
                step(v.tensor_reduce(rs[:, 0, :], lg[:], AX.X, ALU.max))
                after()
                v.tensor_tensor(gt_[:], lg[:], bc(rs[:, 0, :]), ALU.subtract).then_inc(route_shift, 1)

            def first_of_max(src, mx, rank, onehot, onehot_b):
                rev = c_sb[:, None, C_REV:C_REV + E2].broadcast_to([P, BT, E2])
                step(v.tensor_reduce(mx, src, AX.X, ALU.max))
                after()
                step(v.tensor_tensor(rt[:, 0], src, bc(mx), ALU.is_equal))
                after()
                step(v.tensor_tensor(rt[:, 1], rt[:, 0], rev, ALU.mult))
                after()
                step(v.tensor_reduce(rank, rt[:, 1], AX.X, ALU.max))
                after()
                v.tensor_tensor(onehot_b, rt[:, 1], bc(rank), ALU.is_equal)
                step(v.tensor_tensor(onehot, rt[:, 1], bc(rank), ALU.is_equal))
                after()

            def route_b(blk):
                dve.wait_ge(route_exp, blk + 1)
                o = tiles(oh, blk)
                ob = tiles(ohb, blk)
                step(v.tensor_reduce(rs[:, 1, :], gt_[:], AX.X, ALU.add))
                after()
                step(v.reciprocal(rs[:, 2, :], rs[:, 1, :]))
                after()
                step(v.tensor_tensor(gt_[:], gt_[:], bc(rs[:, 2, :]), ALU.mult))
                after()
                first_of_max(gt_[:], rs[:, 3, :], rs[:, 4, :], o[:, :, 0:E2], ob[:, :, 0:E2])
                step(v.scalar_tensor_tensor(lg[:], o[:, :, 0:E2], -BIG, lg[:], ALU.mult, ALU.add))
                after()
                first_of_max(lg[:], rs[:, 5, :], rs[:, 6, :], o[:, :, E2:2 * E2], ob[:, :, E2:2 * E2])
                if blk == 0:
                    dve.wait_ge(v_ones, 1)
                v.tensor_reduce(chose[:], o.rearrange("p t e -> p e t"), AX.X, ALU.add).then_inc(onehot_ready, 1)
                dve.wait_ge(onehot_ready, blk + 1)
                if blk < LAST:
                    v.tensor_tensor(before[:, blk + 1, :], before[:, blk, :], chose[:], ALU.add)
                step(v.tensor_tensor(rt[:, 2], gt_[:], o[:, :, E2:2 * E2], ALU.mult))
                after()
                step(v.tensor_reduce(rs[:, 7, :], rt[:, 2], AX.X, ALU.add))
                after()
                step(v.tensor_tensor(rs[:, 8, :], rs[:, 3, :], rs[:, 7, :], ALU.add))
                after()
                step(v.tensor_scalar(rs[:, 8, :], rs[:, 8, :], 1e-9, None, ALU.max))
                after()
                step(v.reciprocal(rs[:, 9, :], rs[:, 8, :]))
                after()
                tail = tiles(h3r, blk)
                v.tensor_copy(tail[:, :, D], tiles(c_sb[:, C_TOK:C_TOK + TILES], blk))
                v.tensor_tensor(tail[:, :, D + 1], rs[:, 3, :], rs[:, 9, :], ALU.mult)
                step(v.tensor_tensor(rs[:, 8, :], rs[:, 7, :], rs[:, 3, :], ALU.subtract))
                for k, rsrc, length in ((0, 4, LINE1), (1, 6, LINE2)):
                    v.tensor_scalar(tiles(exps, blk)[:, :, k], rs[:, rsrc, :], -float(length), float(E2 * length),
                                    ALU.mult, ALU.add)
                after()
                step(v.tensor_tensor(tail[:, :, D + 2], rs[:, 8, :], rs[:, 9, :], ALU.mult))
                after()

            def route_c(blk):
                dve.wait_ge(pos_ps, blk + 1)
                o = tiles(oh, blk)
                pp = ps[:, B_D, 0:BT * 2 * E2].rearrange("p (t e) -> p t e", t=BT)
                for k in range(2):
                    step(v.tensor_tensor(rt[:, k], pp[:, :, k * E2:(k + 1) * E2], o[:, :, k * E2:(k + 1) * E2],
                                         ALU.mult))
                after()
                for k in range(2):
                    step(v.tensor_reduce(tiles(loc, blk)[:, :, k], rt[:, k], AX.X, ALU.add))
                after()
                step(v.tensor_scalar(past[:], tiles(loc, blk)[:, :, 0], float(CAP), float(CAP), ALU.is_ge, ALU.mult))
                step(v.tensor_tensor(tiles(dest, blk), tiles(loc, blk), tiles(exps, blk), ALU.add))
                after()
                first = tiles(dest, blk)[:, :, 0]
                step(v.tensor_tensor(first, first, past[:], ALU.add))
                after()
                v.tensor_copy(tiles(dest_i, blk), tiles(dest, blk)).then_inc(dest_ready, 1)

            def counts():
                dve.wait_ge(pos_ps, NBLK)
                step(v.tensor_scalar(count[:], ps[:, B_D, BT * 2 * E2:BT * 2 * E2 + E2], float(CAP), None, ALU.min))
                after()
                v.tensor_copy(count_i[:], count[:]).then_inc(count_ready, 1)

            def slot_kinds():
                slot = c_sb[:, None, C_SLOT:C_SLOT + BT].broadcast_to([P, E2, BT])
                step(v.tensor_tensor(second[:], slot, count[:, :, None].broadcast_to([P, E2, BT]), ALU.is_ge))
                after()
                step(v.scalar_tensor_tensor(trash[:], second[:], -float(TOKENS),
                                            c_sb[:, C_TRASH:].rearrange("p (e t) -> p e t", e=E2), ALU.mult, ALU.add))
                after()

            def row_addresses(e):
                dve.wait_ge(rows_in[e], 16)
                number, w_first, w_diff = (rows(e)[:, :, D + i] for i in range(3))
                step(v.scalar_tensor_tensor(addr[:, 0, :], second[:, e, :], float(TOKENS), number, ALU.mult, ALU.add))
                step(v.scalar_tensor_tensor(addr[:, 1, :], number, 0.0, trash[:, e, :], ALU.is_equal, ALU.mult))
                step(v.tensor_tensor(addr[:, 2, :], second[:, e, :], w_diff, ALU.mult))
                after()
                step(v.scalar_tensor_tensor(addr[:, 3, :], addr[:, 0, :], -1.0, addr[:, 1, :], ALU.add, ALU.add))
                step(v.tensor_tensor(row_w[:, e, :], addr[:, 2, :], w_first, ALU.add))
                after()
                v.tensor_copy(back_i[:, e, :], addr[:, 3, :]).then_inc(back_i_ready, 1)
                dve.wait_ge(back_i_ready, e + 1)

            ln1(0)
            dve.wait_ge(small_in, 48)
            modulation()
            ln1(1)
            conv_taps(0)
            residual1(0)
            first_features()
            for s in range(STEPS):
                b, f = divmod(s, BT)
                if f == 1 and live(b - 2):
                    acc_start(b - 2)
                if 0 <= s - LAG - 2 and f != 0:
                    add_expert(s - LAG - 2)
                if f == 0 and live(b + 1):
                    conv_taps(b + 1)
                if f == 1 and live(b + 1):
                    residual1(b + 1)
                if f == 2 and b < 2:
                    rotate(b + 1)
                if f == 2 and b == 1:
                    split2(0)
                if f == 2 and live(b - 4):
                    route_c(b - 4)
                if f == 3:
                    if live(b - 1):
                        mix_a(b - 1)
                    if b == 0:
                        feature(b + 1)
                if s < TILES:
                    attend(s)
                if f == 0:
                    if live(b - 1):
                        residual2(b - 1)
                    if live(b - 3):
                        dve.wait_ge(x3_ready, b - 2)
                        stats(2, b - 3, tiles(x_sb, b - 3))
                if f == 1:
                    if live(b - 1):
                        ln2(b - 1)
                    if live(b + 2):
                        ln1(b + 2)
                    if live(b - 3):
                        norm3(b - 3)
                    if b == 2:
                        residual_scales()
                if f == 2:
                    if b >= 2 and live(b - 1):
                        split2(b - 1)
                    if live(b - 3):
                        route_a(b - 3)
                    if b >= 2 and live(b + 1):
                        rotate(b + 1)
                if f == 3:
                    if b >= 1 and live(b + 1):
                        feature(b + 1)
                    if live(b - 1):
                        mix_b(b - 1)
                    if 0 <= s - LAG - 1:
                        add_expert(s - LAG - 1)
                    if live(b - 3):
                        route_b(b - 3)
            route_b(LAST - 1)
            add_expert(NBLK * E1 - 2)
            add_expert(NBLK * E1 - 1)
            residual3(LAST)
            stats(2, LAST, tiles(x_sb, LAST))
            route_c(LAST - 1)
            norm3(LAST)
            route_a(LAST)
            route_b(LAST)
            route_c(LAST)
            counts()
            slot_kinds()

            def low_part(e):
                dve.wait_ge(rowsT_hi, e + 1)
                if e >= 2:
                    dve.wait_ge(eup_ps, FC * (e - 1))
                v.tensor_tensor(h2l[:, e % 2, :], ps[:, e % 2, :], h2h[:, e % 2, :].bitcast(F32), ALU.subtract) \
                    .then_inc(rowsT_lo, 1)

            for e in range(2):
                row_addresses(e)
                low_part(e)
            for e in range(E2):
                if e + 2 < E2:
                    row_addresses(e + 2)
                    low_part(e + 2)
                if e < E2 - 1:
                    dve.wait_ge(edown_ps, e + 1)
                if e >= 2:
                    dve.wait_ge(chosen_written[e % 2], 16 * BT * (e // 2))
                for j in range(BT):
                    bank = 6 + e % 2
                    if e == E2 - 1:
                        bank = LAST_BANKS[j]
                        dve.wait_ge(edown_ps, e + 1 + j)
                    v.tensor_scalar(xstage(e)[:, j, :], ps[:, bank, j * D:(j + 1) * D], row_w[:, e, j:j + 1],
                                    None, ALU.mult).then_inc(eout_ready, 1)
            for blk in range(NBLK):
                a = tiles(back[:, 0], blk)
                dve.wait_ge(both_ready, blk + 1)
                step(v.tensor_tensor(a, a, modb[:, blk // BPB, 3, None, :].broadcast_to([P, BT, D]), ALU.mult))
                after()
                v.tensor_tensor(tiles(x_sb, blk), tiles(x_sb, blk), a, ALU.add).then_inc(comb_ready, 1)

        @block.tensor
        def _(pe):
            m = nc.tensor
            freed = {}

            def claim(bank, reader, count):
                if bank in freed:
                    pe.wait_ge(*freed[bank])
                freed[bank] = (reader, count)

            def mm(o, l, r, start=True, stop=True):
                return m.matmul(o, l, r, start=start, stop=stop)

            def modulation():
                pe.wait_ge(mod_in, 16)
                pe.wait_ge(sc_ready, 1)
                claim(B_D, mod_ready, 1)
                for i in range(2):
                    last = mm(ps[:, B_D, 2 * i:2 * i + 2], wmod_sb[:, i * D:(i + 1) * D], scT[:])
                last.then_inc(mod_ps, 1)

            def modulation_rows():
                pe.wait_ge(scb_ready, 1)
                for b in range(BATCH):
                    last = mm(ps[:, B_UP[b], :], scb[:, b, :], wmod_sb[:, 2 * D:6 * D])
                last.then_inc(mod_ps, 1)
                freed[B_UP[0]] = freed[B_UP[1]] = (modb_ready, 1)

            def transposes(bank, src, src_ready, count, done, reader):
                pe.wait_ge(src_ready, count)
                claim(bank, reader, count)
                for j in range(BT):
                    last = m.transpose(ps[:, bank, j * P:(j + 1) * P], src[:, j], ident)
                last.then_inc(done, 1)

            def pointwise(blk):
                pe.wait_ge(conv_ready, blk + 1)
                if blk == 0:
                    pe.wait_ge(proj_in, 16)
                claim(pw_bank(blk), x1_ready, blk + 1)
                mm(ps[:, pw_bank(blk), :], proj_sb[:, 0:P], conv[:]).then_inc(pw_ps, 1)

            def qkv(t):
                blk = t // BT
                pe.wait_ge(x1_ready, blk + 1)
                bank = qkv_bank(t)
                claim(bank, qkv_ready, t + 1)
                o = 1 + (t % TPB) * P
                mm(ps[:, bank, 0:3 * D], x1T[:, blk // BPB, o:o + P], proj_sb[:, P:4 * P]).then_inc(qkv_ps, 1)

            def q_transpose(t):
                wait_phi(pe, t)
                claim(B_Q, qT_ready, t + 1)
                m.transpose(ps[:, B_Q, 384:512], phi[:, t // BT % 2, t % BT, 0:D], ident).then_inc(qT_ps, 1)

            def prefix(t):
                blk, j = t // BT, t % BT
                kv_ = kv[:, t % 2, :]
                pe.wait_ge(kv_ready, t + 1)
                claim(B_KV, cum_read, t + 1)
                claim(B_KV + 1, cum_read, t + 1)
                mm(ps[:, B_KV, :], tri, kv_[:, 0:512])
                mm(ps[:, B_KV + 1, :], tri, kv_[:, 512:1024]).then_inc(cum_ps, 1)
                claim(B_M, tail_read, t + 1)
                if t % TPB != TPB - 1:
                    mm(ps[:, B_M, 2 * D + 16:2 * D + 16 + NH9], phi[:, blk % 2, j, D:2 * D], vx[:, blk % 2, j, :])
                if t % TPB != 0:
                    pe.wait_ge(qT_ready, t + 1)
                    pe.wait_ge(state_ready, t)
                    mm(ps[:, B_M, D:D + NH9], qT[:, t % 2, :], state[:])
                mm(ps[:, B_M, 0:D], tri, kv_[:, 1024:CH]).then_inc(tail_ps, 1)

            def att_transpose(t):
                pe.wait_ge(att_ready, t + 1)
                claim(B_Q, attT_ready, t + 1)
                m.transpose(ps[:, B_Q, 384:512], att[:, t % 2, :], ident).then_inc(attT_ps, 1)

            def out_and_gate(blk):
                pe.wait_ge(attT_ready, BT * (blk + 1))
                pe.wait_ge(diff_ready, blk + 1)
                claim(B_D, x2T_ready, blk + 1)
                mm(ps[:, B_D, :], proj_sb[:, 4 * P:5 * P], attT[:])
                claim(B_Q, gate_ready, blk + 1)
                mm(ps[:, B_Q, :], proj_sb[:, 5 * P:6 * P], diff[:]).then_inc(og_ps, 1)

            def x2_transposes(blk):
                pe.wait_ge(x2T_ready, blk + 1)
                claim(B_D, x2_ready, blk + 1)
                for j in range(BT):
                    last = m.transpose(ps[:, B_D, j * P:(j + 1) * P], x2T[:, j * P:(j + 1) * P], ident)
                last.then_inc(x2_ps, 1)

            def mix_logits(blk):
                pe.wait_ge(h2T_ready, blk + 1)
                claim(B_D, mix_shift, blk + 1)
                for j in range(BT):
                    last = mm(ps[:, B_D, j * E1:(j + 1) * E1], h2T[:, j * P:(j + 1) * P], s_sb[:, S_MG:S_MG + E1])
                last.then_inc(mix_ps, 1)

            def mix_weights_transpose(blk):
                pe.wait_ge(mix_ready, blk + 1)
                claim(B_D, gwT_ready, blk + 1)
                m.transpose(ps[:, B_D, 0:P], gwp[:, blk % 2, :], ident).then_inc(gwT_ps, 1)

            def mix_bias(blk):
                pe.wait_ge(gwT_ready, blk + 1)
                if blk == 0:
                    pe.wait_ge(w2_in, 32)
                claim(B_Q, acc_ready, blk + 1)
                for j in range(BT):
                    last = mm(ps[:, B_Q, j * D:(j + 1) * D], gwT[:], b2_sb[:, j, :])
                last.then_inc(b2_ps, 1)

            def three_pass(o, wh, wl, ah, al):
                mm(o, wh, ah, stop=False)
                mm(o, wh, al, start=False, stop=False)
                return mm(o, wl, ah, start=False)

            def up(u):
                e = u // FC
                blk, c = e // E1, u % FC
                pe.wait_ge(h2_split, blk + 1)
                if blk == 0:
                    pe.wait_ge(w_split, e + 1)
                claim(B_UP[u % 2], hid_ready, u + 1)
                w_ = slice(c * P, (c + 1) * P)
                three_pass(ps[:, B_UP[u % 2], :], w1h[:, e % E1, w_], w1l[:, e % E1, w_], h2h[:, blk % 2, :],
                           h2l[:, blk % 2, :]).then_inc(up_ps, 1)

            def down_tile(bank, j, w_, h, ready, count):
                for c in range(FC):
                    if j == 0:
                        pe.wait_ge(ready, count + c + 1)
                    last = mm(ps[:, bank, j * D:(j + 1) * D], h[:, c, j * P:(j + 1) * P], w_[:, c, :],
                              start=(c == 0), stop=(c == FC - 1))
                return last

            def down(bank, w_, h, done, ready, count):
                for j in range(BT):
                    last = down_tile(bank, j, w_, h, ready, count)
                last.then_inc(done, 1)

            def route_logits(blk):
                pe.wait_ge(h3T_ready, blk + 1)
                claim(B_D, route_shift, blk + 1)
                for j in range(BT):
                    last = mm(ps[:, B_D, j * E2:(j + 1) * E2], h3T[:, j * P:(j + 1) * P], s_sb[:, S_WG:S_WG + E2])
                last.then_inc(route_ps, 1)

            def positions(blk):
                pe.wait_ge(onehot_ready, blk + 1)
                claim(B_D, dest_ready, blk + 1)
                for j in range(BT):
                    t = BT * blk + j
                    o = ps[:, B_D, j * 2 * E2:(j + 1) * 2 * E2]
                    mm(o, strict, ohb[:, t, :], stop=False)
                    for i in range(BT * blk, t):
                        mm(o, ones, ohb[:, i, :], start=False, stop=False)
                    last = mm(o, ones, before[:, blk, :], start=False)
                if blk == LAST:
                    o = ps[:, B_D, BT * 2 * E2:(BT + 1) * 2 * E2]
                    for t in range(BT * blk, TILES):
                        mm(o, ones, ohb[:, t, :], start=(t == BT * blk), stop=False)
                    last = mm(o, ones, before[:, blk, :], start=False)
                last.then_inc(pos_ps, 1)

            def warm(products):
                if B_M in freed:
                    pe.wait_ge(*freed[B_M])
                for _ in range(products):
                    mm(ps[:, B_M, 0:2 * P], ones, cm_sb[:].rearrange("p m n -> p (m n)"))

            pe.wait_ge(small_in, 48)
            modulation()
            warm(7)
            transposes(B_D, xh, xh_ready, 1, hT_ps, hT_ready)
            modulation_rows()
            pointwise(0)
            for j in range(BT):
                qkv(j)
            for s in range(STEPS):
                b, f = divmod(s, BT)
                e = s - LAG

                def ups(c0):
                    if 0 <= e < NBLK * E1:
                        for c in range(c0, c0 + 2):
                            up(e * FC + c)

                def downs(ahead=0):
                    k = e - 1 + ahead
                    if 0 <= k < NBLK * E1:
                        bank = mix_bank(k)
                        claim(bank, down_added, k + 1)
                        down(bank, w2_sb[:, k % E1], hid[:, k % 2], down_ps, hid_ready, k * FC)

                def attention(order):
                    for part in order:
                        if part == "q" and s < TILES:
                            q_transpose(s)
                        if part == "a" and 1 <= s <= TILES:
                            att_transpose(s - 1)
                        if part == "p" and s < TILES:
                            prefix(s)

                if f == 0:
                    if live(b + 1):
                        transposes(B_D, xh, xh_ready, b + 2, hT_ps, hT_ready)
                    ups(0)
                    attention("q")
                    if live(b - 2):
                        mix_weights_transpose(b - 2)
                    downs()
                    attention("pa")
                    if live(b - 1):
                        out_and_gate(b - 1)
                    ups(2)
                    if live(b - 2):
                        mix_bias(b - 2)
                if f == 1:
                    ups(0)
                    attention("q")
                    if live(b + 1):
                        pointwise(b + 1)
                    attention("p")
                    if live(b - 1):
                        x2_transposes(b - 1)
                    if live(b + 1):
                        qkv(BT * (b + 1))
                    ups(2)
                    if live(b + 1):
                        qkv(BT * (b + 1) + 1)
                    downs()
                    if live(b + 1):
                        qkv(BT * (b + 1) + 2)
                    if live(b - 4):
                        positions(b - 4)
                    attention("a")
                if f == 2:
                    if live(b + 1):
                        qkv(BT * (b + 1) + 3)
                    ups(0)
                    if live(b - 3):
                        transposes(B_D, tiles(h3, b - 3), h3_ready, b - 2, h3T_ps, h3T_ready)
                    attention("qp")
                    if live(b - 1):
                        transposes(B_D, xm, xm_ready, b, h2T_ps, h2T_ready)
                    ups(2)
                    if live(b - 3):
                        route_logits(b - 3)
                    downs()
                    attention("a")
                if f == 3:
                    attention("q")
                    if live(b - 1):
                        mix_logits(b - 1)
                    ups(0)
                    attention("p")
                    downs()
                    ups(2)
                    attention("a")
            downs(1)
            positions(LAST - 1)
            transposes(B_D, tiles(h3, LAST), h3_ready, NBLK, h3T_ps, h3T_ready)
            route_logits(LAST)
            positions(LAST)
            def rows_transpose(e):
                pe.wait_ge(rows_in[e], 16)
                claim(e % 2, rowsT_lo, e + 1)
                for j in range(BT):
                    last = m.transpose(ps[:, e % 2, j * P:(j + 1) * P], rows(e)[:, j, 0:D], ident)
                last.then_inc(rowsT_ps, 1)

            def expert_up(e):
                pe.wait_ge(rowsT_lo, e + 1)
                pe.wait_ge(w_split, E1 + e + 1)
                wh, wl = up_weights(E1 + e)
                for c in range(FC):
                    u = e * FC + c
                    claim(2 + c, ehid_ready, u + 1)
                    w_ = slice(c * P, (c + 1) * P)
                    three_pass(ps[:, 2 + c, :], wh[:, e % E1, w_], wl[:, e % E1, w_], h2h[:, e % 2, :],
                               h2l[:, e % 2, :]).then_inc(eup_ps, 1)

            pe.wait_ge(moved[0], 16)
            warm(18)
            rows_transpose(0)
            rows_transpose(1)
            expert_up(0)
            pe.wait_ge(wd_in, 16)
            for e in range(E2):
                if e + 2 < E2:
                    rows_transpose(e + 2)
                if e + 1 < E2 - 1:
                    expert_up(e + 1)
                if e < E2 - 1:
                    claim(6 + e % 2, eout_ready, BT * (e + 1))
                    down(6 + e % 2, wd_sb[:, e], hid[:, e % 2], edown_ps, ehid_ready, e * FC)
            expert_up(E2 - 1)
            for j in range(BT):
                claim(LAST_BANKS[j], eout_ready, BT * (E2 - 1) + j + 1)
                down_tile(LAST_BANKS[j], j, wd_sb[:, E2 - 1], hid[:, (E2 - 1) % 2], ehid_ready, (E2 - 1) * FC) \
                    .then_inc(edown_ps, 1)


def kernel(**inputs):
    import ml_dtypes
    import numpy as np
    import concourse.bacc as bacc
    from concourse.bass_utils import run_bass_kernel_spmd

    a = {k: np.asarray(v) for k, v in inputs.items()}
    f = np.float32
    col = lambda v: v.reshape(-1, P).T
    small = np.concatenate([
        a["L0_attn_w_dw"], col(a["L0_attn_b_gate"]), col(a["L0_attn_ln_g"]), col(a["L0_attn_ln_b"]),
        a["L0_attn_w_moe_gate"].T, col(a["L0_attn_b1"]), a["L0_ffn_wg"], a["L0_c"].T], axis=1)
    proj = np.concatenate([a["L0_attn_w_pw"].T, a["L0_attn_w_qkv"].T, a["L0_attn_w_o"].T, a["L0_attn_w_gate"].T],
                          axis=1)
    w1 = a["L0_attn_w1"].transpose(2, 0, 1)
    w2 = a["L0_attn_w2"].reshape(E1, D, FC, P).transpose(3, 0, 2, 1)
    b2 = np.zeros((P, BT, D), f)
    for j in range(BT):
        b2[j * E1:(j + 1) * E1, j, :] = a["L0_attn_b2"]
    w_up = a["L0_ffn_w_gate"].transpose(1, 0, 2)
    w_down = a["L0_ffn_w_down"].reshape(E2, FC, P, D).transpose(2, 0, 1, 3)

    const = np.zeros((P, N_CONST), f)
    i = np.arange(P)
    const[:, C_ID:C_ID + P] = i[:, None] == i
    const[:, C_TRI:C_TRI + P] = i[:, None] <= i
    const[:, C_BD:C_BD + NH9] = (i // DH)[:, None] == np.arange(NH9) % HEADS
    inv = (f(1) / f(10000) ** (np.arange(0, DH, 2, dtype=f) / f(DH))).astype(f)
    theta = (np.arange(SEQ, dtype=f)[:, None] * inv).astype(f)
    cos = np.repeat(np.cos(theta), 2, axis=1).reshape(TPB, P, DH).transpose(1, 0, 2)
    sin = (np.repeat(np.sin(theta), 2, axis=1) * np.tile([-1, 1], DH // 2)).reshape(TPB, P, DH).transpose(1, 0, 2)
    const[:, C_COS:C_COS + TPB * DH] = cos.reshape(P, -1)
    const[:, C_SIN:C_SIN + TPB * DH] = sin.reshape(P, -1)
    const[:, C_REV:C_REV + E2] = E2 - np.arange(E2)
    const[:, C_TOK:C_TOK + TILES] = np.arange(TILES) * P + i[:, None] + 1
    const[:, C_SLOT:C_SLOT + BT] = np.arange(BT) * P + i[:, None]
    const[:, C_TRASH:] = 2 * TOKENS + 1 + np.arange(E2 * BT) * P + i[:, None]
    cmask = np.stack([i[:, None] < i, np.ones((P, P), bool)], axis=1).astype(ml_dtypes.bfloat16)

    arrays = {"x": a["L0_attn_x"], "small": small, "proj": proj, "wmod": a["L0_wmod"], "w1": w1, "w2": w2,
              "b2": b2, "w_up": w_up, "w_down": w_down, "const": const, "cmask": cmask}
    arrays = {f"in_{k}": np.ascontiguousarray(v) for k, v in arrays.items()}
    nc = bacc.Bacc("TRN2", target_bir_lowering=False, num_devices=1)
    args = [nc.dram_tensor(k, v.shape, mybir.dt.from_np(v.dtype), kind="ExternalInput").ap()
            for k, v in arrays.items()]
    args.append(nc.dram_tensor("out", (BATCH, SEQ, D), F32, kind="ExternalOutput").ap())
    block_kernel(nc, *args)
    r = run_bass_kernel_spmd(nc, [arrays], core_ids=[0])
    return r.results[0]["out"]
```
